# Optimizing a Trainium2 kernel written in Bass

```python
import numpy as np
import jax
import jax.numpy as jnp

def _softmax(x, axis=-1):
    return jax.nn.softmax(x, axis=axis)

def _gelu(x):
    return jax.nn.gelu(x, approximate=True)

def _silu(x):
    return jax.nn.silu(x)

def _sigmoid(x):
    return jax.nn.sigmoid(x)

def _layernorm(x, axis=-1, eps=1e-05):
    m = jnp.mean(x, axis=axis, keepdims=True)
    v = jnp.var(x, axis=axis, keepdims=True)
    return (x - m) / jnp.sqrt(v + eps)

def _scatter_add(tgt, idx, src, axis=0):
    return tgt.at[idx].add(src)

def _segment_sum(src, seg, n):
    return jax.ops.segment_sum(src, seg, n)
kernel_name = 'mk_gnn_ffn_d1_gnn_r8_bf09d8'

def setup_inputs(seed: int=0):
    np.random.seed(seed)
    _w = jnp.asarray

    def _rec_inputs():
        import jax
        import jax.numpy as jnp
        _gk = jax.random.key(seed)
        x = -0.0003713 + 1 * jax.random.normal(jax.random.fold_in(_gk, 1), (6250, 256), jnp.float32)
        src = jax.random.randint(jax.random.fold_in(_gk, 2), (100000,), 0, 6250, jnp.int32)
        dst = jax.random.randint(jax.random.fold_in(_gk, 3), (100000,), 0, 6250, jnp.int32)
        _o = jnp.argsort(dst, stable=True)
        src = src[_o]
        dst = dst[_o]
        return (x, src, dst)
    x, src, dst = _rec_inputs()

    def _L0_gnn_setup():
        import jax, jax.numpy as jnp
        import numpy as np
        N = 6250
        E = 100000
        IN = 256
        H = 8
        C = 32
        NEG_SLOPE = 0.2
        LN_EPS = 1e-05

        def _gat_block(x, edge_index, W, att_src, att_dst, bias, ln_scale, ln_bias):
            src, dst = (edge_index[0], edge_index[1])
            h = (x @ W).reshape(N, H, C)
            a_src = jnp.einsum('nhc,hc->nh', h, att_src)
            a_dst = jnp.einsum('nhc,hc->nh', h, att_dst)
            alpha = jax.nn.leaky_relu(a_src[src] + a_dst[dst], NEG_SLOPE)
            amax = jax.ops.segment_max(alpha, dst, num_segments=N)
            amax = jnp.where(jnp.isfinite(amax), amax, 0.0)
            ex = jnp.exp(alpha - amax[dst])
            denom = jax.ops.segment_sum(ex, dst, num_segments=N)
            attn = ex / (denom[dst] + 1e-16)
            msg = h[src] * attn[:, :, None]
            out = jax.ops.segment_sum(msg, dst, num_segments=N)
            out = out.reshape(N, H * C) + bias
            out = out + x
            out = jax.nn.elu(out)
            mu = jnp.mean(out, axis=-1, keepdims=True)
            var = jnp.var(out, axis=-1, keepdims=True)
            return (out - mu) * jax.lax.rsqrt(var + LN_EPS) * ln_scale + ln_bias
        key = jax.random.key(seed)
        ks = jax.random.split(key, 8)
        x = jax.random.normal(ks[0], (N, IN), dtype=jnp.float32)
        edge_index = jax.random.randint(ks[1], (2, E), 0, N, dtype=jnp.int64)
        W = jax.random.normal(ks[2], (IN, H * C), dtype=jnp.float32) / np.sqrt(IN)
        att_src = jax.random.normal(ks[3], (H, C), dtype=jnp.float32) / np.sqrt(C)
        att_dst = jax.random.normal(ks[4], (H, C), dtype=jnp.float32) / np.sqrt(C)
        bias = jnp.zeros((H * C,), dtype=jnp.float32)
        ln_scale = jnp.ones((H * C,), dtype=jnp.float32)
        ln_bias = jnp.zeros((H * C,), dtype=jnp.float32)
        return {'x': x, 'edge_index': edge_index, 'W': W, 'att_src': att_src, 'att_dst': att_dst, 'bias': bias, 'ln_scale': ln_scale, 'ln_bias': ln_bias}
    _L0_gnn_all = _L0_gnn_setup()
    _L0_gnn_in = {k: v for k, v in _L0_gnn_all.items() if k in ('W', 'att_src', 'att_dst', 'bias', 'ln_scale', 'ln_bias')}
    del _L0_gnn_all

    def _L0_ffn_setup():
        import math
        import jax, jax.numpy as jnp
        import numpy as np
        CAPACITY_FACTOR = 1.25
        key = jax.random.key(seed)
        ks = jax.random.split(key, 5)
        B, L, D, F, E = (8, 1024, 256, 1024, 8)
        h = jax.random.normal(ks[0], (B, L, D), dtype=jnp.float32)
        gate_w = jax.random.normal(ks[1], (D, E), dtype=jnp.float32) * 0.02
        gate_b = jnp.zeros((E,), dtype=jnp.float32)
        w1 = jax.random.normal(ks[2], (E, D, F), dtype=jnp.float32) * (1.0 / math.sqrt(D))
        b1 = jnp.zeros((E, F), dtype=jnp.float32)
        w2 = jax.random.normal(ks[3], (E, F, D), dtype=jnp.float32) * (1.0 / math.sqrt(F))
        b2 = jnp.zeros((E, D), dtype=jnp.float32)
        return {'h': h, 'gate_w': gate_w, 'gate_b': gate_b, 'w1': w1, 'b1': b1, 'w2': w2, 'b2': b2}
    _L0_ffn_all = _L0_ffn_setup()
    _L0_ffn_in = {k: v for k, v in _L0_ffn_all.items() if k in ('gate_w', 'gate_b', 'w1', 'b1', 'w2', 'b2')}
    del _L0_ffn_all
    return {'x': x, 'src': src, 'dst': dst, 'L0_gnn_W': _L0_gnn_in['W'], 'L0_gnn_att_src': _L0_gnn_in['att_src'], 'L0_gnn_att_dst': _L0_gnn_in['att_dst'], 'L0_gnn_bias': _L0_gnn_in['bias'], 'L0_gnn_ln_scale': _L0_gnn_in['ln_scale'], 'L0_gnn_ln_bias': _L0_gnn_in['ln_bias'], 'L0_ffn_gate_w': _L0_ffn_in['gate_w'], 'L0_ffn_gate_b': _L0_ffn_in['gate_b'], 'L0_ffn_w1': _L0_ffn_in['w1'], 'L0_ffn_b1': _L0_ffn_in['b1'], 'L0_ffn_w2': _L0_ffn_in['w2'], 'L0_ffn_b2': _L0_ffn_in['b2']}

def reference(x, src, dst, L0_gnn_W, L0_gnn_att_src, L0_gnn_att_dst, L0_gnn_bias, L0_gnn_ln_scale, L0_gnn_ln_bias, L0_ffn_gate_w, L0_ffn_gate_b, L0_ffn_w1, L0_ffn_b1, L0_ffn_w2, L0_ffn_b2):
    import jax
    import jax.numpy as jnp

    def _L0_gnn_ref(x, edge_index, W, att_src, att_dst, bias, ln_scale, ln_bias):
        import jax, jax.numpy as jnp
        import numpy as np
        N = 6250
        E = 100000
        IN = 256
        H = 8
        C = 32
        NEG_SLOPE = 0.2
        LN_EPS = 1e-05

        def _gat_block(x, edge_index, W, att_src, att_dst, bias, ln_scale, ln_bias):
            src, dst = (edge_index[0], edge_index[1])
            h = (x @ W).reshape(N, H, C)
            a_src = jnp.einsum('nhc,hc->nh', h, att_src)
            a_dst = jnp.einsum('nhc,hc->nh', h, att_dst)
            alpha = jax.nn.leaky_relu(a_src[src] + a_dst[dst], NEG_SLOPE)
            amax = jax.ops.segment_max(alpha, dst, num_segments=N)
            amax = jnp.where(jnp.isfinite(amax), amax, 0.0)
            ex = jnp.exp(alpha - amax[dst])
            denom = jax.ops.segment_sum(ex, dst, num_segments=N)
            attn = ex / (denom[dst] + 1e-16)
            msg = h[src] * attn[:, :, None]
            out = jax.ops.segment_sum(msg, dst, num_segments=N)
            out = out.reshape(N, H * C) + bias
            out = out + x
            out = jax.nn.elu(out)
            mu = jnp.mean(out, axis=-1, keepdims=True)
            var = jnp.var(out, axis=-1, keepdims=True)
            return (out - mu) * jax.lax.rsqrt(var + LN_EPS) * ln_scale + ln_bias
        return _gat_block(x, edge_index, W, att_src, att_dst, bias, ln_scale, ln_bias)

    def _L0_ffn_ref(h, gate_w, gate_b, w1, b1, w2, b2):
        import math
        import jax, jax.numpy as jnp
        import numpy as np
        CAPACITY_FACTOR = 1.25
        B, L, D = h.shape
        E = gate_w.shape[1]
        T = B * L
        C = max(1, math.ceil(CAPACITY_FACTOR * T / E))
        x = h.reshape(T, D)
        logits = x @ gate_w + gate_b
        probs = jax.nn.softmax(logits, axis=-1)
        idx = jnp.argmax(probs, axis=-1)
        prb = jnp.take_along_axis(probs, idx[:, None], axis=1)[:, 0]
        one_hot = jax.nn.one_hot(idx, E, dtype=jnp.float32)
        pos = (jnp.cumsum(one_hot, axis=0) * one_hot).sum(-1).astype(jnp.int32) - 1
        kept = pos < C
        pos_safe = jnp.where(kept, pos, C)
        buf = jnp.zeros((E, C, D), dtype=h.dtype).at[idx, pos_safe].set(x, mode='drop')
        hmid = jax.nn.relu(jnp.einsum('ecd,edf->ecf', buf, w1) + b1[:, None, :])
        ybuf = jnp.einsum('ecf,efd->ecd', hmid, w2) + b2[:, None, :]
        pos_g = jnp.minimum(pos, C - 1)
        y_tok = ybuf[idx, pos_g] * (prb * kept)[:, None]
        y = y_tok.reshape(B, L, D)
        y = jnp.nan_to_num(y, nan=0.0, posinf=10000.0, neginf=-10000.0)
        return y
    edge_index = jnp.stack([src, dst])
    x = x + _L0_gnn_ref(_layernorm(x, axis=-1), edge_index, L0_gnn_W, L0_gnn_att_src, L0_gnn_att_dst, L0_gnn_bias, L0_gnn_ln_scale, L0_gnn_ln_bias)
    x = x + _L0_ffn_ref(_layernorm(x, axis=-1)[None], L0_ffn_gate_w, L0_ffn_gate_b, L0_ffn_w1, L0_ffn_b1, L0_ffn_w2, L0_ffn_b2)[0]
    return x

_drawn_inputs = setup_inputs


def setup_inputs(seed=0):
    import zlib

    import numpy as np

    out = dict(_drawn_inputs(seed))
    spreads = {'L0_gnn_bias': (0.0, 0.1),
     'L0_gnn_ln_scale': (1.0, 0.2),
     'L0_gnn_ln_bias': (0.0, 0.1),
     'L0_ffn_gate_b': (0.0, 0.1),
     'L0_ffn_b1': (0.0, 0.8),
     'L0_ffn_b2': (0.0, 0.8)}
    factors = {}
    for name, (base, spread) in spreads.items():
        noise = np.random.default_rng([zlib.crc32(name.encode()), seed]).standard_normal(out[name].shape)
        drawn = base * np.exp(spread * noise) if base else spread * noise
        out[name] = jnp.asarray(drawn.astype(out[name].dtype))
    for name, factor in factors.items():
        out[name] = (out[name] * factor).astype(out[name].dtype)
    return out
```

```python
from contextlib import ExitStack

import concourse.bass as bass
from concourse import mybir

P = 128
F32 = mybir.dt.float32
I32 = mybir.dt.int32
ACT = mybir.ActivationFunctionType
ALU = mybir.AluOpType
AX_X = mybir.AxisListType.X

HEADS, HC = 8, 32
GC = HC + 1
SUB = 2
STEP = SUB * P
UN = 4
NJ = SUB * UN
PH = 4
PAD_NODE = 9999
BIG = 1.0e30
SLOPE = 0.2
EPS = 1e-5
FAR = 1 << 20
FMAX = 3.4028234663852886e38


def wait_for(eng, sem, count):
    if isinstance(count, int) and count <= 0:
        return
    eng.wait_ge(sem, count)


def own(eng, carrier):
    eng.sem_inc(carrier, 1)


def slots(eng, total, period, stages):
    lag_max = max(lag for lag, _ in stages)
    loops = (total - period) // period
    assert lag_max <= period and loops >= 1

    def straight(s):
        for lag, f in stages:
            t = s - lag
            if 0 <= t < total:
                f(t, t % period, t // period)

    for s in range(period):
        straight(s)
    with eng.Fori(1, 1 + loops) as k:
        for r in range(period):
            for lag, f in stages:
                d = r - lag
                f(k * period + d, d % period, k + d // period)
    for s in range(period * (1 + loops), total + lag_max):
        straight(s)


def build(nc, x, ed, dstp, W, att_s, att_d, bias, ln_s, ln_b, gate_w, gate_b, w1, b1, w2, b2, out):
    N, D = x.shape
    E = ed.shape[0] - 2 * STEP
    NB = -(-N // P)
    TAIL = N - (NB - 1) * P
    ROW = HEADS * GC
    NX = gate_w.shape[1]
    F = w1.shape[2]
    CAP = -(-5 * N // (4 * NX))
    SL = -(-CAP // P) * P
    NSTEP = (E + NB * (STEP - 1)) // STEP
    NBATCH = -(-NSTEP // UN)
    TS = 4 * P
    assert NBATCH * UN <= TS and D == HEADS * HC
    EC = dstp.shape[1]
    KD = D // P
    FC = F // P

    table = nc.dram_tensor("table", [NB * P, ROW], F32).ap()
    sched_e = nc.dram_tensor("sched_e", [P, TS // P], I32).ap()
    sched_b = nc.dram_tensor("sched_b", [P, TS // P], I32).ap()
    sched_f = nc.dram_tensor("sched_f", [P, TS // P], F32).ap()
    xbuf = nc.dram_tensor("xbuf", [NX * SL, D], F32).ap()
    ybuf = nc.dram_tensor("ybuf", [NX * SL, D], F32).ap()

    with ExitStack() as ctx:
        def sb(name, shape, dt=F32):
            return ctx.enter_context(nc.sbuf_tensor(name, shape, dt))

        def sem(name):
            return ctx.enter_context(nc.semaphore(name))

        bank = [ctx.enter_context(nc.psum_tensor(f"bank{i}", [P, 512], F32)) for i in range(8)]

        x_sb = sb("x_sb", [P, NB, D])
        acc = sb("acc", [P, NB * ROW])
        G = sb("G", [P, PH, NJ * ROW])
        oh = sb("oh", [P, 2, NJ, P])
        ohT = sb("ohT", [P, 2, NJ, P])
        adst = sb("adst", [P, NB * HEADS])
        ms = sb("ms", [P, NB * HEADS])
        mv = sb("mv", [P, NB, 2])
        rstd = sb("rstd", [P, NB])
        ident = sb("ident", [P, P])
        iota_n = sb("iota_n", [P, P])
        ones = sb("ones", [P, P])
        is_last_p = sb("is_last_p", [P, 1])
        epst = sb("epst", [P, 1])
        etab = sb("etab", [1, TS], I32)
        btab = sb("btab", [1, TS], I32)
        bbase = sb("bbase", [P, TS])
        s_const = sem("s_const")
        gate, gate_pe, gate_act, gate_dve = (sem(n) for n in ("gate", "gate_pe", "gate_act", "gate_dve"))

        with ExitStack() as c1:
            def sb1(name, shape, dt=F32):
                return c1.enter_context(nc.sbuf_tensor(name, shape, dt))

            def sem1(name):
                return ctx.enter_context(nc.semaphore(name))

            Ws = oh[:, :, :, :].rearrange("p a b c -> p (a b c)")[:, 0:KD * D].rearrange("p (k d) -> p k d", k=KD)
            Wt = ohT[:, :, :, :].rearrange("p a b c -> p (a b c)")[:, 0:KD * D].rearrange("p (k d) -> p k d", k=KD)
            Wx = sb1("Wx", [P, KD, ROW + HEADS])
            att = sb1("att", [P, 2, D])
            st6 = sb1("st6", [P, NB, 6])
            dif = sb1("dif", [P, NB])
            xn = sb1("xn", [P, 2, D])
            xnT = sb1("xnT", [P, 2, D])
            hrow = sb1("hrow", [P, 2, ROW])
            dsts = G[:, 1, 0:EC].bitcast(I32)
            cmp = [G[:, 2 + i, 0:EC] for i in range(2)]
            cnt = sb1("cnt", [P, NB])
            rp = sb1("rp", [P, NB + 1])
            cf = sb1("cf", [P, NB])
            ci = sb1("ci", [P, NB], I32)
            nf = sb1("nf", [P, NB])
            csi = sb1("csi", [P, NB])
            fb = sb1("fb", [P, NB])
            df = sb1("df", [P, NB])
            sid = sb1("sid", [P, 4], I32)
            sidf = sb1("sidf", [P, 4])
            ge = sb1("ge", [P, 4, NB])
            gd = sb1("gd", [P, 4, NB])
            bs = sb1("bs", [P, 4])
            fs = sb1("fs", [P, 4])
            es = sb1("es", [P, 4])
            esi = sb1("esi", [P, 4], I32)
            bsi = sb1("bsi", [P, 4], I32)
            bsf = sb1("bsf", [P, 4])

            s_x = sem1("s_x")
            s_w = sem1("s_w")
            s_dst = sem1("s_dst")
            s_tail0 = sem1("s_tail0")
            s_zero = sem1("s_zero")
            s_zst = sem1("s_zst")
            dA = sem1("dA")
            dB = sem1("dB")
            s_std = sem1("s_std")
            s_rstd = sem1("s_rstd")
            s_xn = sem1("s_xn")
            s_xt = sem1("s_xt")
            s_xtc = sem1("s_xtc")
            s_h = sem1("s_h")
            s_hr = sem1("s_hr")
            s_tab = [sem1("s_tab0"), sem1("s_tab1")]
            s_cnt = sem1("s_cnt")
            s_cps = sem1("s_cps")
            s_sch = sem1("s_sch")
            s_schd = sem1("s_schd")
            s_schl = sem1("s_schl")
            block = c1.enter_context(nc.Block())

            @block.sync
            def _(sp):
                sp.dma_start(x_sb[:, 0:NB - 1, :], x[0:(NB - 1) * P, :].rearrange("(t p) d -> p t d", p=P)).then_inc(s_x, 16)
                sp.wait_ge(s_tail0, 1)
                sp.dma_start(x_sb[0:TAIL, NB - 1, :], x[(NB - 1) * P:N, :]).then_inc(s_x, 16)
                sp.wait_ge(s_zero, 1)
                for c in range(NX):
                    sp.dma_start(xbuf[c * SL:(c + 1) * SL, :].rearrange("(p s) d -> p (s d)", p=P),
                                 G[:, 0, 0:SL // P * D]).then_inc(s_zst, 16)

                def put_rows(t, r, n):
                    sp.wait_ge(s_hr, t + 1)
                    sp.dma_start(table[bass.ds(t * P, P), :], hrow[:, r, :]).then_inc(s_tab[r], 16)

                slots(sp, NB, 2, [(0, put_rows)])
                sp.wait_ge(s_sch, 1)
                sp.dma_start(sched_e, esi[:, :]).then_inc(s_schd, 16)
                sp.dma_start(sched_b, bsi[:, :]).then_inc(s_schd, 16)
                sp.dma_start(sched_f, bsf[:, :]).then_inc(s_schd, 16)
                sp.wait_ge(s_schd, 48)
                sp.dma_start(etab[:, :], sched_e.rearrange("(a p) q -> a (p q)", a=1)).then_inc(s_schl, 16)
                sp.dma_start(btab[:, :], sched_b.rearrange("(a p) q -> a (p q)", a=1)).then_inc(s_schl, 16)
                sp.dma_start(bbase[:, :], sched_f.rearrange("(a p) q -> a (p q)", a=1).to_broadcast([P, TS])).then_inc(s_schl, 16)
                sp.wait_ge(s_schl, 48)
                sp.wait_ge(s_tab[0], 16 * ((NB + 1) // 2))
                sp.wait_ge(s_tab[1], 16 * (NB // 2))
                sp.wait_ge(s_zst, 16 * NX)

            @block.gpsimd
            def _(pool):
                pool.memset(G[:, 0, :], 0.0).then_inc(s_zero, 1)
                pool.iota(iota_n[:, :], [[1, P]], base=0, channel_multiplier=0,
                          allow_small_or_imprecise_dtypes=True).then_inc(s_const, 1)
                pool.iota(sid[:, :], [[1, 4]], base=0, channel_multiplier=4).then_inc(s_const, 1)
                pool.memset(ident[:, :], 0.0).then_inc(s_const, 1)
                pool.memset(is_last_p[:, :], 0.0).then_inc(s_const, 1)
                pool.wait_ge(s_const, 4)
                pool.affine_select(out=ident[:, :], in_=ident[:, :], compare_op=ALU.not_equal, fill=1.0, base=0,
                                   pattern=[[-1, P]], channel_multiplier=1).then_inc(s_const, 1)
                pool.affine_select(out=is_last_p[:, :], in_=is_last_p[:, :], compare_op=ALU.not_equal, fill=1.0,
                                   base=-(P - 1), pattern=[[0, 1]], channel_multiplier=1).then_inc(s_const, 1)
                pool.memset(acc[:, :], 0.0).then_inc(s_const, 1)

            @block.scalar
            def _(act):
                act.dma_start(Ws, W.rearrange("(k p) d -> p k d", p=P)).then_inc(s_w, 16)
                for i, a in enumerate((att_s, att_d)):
                    act.dma_start(att[:, i, :], a.rearrange("(o h) c -> o (h c)", o=1).to_broadcast([P, D])).then_inc(s_w, 16)
                act.dma_start(dsts, dstp).then_inc(s_dst, 16)
                act.wait_ge(dA, 4)
                act.activation(rstd[:, :], mv[:, :, 1], ACT.Sqrt, bias=epst[:, :]).then_inc(s_std, 1)

                def copy_xt(t, r, n):
                    act.wait_ge(s_xt, t + 1)
                    wait_for(act, s_h, t - 1)
                    act.copy(xnT[:, r, :], bank[r][:, 0:D]).then_inc(s_xtc, 1)

                def copy_h(t, r, n):
                    act.wait_ge(s_h, t + 1)
                    wait_for(act, s_tab[r], 16 * n)
                    act.copy(hrow[:, r, :], bank[2 + r][:, 0:ROW])
                    act.copy(adst[:, bass.ds(t * HEADS, HEADS)], bank[2 + r][:, ROW:ROW + HEADS]).then_inc(s_hr, 1)

                slots(act, NB, 2, [(0, copy_xt), (1, copy_h)])

            @block.tensor
            def _(pe):
                pe.wait_ge(s_const, 7)

                def turn(t, r, n):
                    pe.wait_ge(s_xn, t + 1)
                    wait_for(pe, s_xtc, t - 1)
                    for k in range(KD):
                        mm = pe.transpose(bank[r][:, k * P:(k + 1) * P], xn[:, r, k * P:(k + 1) * P], ident[:, :])
                    mm.then_inc(s_xt, 1)

                def project(t, r, n):
                    pe.wait_ge(s_xtc, t + 1)
                    wait_for(pe, s_hr, t - 1)
                    for k in range(KD):
                        mm = pe.matmul(bank[2 + r][:, 0:ROW + HEADS], xnT[:, r, k * P:(k + 1) * P], Wx[:, k, :],
                                       start=(k == 0), stop=(k == KD - 1))
                    mm.then_inc(s_h, 1)

                slots(pe, NB, 2, [(0, turn), (1, project)])
                pe.wait_ge(s_cnt, NB)
                pe.matmul(bank[4][:, 0:NB], ones[:, :], cnt[:, :], start=True, stop=True).then_inc(s_cps, 1)

            @block.vector
            def _(dve):
                dve.memset(x_sb[:, NB - 1, :], 0.0).then_inc(s_tail0, 1)
                dve.memset(ms[:, :], -BIG)
                dve.memset(epst[:, :], EPS).then_inc(dA, 1)
                dve.memset(ones[:, :], 1.0).then_inc(dA, 1)
                dve.wait_ge(s_x, 32)

                def stats(t, r, n):
                    dve.bn_stats(st6[:, bass.ds(t, 1), :].rearrange("p a s -> p (a s)"),
                                 x_sb[:, bass.ds(t, 1), :].rearrange("p a s -> p (a s)"))

                slots(dve, NB - 1, 2, [(0, stats)])
                dve.bn_stats(st6[:, NB - 1, :], x_sb[:, NB - 1, :]).then_inc(dA, 1)
                dve.wait_ge(dA, 3)

                dve.tensor_tensor(mv[:, :, 0], st6[:, :, 1], st6[:, :, 4], ALU.add).then_inc(dB, 1)
                dve.tensor_tensor(mv[:, :, 1], st6[:, :, 2], st6[:, :, 5], ALU.add).then_inc(dB, 1)
                dve.tensor_tensor(dif[:, :], st6[:, :, 1], st6[:, :, 4], ALU.subtract).then_inc(dB, 1)
                dve.wait_ge(dB, 3)
                dve.scalar_tensor_tensor(dif[:, :], dif[:, :], 0.25, dif[:, :], ALU.mult, ALU.mult).then_inc(dB, 1)
                dve.tensor_scalar(mv[:, :, 0], mv[:, :, 0], 0.5, None, ALU.mult).then_inc(dB, 1)
                dve.wait_ge(dB, 5)
                dve.scalar_tensor_tensor(mv[:, :, 1], mv[:, :, 1], 1.0 / D, dif[:, :], ALU.mult, ALU.add).then_inc(dA, 1)
                dve.wait_ge(s_w, 48)
                for k in range(KD):
                    last = dve.tensor_copy(Wx[:, k, 0:ROW].rearrange("p (h g) -> p h g", g=GC)[:, :, 0:HC],
                                           Ws[:, k, :].rearrange("p (h c) -> p h c", c=HC))
                for i in range(2):
                    for k in range(KD):
                        dve.tensor_tensor(Wt[:, k, :], Ws[:, k, :], att[:, i, :], ALU.mult).then_inc(dA, 1)
                    dve.wait_ge(dA, 4 + 4 * i + 2)
                    for k in range(KD):
                        dst = (Wx[:, k, 0:ROW].rearrange("p (h g) -> p h g", g=GC)[:, :, HC] if i == 0
                               else Wx[:, k, ROW:ROW + HEADS])
                        dve.tensor_reduce(dst, Wt[:, k, :].rearrange("p (h c) -> p h c", c=HC), AX_X, ALU.add).then_inc(dA, 1)
                    dve.wait_ge(dA, 4 + 4 * i + 4)
                dve.wait_ge(s_std, 1)
                dve.reciprocal(rstd[:, :], rstd[:, :]).then_inc(s_rstd, 1)
                dve.wait_ge(s_rstd, 1)

                def normalise(t, r, n):
                    wait_for(dve, s_xt, t - 1)
                    dve.tensor_scalar(xn[:, r, :], x_sb[:, bass.ds(t, 1), :].rearrange("p a s -> p (a s)"),
                                      mv[:, bass.ds(t, 1), 0], rstd[:, bass.ds(t, 1)],
                                      ALU.subtract, ALU.mult).then_inc(s_xn, 1)

                slots(dve, NB, 2, [(0, normalise)])

                dve.wait_ge(s_dst, 16)
                for b in range(1, NB + 1):
                    bound = float(b * P) if b < NB else float(PAD_NODE)
                    wait_for(dve, s_cnt, b - 2)
                    dve.tensor_scalar(cmp[b % 2], dsts, bound, 0.0, ALU.is_lt, ALU.add,
                                      accum_out=cnt[:, b - 1:b]).then_inc(s_cnt, 1)
                dve.wait_ge(s_cps, 1)
                link = sem1("link")
                dve.memset(rp[:, 0:1], 0.0).then_inc(link, 1)
                dve.tensor_copy(rp[:, 1:NB + 1], bank[4][:, 0:NB]).then_inc(link, 1)
                dve.wait_ge(link, 2)
                dve.tensor_tensor(cf[:, :], rp[:, 1:NB + 1], rp[:, 0:NB], ALU.subtract).then_inc(link, 1)
                dve.wait_ge(link, 3)
                dve.tensor_scalar(ci[:, :], cf[:, :], float(STEP - 1), None, ALU.add).then_inc(link, 1)
                dve.wait_ge(link, 4)
                dve.tensor_scalar(ci[:, :], ci[:, :], STEP.bit_length() - 1, None, ALU.logical_shift_right).then_inc(link, 1)
                dve.wait_ge(link, 5)
                dve.tensor_copy(nf[:, :], ci[:, :]).then_inc(link, 1)
                dve.wait_ge(link, 6)
                dve.tensor_tensor_scan(csi[:, :], ones[:, 0:NB], nf[:, :], 0.0, ALU.mult, ALU.add).then_inc(link, 1)
                dve.wait_ge(link, 7)
                dve.tensor_tensor(fb[:, :], csi[:, :], nf[:, :], ALU.subtract).then_inc(link, 1)
                dve.wait_ge(link, 8)
                dve.scalar_tensor_tensor(fb[:, :], fb[:, :], -float(STEP), rp[:, 0:NB], ALU.mult, ALU.add).then_inc(link, 1)
                dve.memset(df[:, NB - 1:NB], 0.0).then_inc(link, 1)
                dve.tensor_copy(sidf[:, :], sid[:, :]).then_inc(link, 1)
                dve.wait_ge(link, 11)
                dve.tensor_tensor(df[:, 0:NB - 1], fb[:, 1:NB], fb[:, 0:NB - 1], ALU.subtract).then_inc(link, 1)
                for q in range(4):
                    dve.tensor_scalar(ge[:, q, :], csi[:, :], sidf[:, q:q + 1], None, ALU.is_le).then_inc(link, 1)
                dve.wait_ge(link, 16)
                dve.tensor_reduce(bs[:, :], ge[:, :, :], AX_X, ALU.add).then_inc(link, 1)
                dve.tensor_tensor(gd[:, :, :], ge[:, :, :], df[:, :].unsqueeze(1).to_broadcast([P, 4, NB]),
                                  ALU.mult).then_inc(link, 1)
                dve.wait_ge(link, 18)
                dve.tensor_reduce(fs[:, :], gd[:, :, :], AX_X, ALU.add).then_inc(link, 1)
                dve.tensor_scalar(bsf[:, :], bs[:, :], float(NB - 1), None, ALU.min).then_inc(link, 1)
                dve.wait_ge(link, 20)
                dve.scalar_tensor_tensor(es[:, :], sidf[:, :], float(STEP), fs[:, :], ALU.mult, ALU.add).then_inc(link, 1)
                dve.tensor_copy(bsi[:, :], bsf[:, :]).then_inc(link, 1)
                dve.wait_ge(link, 22)
                dve.tensor_scalar(esi[:, :], es[:, :], float(E), None, ALU.min).then_inc(link, 1)
                dve.tensor_scalar(bsf[:, :], bsf[:, :], float(P), None, ALU.mult).then_inc(link, 1)
                dve.wait_ge(link, 24)
                dve.engine_nop().then_inc(s_sch, 1)

        with ExitStack() as c2:
            def sb2(name, shape, dt=F32):
                return c2.enter_context(nc.sbuf_tensor(name, shape, dt))

            def sem2(name):
                return ctx.enter_context(nc.semaphore(name))

            ei = sb2("ei", [P, PH, NJ, 4], I32)
            nq = sb2("nq", [P, NJ])
            lq = sb2("lq", [P, NJ])
            drel = sb2("drel", [P, NJ])
            mk = sb2("mk", [P, 2, NJ * HEADS])
            scm = sb2("scm", [P, 2, NJ * HEADS])
            mT = sb2("mT", [NJ * HEADS, P])
            fm = sb2("fm", [NJ * HEADS, P])
            lm = sb2("lm", [P, NJ, HEADS + 1])
            t8 = sb2("t8", [P, NJ])
            cand = sb2("cand", [P, NJ, HEADS])
            cm = sb2("cm", [P, UN, HEADS])
            zb = sb2("zb", [P, UN, HEADS])
            om = sb2("om", [P, UN, HEADS])
            zl = sb2("zl", [P, UN, HEADS])
            dm = sb2("dm", [P, 2, UN, 2 * HEADS])
            dfm = sb2("dfm", [P, 2, UN, HEADS])
            so = sb2("so", [P, 2, UN, HEADS])
            a1 = sb2("a1", [P, NJ, HEADS])
            a2 = sb2("a2", [P, NJ, HEADS])
            a3 = sb2("a3", [P, NJ, HEADS])
            a4 = sb2("a4", [P, NJ, HEADS])

            s_ei = [sem2(f"s_ei{r}") for r in range(PH)]
            s_g = [sem2(f"s_g{r}") for r in range(PH)]
            a_sc, a_mk, a_oh, a_so, a_ex = (sem2(n) for n in ("a_sc", "a_mk", "a_oh", "a_so", "a_ex"))
            p_tr, p_oh, p_fm, p_nm, p_de, p_agg = (sem2(n) for n in ("p_tr", "p_oh", "p_fm", "p_nm", "p_de", "p_agg"))
            d_pre, d_mk, d_oh, d_scan, d_lm, d_ch, d_al, d_msg, d_acc = (
                sem2(n) for n in ("d_pre", "d_mk", "d_oh", "d_scan", "d_lm", "d_ch", "d_al", "d_msg", "d_acc"))
            N_PRE, N_CH, N_AL = 4, 7 + 2 * UN, 4

            bTR, bOH, bNM, bDE, bAG = bank[0], bank[1:3], bank[3], bank[4], bank[5:7]

            def G4(r):
                return G[:, r, :].rearrange("p (j h g) -> p j h g", j=NJ, g=GC)

            block = c2.enter_context(nc.Block())

            def schedule_regs(eng, tab, regs, t, top):
                eng.load(regs, tab[0:1, bass.ds(t * UN, UN)])
                return [eng.snap(q, min_val=0, max_val=top) for q in regs]

            @block.sync
            def _(sp):
                regs = [sp.alloc_register(f"sp_e{u}") for u in range(UN)]

                def load_edges(t, r, n):
                    e0 = schedule_regs(sp, etab, regs, t, E)
                    wait_for(sp, s_g[r], 16 * NJ * n)
                    wait_for(sp, d_pre, N_PRE * (t - PH + 1))
                    for u in range(UN):
                        sp.dma_start(ei[:, r, u * SUB:(u + 1) * SUB, :].rearrange("p s c -> p (s c)"),
                                     ed[bass.ds(e0[u], STEP), :].rearrange("(p s) c -> p (s c)", s=SUB)).then_inc(s_ei[r], 16)

                slots(sp, NBATCH, PH, [(0, load_edges)])

            @block.gpsimd
            def _(pool):
                def gather(t, r, n):
                    pool.wait_ge(s_ei[r], 16 * UN * (n + 1))
                    own(pool, gate)
                    if not (isinstance(t, int) and t < PH):
                        pool.wait_ge(p_agg, UN * (t - PH + 1))
                        own(pool, gate)
                    for j in range(NJ):
                        pool.indirect_dma_start(G[:, r, j * ROW:(j + 1) * ROW], None, table,
                                                bass.IndirectOffsetOnAxis(ei[:, r, j, 0:1], 0)).then_inc(s_g[r], 16)

                slots(pool, NBATCH, PH, [(0, gather)])

            @block.scalar
            def _(act):
                def scale_old(t, r, n):
                    act.wait_ge(d_ch, N_CH * (t + 1))
                    act.activation(so[:, r % 2], dfm[:, r % 2], ACT.Exp).then_inc(a_so, 1)

                def take_asrc(t, r, n):
                    act.wait_ge(s_g[r], 16 * NJ * (n + 1))
                    wait_for(act, d_al, N_AL * (t - 1))
                    act.copy(scm[:, r % 2].rearrange("p (j h) -> p j h", h=HEADS), G4(r)[:, :, :, HC]).then_inc(a_sc, 1)

                def exps(t, r, n):
                    act.wait_ge(d_al, N_AL * (t + 1))
                    act.activation(G4(r)[:, :, :, HC], a4[:, :, :], ACT.Exp).then_inc(a_ex, 1)

                def copy_mask(t, r, n):
                    act.wait_ge(p_tr, t + 1)
                    wait_for(act, d_scan, t)
                    act.copy(mT[:, :], bTR[0:NJ * HEADS, P:2 * P]).then_inc(a_mk, 1)

                def copy_oht(t, r, n):
                    for half in range(2):
                        act.wait_ge(p_oh, 2 * t + half + 1)
                        if half == 0:
                            wait_for(act, p_de, t - 1)
                        act.copy(ohT[:, r % 2, half * 4:half * 4 + 4, :].rearrange("p j e -> p (j e)"),
                                 bOH[half][:, :]).then_inc(a_oh, 1)

                slots(act, NBATCH, PH, [(1, scale_old), (0, take_asrc), (1, exps), (0, copy_mask), (0, copy_oht)])

            @block.tensor
            def _(pe):
                def spread(t, r, n):
                    pe.wait_ge(a_oh, 2 * t + 2)
                    pe.wait_ge(d_ch, N_CH * (t + 1))
                    wait_for(pe, d_al, N_AL * t)
                    for j in range(NJ):
                        mm = pe.matmul(bDE[:, j * 16:j * 16 + 16], ohT[:, r % 2, j, :], dm[:, r % 2, j // SUB, :],
                                       start=True, stop=True)
                    mm.then_inc(p_de, 1)

                def turn(t, r, n):
                    wait_for(pe, d_lm, t)
                    pe.wait_ge(a_sc, t + 1)
                    pe.wait_ge(d_mk, t + 1)
                    own(pe, gate_pe)
                    pe.transpose(bTR[0:NJ * HEADS, 0:P], scm[:, r % 2], ident[:, :])
                    pe.transpose(bTR[0:NJ * HEADS, P:2 * P], mk[:, r % 2], ident[:, :]).then_inc(p_tr, 1)

                def turn_oh(t, r, n):
                    for half in range(2):
                        pe.wait_ge(d_oh, 2 * t + half + 1)
                        wait_for(pe, a_oh, 2 * (t - 1) + half + 1)
                        for j in range(4):
                            mm = pe.transpose(bOH[half][:, j * P:(j + 1) * P], oh[:, r % 2, half * 4 + j, :], ident[:, :])
                        mm.then_inc(p_oh, 1)

                def turn_max(t, r, n):
                    pe.wait_ge(d_scan, t + 1)
                    own(pe, gate_pe)
                    pe.transpose(bTR[:, 2 * P:2 * P + NJ * HEADS], fm[:, :], ident[0:NJ * HEADS, 0:NJ * HEADS]).then_inc(p_fm, 1)

                def node_max(t, r, n):
                    pe.wait_ge(d_lm, t + 1)
                    wait_for(pe, d_ch, N_CH * t)
                    for j in range(NJ):
                        mm = pe.matmul(bNM[:, j * 9:j * 9 + 9], oh[:, r % 2, j, :], lm[:, j, :], start=True, stop=True)
                    mm.then_inc(p_nm, 1)

                def total(u):
                    def f(t, r, n):
                        pe.wait_ge(d_msg, UN * t + u + 1)
                        wait_for(pe, d_acc, UN * t + u - 1)
                        for s in range(SUB):
                            j = u * SUB + s
                            mm = pe.matmul(bAG[u % 2][:, 0:ROW], oh[:, r % 2, j, :], G[:, r, j * ROW:(j + 1) * ROW],
                                           start=(s == 0), stop=(s == SUB - 1))
                        mm.then_inc(p_agg, 1)
                    return f

                slots(pe, NBATCH, PH, [(1, spread), (0, turn), (0, turn_oh), (0, turn_max), (1, total(0)),
                                       (0, node_max), (1, total(1)), (1, total(2)), (1, total(3))])

            @block.vector
            def _(dve):
                regs_now = [dve.alloc_register(f"dve_b{u}") for u in range(UN)]
                regs_old = [dve.alloc_register(f"dve_o{u}") for u in range(UN)]
                now = {}
                old = {}

                def edge_marks(t, r, n):
                    e = ei[:, r]
                    dve.wait_ge(s_ei[r], 16 * UN * (n + 1))
                    dve.tensor_tensor(nq[:, :], e[:, :, 2], e[:, :, 1], ALU.not_equal).then_inc(d_pre, 1)
                    dve.tensor_tensor(lq[:, :], e[:, :, 2], e[:, :, 3], ALU.not_equal).then_inc(d_pre, 1)
                    dve.tensor_tensor(drel[:, :].rearrange("p (u s) -> p u s", s=SUB),
                                      e[:, :, 2].rearrange("p (u s) -> p u s", s=SUB),
                                      bbase[:, bass.ds(t * UN, UN)].unsqueeze(2).to_broadcast([P, UN, SUB]),
                                      ALU.subtract).then_inc(d_pre, 1)
                    dve.wait_ge(d_pre, N_PRE * t + 3)
                    wait_for(dve, p_tr, t - 1)
                    dve.tensor_scalar(mk[:, r % 2].rearrange("p (j h) -> p j h", h=HEADS),
                                      nq[:, :].unsqueeze(2).to_broadcast([P, NJ, HEADS]), -BIG, None, ALU.mult).then_inc(d_mk, 1)
                    wait_for(dve, p_nm, t)
                    dve.tensor_scalar(lm[:, :, HEADS], lq[:, :], is_last_p[:, 0:1], None, ALU.max).then_inc(d_pre, 1)
                    wait_for(dve, p_agg, UN * (t - 1))
                    for j in range(NJ):
                        o = dve.tensor_scalar(oh[:, r % 2, j, :], iota_n[:, :], drel[:, j:j + 1], None, ALU.is_equal)
                        if j % 4 == 3:
                            o.then_inc(d_oh, 1)

                def alphas(t, r, n):
                    de = bDE[:, 0:NJ * 16].rearrange("p (j c) -> p j c", c=16)
                    dve.wait_ge(p_de, t + 1)
                    dve.tensor_tensor(a1[:, :, :], scm[:, r % 2].rearrange("p (j h) -> p j h", h=HEADS),
                                      de[:, :, 0:HEADS], ALU.add).then_inc(d_al, 1)
                    dve.wait_ge(d_al, N_AL * t + 1)
                    dve.scalar_tensor_tensor(a2[:, :, :], a1[:, :, :], SLOPE, a1[:, :, :], ALU.mult, ALU.max).then_inc(d_al, 1)
                    dve.wait_ge(d_al, N_AL * t + 2)
                    dve.tensor_tensor(a3[:, :, :], a2[:, :, :], de[:, :, HEADS:16], ALU.subtract).then_inc(d_al, 1)
                    dve.wait_ge(d_al, N_AL * t + 3)
                    wait_for(dve, a_ex, t)
                    dve.tensor_scalar(a4[:, :, :], a3[:, :, :], 0.0, None, ALU.min).then_inc(d_al, 1)

                def scan(t, r, n):
                    dve.wait_ge(a_mk, t + 1)
                    wait_for(dve, p_fm, t)
                    dve.tensor_tensor_scan(fm[:, :], mT[:, :], bTR[0:NJ * HEADS, 0:P], -BIG, ALU.add, ALU.max).then_inc(d_scan, 1)

                def last_max(t, r, n):
                    dve.wait_ge(p_fm, t + 1)
                    dve.wait_ge(d_pre, N_PRE * (t + 1))
                    dve.tensor_tensor(lm[:, :, 0:HEADS],
                                      bTR[:, 2 * P:2 * P + NJ * HEADS].rearrange("p (j h) -> p j h", h=HEADS),
                                      lm[:, :, HEADS].unsqueeze(2).to_broadcast([P, NJ, HEADS]), ALU.mult).then_inc(d_lm, 1)

                def maxima(t, r, n):
                    nm = bNM[:, 0:NJ * 9].rearrange("p (j c) -> p j c", c=9)
                    c0 = N_CH * t
                    b = now[id(t)]
                    wait_for(dve, p_de, t - 1)
                    wait_for(dve, a_so, t - 1)
                    dve.wait_ge(p_nm, t + 1)
                    dve.tensor_scalar(t8[:, :], nm[:, :, HEADS], BIG, -BIG, ALU.mult, ALU.add).then_inc(d_ch, 1)
                    dve.wait_ge(d_ch, c0 + 1)
                    dve.tensor_tensor(cand[:, :, :], nm[:, :, 0:HEADS], t8[:, :].unsqueeze(2).to_broadcast([P, NJ, HEADS]),
                                      ALU.add).then_inc(d_ch, 1)
                    dve.wait_ge(d_ch, c0 + 2)
                    cs = cand[:, :, :].rearrange("p (u s) h -> p u s h", s=SUB)
                    dve.tensor_tensor(cm[:, :, :], cs[:, :, 0, :], cs[:, :, 1, :], ALU.max).then_inc(d_ch, 1)
                    dve.wait_ge(d_ch, c0 + 3)
                    for u in range(UN):
                        dve.tensor_copy(dm[:, r % 2, u, 0:HEADS], adst[:, bass.ds(b[u] * HEADS, HEADS)])
                        o = dve.tensor_tensor(zb[:, u, :], cm[:, u, :], adst[:, bass.ds(b[u] * HEADS, HEADS)], ALU.add)
                    o.then_inc(d_ch, 1)
                    dve.wait_ge(d_ch, c0 + 4)
                    dve.scalar_tensor_tensor(zl[:, :, :], zb[:, :, :], SLOPE, zb[:, :, :], ALU.mult, ALU.max).then_inc(d_ch, 1)
                    for u in range(UN):
                        mb = ms[:, bass.ds(b[u] * HEADS, HEADS)]
                        dve.wait_ge(d_ch, c0 + 5 + 2 * u)
                        dve.tensor_copy(om[:, u, :], mb).then_inc(d_ch, 1)
                        dve.wait_ge(d_ch, c0 + 6 + 2 * u)
                        dve.tensor_tensor(mb, om[:, u, :], zl[:, u, :], ALU.max).then_inc(d_ch, 1)
                    dve.tensor_tensor(dm[:, r % 2, :, HEADS:2 * HEADS], om[:, :, :], zl[:, :, :], ALU.max).then_inc(d_ch, 1)
                    dve.wait_ge(d_ch, c0 + 6 + 2 * UN)
                    dve.tensor_tensor(dfm[:, r % 2], om[:, :, :], dm[:, r % 2, :, HEADS:2 * HEADS],
                                      ALU.subtract).then_inc(d_ch, 1)

                def weigh(u):
                    def f(t, r, n):
                        if u == 0:
                            dve.wait_ge(a_ex, t + 1)
                        g = G4(r)[:, u * SUB:(u + 1) * SUB].rearrange("p s h g -> p (s h) g")
                        dve.tensor_tensor(g[:, :, 0:HC], g[:, :, 0:HC], g[:, :, HC:GC].to_broadcast([P, SUB * HEADS, HC]),
                                          ALU.mult).then_inc(d_msg, 1)
                    return f

                def gather_sums(u):
                    def f(t, r, n):
                        a = acc[:, bass.ds(old[id(t)][u] * ROW, ROW)].rearrange("p (h g) -> p h g", g=GC)
                        if u == 0:
                            dve.wait_ge(a_so, t + 1)
                        wait_for(dve, d_acc, UN * t + u)
                        dve.tensor_tensor(a, a, so[:, r % 2, u, :].unsqueeze(2).to_broadcast([P, HEADS, GC]),
                                          ALU.mult).then_inc(d_sc, 1)
                        dve.wait_ge(d_sc, UN * t + u + 1)
                        dve.wait_ge(p_agg, UN * t + u + 1)
                        dve.tensor_tensor(a, a, bAG[u % 2][:, 0:ROW].rearrange("p (h g) -> p h g", g=GC), ALU.add).then_inc(d_acc, 1)
                    return f

                d_sc = sem2("d_sc")

                def regs_for_now(t, r, n):
                    now.clear()
                    now[id(t)] = schedule_regs(dve, btab, regs_now, t, NB - 1)

                def chain(t, r, n):
                    regs_for_now(t, r, n)
                    maxima(t, r, n)

                def sums(t, r, n):
                    old.clear()
                    old[id(t)] = schedule_regs(dve, btab, regs_old, t, NB - 1)
                    gather_sums(0)(t, r, n)

                def sums_rest(t, r, n):
                    old[id(t)] = list(old.values())[0]
                    for u in range(1, UN):
                        gather_sums(u)(t, r, n)

                slots(dve, NBATCH, PH, [(0, edge_marks), (1, alphas), (0, scan), (1, weigh(0)), (1, weigh(1)),
                                        (0, last_max), (1, weigh(2)), (1, weigh(3)), (1, sums), (0, chain),
                                        (1, sums_rest)])

        rw = sb("rw", [P, NB])
        gidx = sb("gidx", [P, NB], I32)
        with ExitStack() as c3:
            def sb3(name, shape, dt=F32):
                return c3.enter_context(nc.sbuf_tensor(name, shape, dt))

            def sem3(name):
                return ctx.enter_context(nc.semaphore(name))

            biasT = sb3("biasT", [P, 3, D])
            gw = sb3("gw", [P, KD, NX])
            gb = sb3("gb", [P, NX])
            nmr = sb3("nmr", [P, NB])
            rden = sb3("rden", [P, NB, HEADS])
            st = sb3("st", [P, NB, 6])
            mean = sb3("mean", [P, NB])
            var = sb3("var", [P, NB])
            dif = sb3("dif3", [P, NB])
            rs = sb3("rs", [P, NB])
            xr, xb, o1, o2 = (G[:, i, 0:2 * D].rearrange("p (r d) -> p r d", r=2) for i in range(4))
            exb, gn, m1, xt2 = (G[:, i, 2 * D:4 * D].rearrange("p (r d) -> p r d", r=2) for i in range(4))
            xs = sb3("xs", [P, 2, D])
            ohf = oh[:, :, :, :].rearrange("p a b c -> p (a b c)")
            ohTf = ohT[:, :, :, :].rearrange("p a b c -> p (a b c)")
            NE = NB * NX

            def small(i):
                base = (ohf, ohTf)[i // 4]
                return base[:, (i % 4) * 512:(i % 4) * 512 + NE].rearrange("p (t e) -> p t e", e=NX)

            L, dl, pe_, eq, used, first, tot, inc = (small(i) for i in range(8))
            pos = G[:, 0, 1024:1024 + NE].rearrange("p (t e) -> p t e", e=NX)
            fp = G[:, 1, 1024:1024 + NE].rearrange("p (t e) -> p t e", e=NX)
            fe = G[:, 2, 1024:1024 + NE].rearrange("p (t e) -> p t e", e=NX)
            mx, ssum, prb, posf, ef, fsum, kept, slot, sfar, pcl, gf = (sb3(f"tk{i}", [P, NB]) for i in range(11))
            sidx = sb3("sidx", [P, NB], I32)
            tri = sb3("tri", [P, P])
            e8 = sb3("e8", [P, NX])
            vcol = sb3("vcol", [P, 1])

            s_par = sem3("s_par")
            c_const = sem3("c_const")
            v_ = sem3("v_")
            v_var, a_std, a_p = (sem3(n) for n in ("v_var", "a_std", "a_p"))
            r_xr, r_xb, r_o1, r_o2, r_ex, r_e1, r_v, r_st = (sem3("r_" + n) for n in "xr xb o1 o2 ex e1 v st".split())
            q_g, q_xb, q_m, q_x1, q_st = (sem3("q_" + n) for n in "g xb m x1 st".split())
            w_n, w_k, w_t, w_tc, w_l, w_L = (sem3("w_" + n) for n in "n k t tc l L".split())
            v_first, p_cum, v_idx, s_sc = (sem3(n) for n in ("v_first", "p_cum", "v_idx", "s_sc"))
            v_nmr, v_dl = sem3("v_nmr"), sem3("v_dl")

            def tile(a, t):
                return a[:, bass.ds(t, 1), :].rearrange("p a s -> p (a s)")

            def acc_row(t):
                return acc[:, bass.ds(t * ROW, D)]

            block = c3.enter_context(nc.Block())

            @block.sync
            def _(sp):
                for i, a in enumerate((bias, ln_s, ln_b)):
                    sp.dma_start(biasT[:, i, :], a.rearrange("(o d) -> o d", o=1).to_broadcast([P, D])).then_inc(s_par, 16)
                sp.dma_start(gw[:, :, :], gate_w.rearrange("(k p) e -> p k e", p=P)).then_inc(s_par, 16)
                sp.dma_start(gb[:, :], gate_b.rearrange("(o d) -> o d", o=1).to_broadcast([P, NX])).then_inc(s_par, 16)

            @block.gpsimd
            def _(pool):
                pool.memset(tri[:, :], 1.0).then_inc(c_const, 1)
                pool.memset(vcol[:, :], 1.0).then_inc(c_const, 1)
                pool.iota(e8[:, :], [[1, NX]], base=0, channel_multiplier=0,
                          allow_small_or_imprecise_dtypes=True).then_inc(c_const, 1)
                pool.wait_ge(c_const, 3)
                pool.affine_select(out=tri[:, :], in_=tri[:, :], compare_op=ALU.is_ge, fill=0.0, base=0,
                                   pattern=[[1, P]], channel_multiplier=-1).then_inc(c_const, 1)
                pool.affine_select(out=vcol[:, :], in_=vcol[:, :], compare_op=ALU.is_ge, fill=0.0, base=TAIL - 1,
                                   pattern=[[0, 1]], channel_multiplier=-1).then_inc(c_const, 1)
                pool.wait_ge(s_par, 80)

                def add_bias(t, r, n):
                    pool.wait_ge(r_xr, t + 1)
                    wait_for(pool, r_o2, t - 1)
                    pool.tensor_tensor(xb[:, r, :], xr[:, r, :], biasT[:, 0, :], ALU.add).then_inc(r_xb, 1)

                slots(pool, NB, 2, [(0, add_bias)])

                def add_lnb(t, r, n):
                    pool.tensor_tensor(tile(x_sb, t), tile(x_sb, t), biasT[:, 2, :], ALU.add).then_inc(q_xb, 1)

                slots(pool, NB, 2, [(0, add_lnb)])

                def keep_xn(t, r, n):
                    pool.wait_ge(w_n, t + 1)
                    pool.tensor_copy(acc_row(t), xs[:, r, :]).then_inc(w_k, 1)

                slots(pool, NB, 2, [(0, keep_xn)])
                pool.wait_ge(v_idx, 1)
                pool.wait_ge(w_k, NB)
                for t in range(NB):
                    pool.indirect_dma_start(xbuf, bass.IndirectOffsetOnAxis(sidx[:, t:t + 1], 0),
                                            acc[:, t * ROW:t * ROW + D], None,
                                            bounds_check=NX * SL - 1, oob_is_err=False).then_inc(s_sc, 16)
                pool.wait_ge(s_sc, 16 * NB)

            @block.scalar
            def _(act):
                act.wait_ge(v_nmr, 1)

                def norm_x(t, r, n):
                    wait_for(act, r_xb, t - 1)
                    own(act, gate_act)
                    act.activation(xr[:, r, :], tile(x_sb, t), ACT.Identity, scale=rstd[:, bass.ds(t, 1)],
                                   bias=nmr[:, bass.ds(t, 1)]).then_inc(r_xr, 1)

                def exp_o(t, r, n):
                    act.wait_ge(r_o2, t + 1)
                    wait_for(act, r_v, t - 1)
                    act.activation(exb[:, r, :], o2[:, r, :], ACT.Exp).then_inc(r_ex, 1)

                slots(act, NB, 2, [(0, norm_x), (1, exp_o)])
                act.wait_ge(v_var, 1)
                act.activation(rs[:, :], var[:, :], ACT.Sqrt, bias=epst[:, :]).then_inc(a_std, 1)
                act.wait_ge(v_nmr, 2)

                def norm_v(t, r, n):
                    wait_for(act, q_m, t - 1)
                    own(act, gate_act)
                    act.activation(gn[:, r, :], acc_row(t), ACT.Identity, scale=rs[:, bass.ds(t, 1)],
                                   bias=nmr[:, bass.ds(t, 1)]).then_inc(q_g, 1)

                slots(act, NB, 2, [(0, norm_v)])
                act.wait_ge(v_var, 2)
                act.activation(rs[:, :], var[:, :], ACT.Sqrt, bias=epst[:, :]).then_inc(a_std, 1)
                act.wait_ge(v_nmr, 3)

                def norm_x1(t, r, n):
                    wait_for(act, w_t, t - 1)
                    wait_for(act, w_k, t - 1)
                    own(act, gate_act)
                    act.activation(xs[:, r, :], tile(x_sb, t), ACT.Identity, scale=rs[:, bass.ds(t, 1)],
                                   bias=nmr[:, bass.ds(t, 1)]).then_inc(w_n, 1)

                def copy_xt(t, r, n):
                    act.wait_ge(w_t, t + 1)
                    wait_for(act, w_l, t - 1)
                    act.copy(xt2[:, r, :], bank[r][:, 0:D]).then_inc(w_tc, 1)

                slots(act, NB, 2, [(0, norm_x1), (1, copy_xt)])
                act.wait_ge(v_dl, 1)
                act.activation(pe_, dl, ACT.Exp).then_inc(a_p, 1)

            @block.tensor
            def _(pe):
                pe.wait_ge(s_par, 80)
                pe.wait_ge(c_const, 5)

                def turn(t, r, n):
                    pe.wait_ge(w_n, t + 1)
                    wait_for(pe, w_tc, t - 1)
                    for k in range(KD):
                        mm = pe.transpose(bank[r][:, k * P:(k + 1) * P],
                                          xs[:, r, k * P:(k + 1) * P], ident[:, :])
                    mm.then_inc(w_t, 1)

                def logits(t, r, n):
                    pe.wait_ge(w_tc, t + 1)
                    wait_for(pe, w_L, t - 1)
                    for k in range(KD):
                        mm = pe.matmul(bank[2 + r][:, 0:NX], xt2[:, r, k * P:(k + 1) * P], gw[:, k, :],
                                       start=(k == 0), stop=(k == KD - 1))
                    mm.then_inc(w_l, 1)

                slots(pe, NB, 2, [(0, turn), (1, logits)])
                pe.wait_ge(v_first, 1)
                pe.matmul(bank[4][:, 0:NE], tri[:, :], first.rearrange("p t e -> p (t e)"), start=True, stop=True)
                pe.matmul(bank[5][:, 0:NE], ones[:, :], first.rearrange("p t e -> p (t e)"), start=True,
                          stop=True).then_inc(p_cum, 1)

            @block.vector
            def _(dve):
                link = [0]

                def chained(ins, wait=True):
                    link[0] += 1
                    ins.then_inc(v_, 1)
                    if wait:
                        dve.wait_ge(v_, link[0])

                def join_stats(n):
                    chained(dve.tensor_tensor(mean[:, :], st[:, :, 1], st[:, :, 4], ALU.add), False)
                    chained(dve.tensor_tensor(var[:, :], st[:, :, 2], st[:, :, 5], ALU.add), False)
                    chained(dve.tensor_tensor(dif[:, :], st[:, :, 1], st[:, :, 4], ALU.subtract))
                    chained(dve.scalar_tensor_tensor(dif[:, :], dif[:, :], 0.25, dif[:, :], ALU.mult, ALU.mult))
                    dve.scalar_tensor_tensor(var[:, :], var[:, :], 1.0 / D, dif[:, :], ALU.mult, ALU.add).then_inc(v_var, 1)
                    dve.wait_ge(a_std, n)
                    chained(dve.reciprocal(rs[:, :], rs[:, :]))
                    dve.scalar_tensor_tensor(nmr[:, :], mean[:, :], -0.5, rs[:, :], ALU.mult, ALU.mult).then_inc(v_nmr, 1)

                dve.scalar_tensor_tensor(nmr[:, :], mv[:, :, 0], -1.0, rstd[:, :], ALU.mult, ALU.mult).then_inc(v_nmr, 1)
                dens = acc[:, :].rearrange("p (t h g) -> p (t h) g", h=HEADS, g=GC)[:, :, HC]
                rflat = rden[:, :, :].rearrange("p t h -> p (t h)")
                chained(dve.tensor_scalar(rflat, dens, 1e-16, None, ALU.add))
                chained(dve.reciprocal(rflat, rflat))

                def residual(t, r, n):
                    wait_for(dve, r_o2, t - 1)
                    dve.tensor_tensor(o1[:, r, :].rearrange("p (h c) -> p h c", c=HC),
                                      acc[:, bass.ds(t * ROW, ROW)].rearrange("p (h g) -> p h g", g=GC)[:, :, 0:HC],
                                      rden[:, bass.ds(t, 1), :].rearrange("p a h -> p (a h)").unsqueeze(2).to_broadcast([P, HEADS, HC]),
                                      ALU.mult).then_inc(r_o1, 1)
                    dve.wait_ge(r_o1, t + 1)
                    dve.wait_ge(r_xb, t + 1)
                    wait_for(dve, r_v, t - 1)
                    dve.tensor_tensor(o2[:, r, :], o1[:, r, :], xb[:, r, :], ALU.add).then_inc(r_o2, 1)

                def elu(t, r, n):
                    dve.wait_ge(r_ex, t + 1)
                    dve.tensor_scalar(exb[:, r, :], exb[:, r, :], 1.0, -1.0, ALU.min, ALU.add).then_inc(r_e1, 1)
                    dve.wait_ge(r_e1, t + 1)
                    dve.scalar_tensor_tensor(acc_row(t), o2[:, r, :], 0.0, exb[:, r, :], ALU.max, ALU.add).then_inc(r_v, 1)
                    dve.wait_ge(r_v, t + 1)
                    dve.bn_stats(tile(st, t), acc_row(t)).then_inc(r_st, 1)

                slots(dve, NB, 2, [(0, residual), (1, elu)])
                dve.wait_ge(r_st, NB)
                join_stats(1)

                def second(t, r, n):
                    dve.wait_ge(q_g, t + 1)
                    wait_for(dve, q_x1, t - 1)
                    dve.tensor_tensor(m1[:, r, :], gn[:, r, :], biasT[:, 1, :], ALU.mult).then_inc(q_m, 1)

                def second_add(t, r, n):
                    dve.wait_ge(q_m, t + 1)
                    dve.wait_ge(q_xb, t + 1)
                    dve.tensor_tensor(tile(x_sb, t), m1[:, r, :], tile(x_sb, t), ALU.add).then_inc(q_x1, 1)
                    dve.wait_ge(q_x1, t + 1)
                    dve.bn_stats(tile(st, t), tile(x_sb, t)).then_inc(q_st, 1)

                slots(dve, NB, 2, [(0, second), (1, second_add)])
                dve.wait_ge(q_st, NB)
                join_stats(2)

                def take_logits(t, r, n):
                    dve.wait_ge(w_l, t + 1)
                    dve.tensor_tensor(L[:, bass.ds(t, 1), :].rearrange("p a e -> p (a e)"), bank[2 + r][:, 0:NX], gb[:, :],
                                      ALU.add).then_inc(w_L, 1)

                slots(dve, NB, 2, [(0, take_logits)])
                dve.wait_ge(w_L, NB)

                def over_e(a):
                    return a[:, :].unsqueeze(2).to_broadcast([P, NB, NX])

                chained(dve.tensor_reduce(mx[:, :], L, AX_X, ALU.max))
                dve.tensor_tensor(dl, L, over_e(mx), ALU.subtract).then_inc(v_dl, 1)
                dve.wait_ge(a_p, 1)
                chained(dve.tensor_reduce(ssum[:, :], pe_, AX_X, ALU.add), False)
                chained(dve.tensor_scalar(eq, pe_, 1.0, None, ALU.is_ge), False)
                chained(dve.memset(used, 0.0))
                chained(dve.reciprocal(prb[:, :], ssum[:, :]), False)
                for e in range(1, NX):
                    chained(dve.tensor_tensor(used[:, :, e], used[:, :, e - 1], eq[:, :, e - 1], ALU.max))
                chained(dve.tensor_tensor(first, eq, used, ALU.is_gt))
                dve.wait_ge(c_const, 5)
                dve.tensor_scalar(first[:, NB - 1, :], first[:, NB - 1, :], vcol[:, 0:1], None, ALU.mult).then_inc(v_first, 1)
                dve.wait_ge(p_cum, 1)
                chained(dve.tensor_copy(tot.rearrange("p t e -> p (t e)"), bank[5][:, 0:NE]))
                for e in range(NX):
                    chained(dve.tensor_tensor_scan(inc[:, :, e], ones[:, 0:NB], tot[:, :, e], 0.0, ALU.mult, ALU.add), e == NX - 1)
                chained(dve.tensor_tensor(inc, inc, tot, ALU.subtract))
                chained(dve.scalar_tensor_tensor(pos.rearrange("p t e -> p (t e)"), bank[4][:, 0:NE], -1.0,
                                                 inc.rearrange("p t e -> p (t e)"), ALU.add, ALU.add))
                chained(dve.tensor_tensor(fp, pos, first, ALU.mult), False)
                chained(dve.tensor_tensor(fe, first, e8[:, :].unsqueeze(1).to_broadcast([P, NB, NX]), ALU.mult))
                chained(dve.tensor_reduce(posf[:, :], fp, AX_X, ALU.add), False)
                chained(dve.tensor_reduce(ef[:, :], fe, AX_X, ALU.add), False)
                chained(dve.tensor_reduce(fsum[:, :], first, AX_X, ALU.add))
                chained(dve.scalar_tensor_tensor(kept[:, :], posf[:, :], float(CAP), fsum[:, :], ALU.is_lt, ALU.mult), False)
                chained(dve.scalar_tensor_tensor(slot[:, :], ef[:, :], float(SL), posf[:, :], ALU.mult, ALU.add), False)
                chained(dve.tensor_scalar(pcl[:, :], posf[:, :], float(CAP - 1), None, ALU.min))
                chained(dve.scalar_tensor_tensor(sfar[:, :], slot[:, :], -float(FAR), kept[:, :], ALU.add, ALU.mult), False)
                chained(dve.scalar_tensor_tensor(gf[:, :], ef[:, :], float(SL), pcl[:, :], ALU.mult, ALU.add), False)
                chained(dve.tensor_tensor(rw[:, :], prb[:, :], kept[:, :], ALU.mult))
                chained(dve.tensor_copy(gidx[:, :], gf[:, :]))
                dve.tensor_scalar(sidx[:, :], sfar[:, :], float(FAR), None, ALU.add).then_inc(v_idx, 1)

        with ExitStack() as c4:
            def sem4(name):
                return ctx.enter_context(nc.semaphore(name))

            CH = SL // 2
            MT = CH // P
            NI = 2 * NX
            w1s = [acc[:, i * KD * F:(i + 1) * KD * F].rearrange("p (k f) -> p k f", k=KD) for i in range(2)]
            o = 2 * KD * F
            w2s = [acc[:, o + i * FC * D:o + (i + 1) * FC * D].rearrange("p (c d) -> p c d", c=FC) for i in range(2)]
            o += 2 * FC * D
            xe = [acc[:, o + i * MT * D:o + (i + 1) * MT * D] for i in range(4)]
            assert o + 4 * MT * D <= NB * ROW and 4 * P * MT == 4 * CH
            h1 = [G[:, 2 * i:2 * i + 2, :].rearrange("p a b -> p (a b)")[:, 0:FC * CH].rearrange("p (c n) -> p c n", c=FC)
                  for i in range(2)]
            xT = [oh[:, i].rearrange("p a b -> p (a b)")[:, 0:KD * CH].rearrange("p (k n) -> p k n", k=KD) for i in range(2)]
            yo = [ohT[:, i].rearrange("p a b -> p (a b)")[:, 0:MT * D].rearrange("p (m d) -> p m d", m=MT) for i in range(2)]
            b1s = c4.enter_context(nc.sbuf_tensor("b1s", [P, NX * FC], F32))
            b2s = c4.enter_context(nc.sbuf_tensor("b2s", [P, NX * D], F32))

            s_b = sem4("s_b")
            s_wt = [sem4(f"s_wt{i}") for i in range(2)]
            s_xe = [sem4(f"s_xe{i}") for i in range(4)]
            s_yo = [sem4(f"s_yo{i}") for i in range(2)]
            m_t, m_th, m_xt, m_h, m_relu, m_y, m_yo = (sem4("m_" + n) for n in "t th xt h relu y yo".split())
            block = c4.enter_context(nc.Block())

            @block.sync
            def _(sp):
                sp.dma_start(b1s[:, :], b1).then_inc(s_b, 16)
                sp.dma_start(b2s[:, :], b2.rearrange("(o e) d -> o (e d)", o=1).to_broadcast([P, NX * D])).then_inc(s_b, 16)

                def load(t, r, n):
                    wait_for(sp, m_t, t - 3)
                    sp.dma_start(xe[r].rearrange("p (m d) -> p m d", m=MT),
                                 xbuf[bass.ds(t * CH, CH), :].rearrange("(m p) d -> p m d", p=P)).then_inc(s_xe[r], 16)
                    if r % 2 == 0:
                        e = 2 * n + r // 2
                        wait_for(sp, m_y, MT * (t - 2))
                        sp.dma_start(w1s[r // 2], w1[bass.ds(e, 1)].rearrange("o (k p) f -> p (o k) f", p=P)).then_inc(s_wt[r // 2], 16)
                        sp.dma_start(w2s[r // 2], w2[bass.ds(e, 1)].rearrange("o (c p) d -> p (o c) d", p=P)).then_inc(s_wt[r // 2], 16)

                slots(sp, NI, 4, [(0, load)])

            @block.gpsimd
            def _(pool):
                def store(t, r, n):
                    pool.wait_ge(m_yo, MT * (t + 1))
                    own(pool, gate)
                    pool.dma_start(ybuf[bass.ds(t * CH, CH), :].rearrange("(m p) d -> p m d", p=P), yo[r % 2]).then_inc(s_yo[r % 2], 16)

                slots(pool, NI, 4, [(0, store)])
                for i in range(2):
                    pool.wait_ge(s_yo[i], 16 * (NI // 2))

            @block.tensor
            def _(pe):
                def turn(t, r, n):
                    pe.wait_ge(s_xe[r], 16 * (n + 1))
                    for half in range(2):
                        wait_for(pe, m_xt, 2 * t + half - 1)
                        for m in range(MT // 2):
                            for k in range(KD):
                                c = half * (MT // 2) + m
                                mm = pe.transpose(bank[half][:, k * 256 + m * P:k * 256 + (m + 1) * P],
                                                  xe[r][:, c * D + k * P:c * D + (k + 1) * P], ident[:, :])
                        mm.then_inc(m_t if half == 1 else m_th, 1)

                def up(t, r, n):
                    pe.wait_ge(m_xt, 2 * t + 2)
                    pe.wait_ge(s_wt[r // 2], 32 * (n + 1))
                    for c in range(FC):
                        wait_for(pe, m_relu, FC * t + c - 3)
                        for k in range(KD):
                            mm = pe.matmul(bank[2 + c % 4][:, 0:CH], w1s[r // 2][:, k, c * P:(c + 1) * P], xT[r % 2][:, k, :],
                                           start=(k == 0), stop=(k == KD - 1))
                        mm.then_inc(m_h, 1)

                def down(t, r, n):
                    pe.wait_ge(m_relu, FC * (t + 1))
                    for m in range(MT):
                        wait_for(pe, m_yo, MT * t + m - 1)
                        for c in range(FC):
                            mm = pe.matmul(bank[6 + m % 2][:, 0:D], h1[r % 2][:, c, m * P:(m + 1) * P], w2s[r // 2][:, c, :],
                                           start=(c == 0), stop=(c == FC - 1))
                        mm.then_inc(m_y, 1)

                slots(pe, NI, 4, [(1, up), (0, turn), (1, down)])

            @block.scalar
            def _(act):
                act.wait_ge(s_b, 32)

                def relu(t, r, n):
                    wait_for(act, m_y, MT * (t - 1))
                    for c in range(FC):
                        act.wait_ge(m_h, FC * t + c + 1)
                        e = 2 * n + r // 2
                        own(act, gate_act)
                        act.activation(h1[r % 2][:, c, :], bank[2 + c % 4][:, 0:CH], ACT.Relu,
                                       bias=b1s[:, bass.ds(e * FC + c, 1)]).then_inc(m_relu, 1)

                slots(act, NI, 4, [(0, relu)])

            @block.vector
            def _(dve):
                dve.wait_ge(s_b, 32)

                def copy_xt(t, r, n):
                    wait_for(dve, m_h, FC * (t - 1))
                    for half in range(2):
                        if half == 0:
                            dve.wait_ge(m_th, t + 1)
                        else:
                            dve.wait_ge(m_t, t + 1)
                        dve.tensor_copy(xT[r % 2][:, :, half * 256:(half + 1) * 256],
                                        bank[half][:, :].rearrange("p (k n) -> p k n", k=KD)).then_inc(m_xt, 1)

                def add_b2(t, r, n):
                    e = 2 * n + r // 2
                    wait_for(dve, s_yo[r % 2], 16 * (2 * n + r // 2))
                    for m in range(MT):
                        dve.wait_ge(m_y, MT * t + m + 1)
                        dve.tensor_tensor(yo[r % 2][:, m, :], bank[6 + m % 2][:, 0:D], b2s[:, bass.ds(e * D, D)],
                                          ALU.add).then_inc(m_yo, 1)

                slots(dve, NI, 4, [(0, copy_xt), (1, add_b2)])

        with ExitStack() as c5:
            def sem5(name):
                return ctx.enter_context(nc.semaphore(name))

            NG = 4
            yg = [G[:, i, 0:D] for i in range(NG)]
            yw = [G[:, i, D:2 * D] for i in range(NG)]
            yc = [G[:, i, 2 * D:3 * D] for i in range(NG)]
            bad = [G[:, i, 3 * D:4 * D].bitcast(I32) for i in range(NG)]
            nan = [G[:, i, 4 * D:5 * D].bitcast(I32) for i in range(NG)]
            res = [G[:, i, 5 * D:6 * D] for i in range(NG)]
            zero = oh[:, 0].rearrange("p a b -> p (a b)")[:, 0:D]
            s_yg = [sem5(f"s_yg{i}") for i in range(NG)]
            s_res = [sem5(f"s_res{i}") for i in range(NG)]
            z_, k_w, k_b, k_n, k_c, k_p, k_q, k_o = (sem5("k_" + n) for n in "z w b n c p q o".split())
            block = c5.enter_context(nc.Block())

            @block.gpsimd
            def _(pool):
                for t in range(NB):
                    i = t % NG
                    if t >= NG:
                        pool.wait_ge(k_w, t - NG + 1)
                    pool.indirect_dma_start(yg[i], None, ybuf, bass.IndirectOffsetOnAxis(gidx[:, t:t + 1], 0)).then_inc(s_yg[i], 16)

            @block.scalar
            def _(act):
                def weigh_y(t, r, n):
                    act.wait_ge(s_yg[r], 16 * (n + 1))
                    wait_for(act, k_o, t - NG + 1)
                    own(act, gate_act)
                    act.activation(yw[r], yg[r], ACT.Copy, scale=rw[:, bass.ds(t, 1)]).then_inc(k_w, 1)

                slots(act, NB, NG, [(0, weigh_y)])

            @block.vector
            def _(dve):
                dve.memset(zero, 0.0).then_inc(z_, 1)
                dve.wait_ge(z_, 1)

                def masks(t, r, n):
                    dve.wait_ge(k_w, t + 1)
                    dve.tensor_scalar(bad[r], yw[r], 0.0, 0.0, ALU.mult, ALU.not_equal).then_inc(k_b, 1)
                    dve.tensor_tensor(nan[r], yw[r], yw[r], ALU.not_equal).then_inc(k_n, 1)
                    dve.tensor_scalar(yc[r], yw[r], 10000.0, -10000.0, ALU.min, ALU.max).then_inc(k_c, 1)

                def replace(t, r, n):
                    dve.wait_ge(k_c, t + 1)
                    dve.wait_ge(k_n, t + 1)
                    dve.wait_ge(k_b, t + 1)
                    own(dve, gate_dve)
                    dve.copy_predicated(yw[r], bad[r], yc[r]).then_inc(k_p, 1)

                def replace_nan(t, r, n):
                    dve.wait_ge(k_p, t + 1)
                    own(dve, gate_dve)
                    dve.copy_predicated(yw[r], nan[r], zero).then_inc(k_q, 1)

                def total(t, r, n):
                    dve.wait_ge(k_q, t + 1)
                    wait_for(dve, s_res[r], 16 * n)
                    dve.tensor_tensor(res[r], yw[r], tile(x_sb, t), ALU.add).then_inc(k_o, 1)

                slots(dve, NB, NG, [(0, masks), (1, replace), (2, replace_nan), (3, total)])

            @block.sync
            def _(sp):
                def store(t, r, n):
                    sp.wait_ge(k_o, t + 1)
                    sp.dma_start(out[bass.ds(t * P, P), :], res[r]).then_inc(s_res[r], 16)

                slots(sp, NB - 1, NG, [(0, store)])
                sp.wait_ge(k_o, NB)
                sp.dma_start(out[(NB - 1) * P:N, :], res[(NB - 1) % NG][0:TAIL, :]).then_inc(s_res[(NB - 1) % NG], 16)
                for i in range(NG):
                    sp.wait_ge(s_res[i], 16 * len(range(i, NB, NG)))


def kernel(**inputs):
    import numpy as np
    import concourse.bacc as bacc
    from concourse.bass_utils import run_bass_kernel_spmd as run

    nc = bacc.Bacc("TRN2", target_bir_lowering=False, num_devices=1)
    src, dst = np.asarray(inputs["src"]), np.asarray(inputs["dst"])
    e = src.shape[0]
    pad = np.full(2 * STEP, PAD_NODE, np.int32)
    d = np.concatenate([np.full(SUB, -1, np.int32), dst, pad, np.full(SUB, PAD_NODE, np.int32)])
    m = e + 2 * STEP
    ed = np.stack([np.concatenate([src, np.zeros(2 * STEP, np.int32)]), d[0:m], d[SUB:SUB + m], d[2 * SUB:2 * SUB + m]], axis=1)
    cols = -(-e // P)
    dstp = np.concatenate([dst, np.full(P * cols - e, PAD_NODE, np.int32)]).reshape(P, cols)
    arrays = {"ed": np.ascontiguousarray(ed), "dstp": np.ascontiguousarray(dstp)}
    for name in ("x", "L0_gnn_W", "L0_gnn_att_src", "L0_gnn_att_dst", "L0_gnn_bias", "L0_gnn_ln_scale", "L0_gnn_ln_bias",
                 "L0_ffn_gate_w", "L0_ffn_gate_b", "L0_ffn_w1", "L0_ffn_b1", "L0_ffn_w2", "L0_ffn_b2"):
        arrays[name] = np.ascontiguousarray(inputs[name])
    b1 = arrays["L0_ffn_b1"]
    arrays["L0_ffn_b1"] = np.ascontiguousarray(b1.reshape(b1.shape[0], -1, P).transpose(2, 0, 1).reshape(P, -1))
    aps = {k: nc.dram_tensor("in_" + k, a.shape, mybir.dt.from_np(a.dtype), kind="ExternalInput").ap() for k, a in arrays.items()}
    o = nc.dram_tensor("out", [arrays["x"].shape[0], arrays["x"].shape[1]], F32, kind="ExternalOutput").ap()
    build(nc, aps["x"], aps["ed"], aps["dstp"], *[aps[k] for k in list(arrays)[3:]], o)
    r = run(nc, [{"in_" + k: a for k, a in arrays.items()}], core_ids=[0])
    return r.results[0]["out"]
```

```python
from contextlib import ExitStack

import concourse.bass as bass
from concourse import mybir

P = 128
F32 = mybir.dt.float32
I32 = mybir.dt.int32
BF16 = mybir.dt.bfloat16
ACT = mybir.ActivationFunctionType
ALU = mybir.AluOpType
AX_X = mybir.AxisListType.X

HEADS, HC = 8, 32
GC = HC + 1
SUB = 4
STEP = SUB * P
UN = 2
NJ = SUB * UN
NA = 6
NQ = 4
PW = NJ // NQ
PH = 4
PAD_NODE = 9999
BIG = 1.0e30
SLOPE = 0.2
EPS = 1e-5
FAR = 1 << 20
FMAX = 3.4028234663852886e38


def wait_for(eng, sem, count):
    if isinstance(count, int) and count <= 0:
        return
    eng.wait_ge(sem, count)


def own(eng, carrier):
    eng.sem_inc(carrier, 1)


def slots(eng, total, period, stages):
    lag_max = max(lag for lag, _ in stages)
    loops = (total - period) // period
    assert lag_max <= period and loops >= 1

    def straight(s):
        for lag, f in stages:
            t = s - lag
            if 0 <= t < total:
                f(t, t % period, t // period)

    for s in range(period):
        straight(s)
    with eng.Fori(1, 1 + loops) as k:
        for r in range(period):
            for lag, f in stages:
                d = r - lag
                f(k * period + d, d % period, k + d // period)
    for s in range(period * (1 + loops), total + lag_max):
        straight(s)


def build(nc, x, ed, dstp, W, att_s, att_d, bias, ln_s, ln_b, gate_w, gate_b, w1, b1, w2, b2, out):
    N, D = x.shape
    E = ed.shape[0] - 2 * STEP
    NB = -(-N // P)
    TAIL = N - (NB - 1) * P
    ROW = HEADS * GC
    NX = gate_w.shape[1]
    F = w1.shape[2]
    CAP = -(-5 * N // (4 * NX))
    SL = -(-CAP // P) * P
    NSTEP = (E + NB * (STEP - 1)) // STEP
    NBATCH = -(-NSTEP // UN)
    TS = 4 * P
    assert NBATCH * UN <= TS and D == HEADS * HC
    EC = dstp.shape[1]
    KD = D // P
    FC = F // P

    table = nc.dram_tensor("table", [NB * P, ROW], F32).ap()
    sched_e = nc.dram_tensor("sched_e", [P, TS // P], I32).ap()
    sched_b = nc.dram_tensor("sched_b", [P, TS // P], I32).ap()
    sched_f = nc.dram_tensor("sched_f", [P, TS // P], F32).ap()
    XR = D + 2
    xbuf = nc.dram_tensor("xbuf", [NX * SL, XR], F32).ap()
    xres = nc.dram_tensor("xres", [NB * P, D], F32).ap()

    with ExitStack() as ctx:
        def sb(name, shape, dt=F32):
            return ctx.enter_context(nc.sbuf_tensor(name, shape, dt))

        def sem(name):
            return ctx.enter_context(nc.semaphore(name))

        bank = [ctx.enter_context(nc.psum_tensor(f"bank{i}", [P, 512], F32)) for i in range(8)]

        x_sb = sb("x_sb", [P, NB, D])
        acc = sb("acc", [P, NB * ROW])
        G = sb("G", [P, PH, NJ * ROW])
        oh = sb("oh", [P, 2, NJ, P])
        ohT = sb("ohT", [P, 2, NJ, P])
        adst = sb("adst", [P, NB * HEADS])
        mv = sb("mv", [P, NB, 2])
        rstd = sb("rstd", [P, NB])
        ident = sb("ident", [P, P])
        iota_n = sb("iota_n", [P, P])
        ones = sb("ones", [P, P])
        is_last_p = sb("is_last_p", [P, 1])
        epst = sb("epst", [P, 1])
        etab = sb("etab", [1, TS], I32)
        btab = sb("btab", [1, TS], I32)
        bbase = sb("bbase", [P, TS])
        s_const = sem("s_const")
        gate, gate_sp, gate_pe, gate_act, gate_dve = (sem(n) for n in ("gate", "gate_sp", "gate_pe", "gate_act", "gate_dve"))

        with ExitStack() as c1:
            def sb1(name, shape, dt=F32):
                return c1.enter_context(nc.sbuf_tensor(name, shape, dt))

            def sem1(name):
                return ctx.enter_context(nc.semaphore(name))

            Ws = oh[:, :, :, :].rearrange("p a b c -> p (a b c)")[:, 0:KD * D].rearrange("p (k d) -> p k d", k=KD)
            Wt = ohT[:, :, :, :].rearrange("p a b c -> p (a b c)")[:, 0:KD * D].rearrange("p (k d) -> p k d", k=KD)
            Wx = sb1("Wx", [P, KD, ROW + HEADS])
            att = sb1("att", [P, 2, D])
            st6 = sb1("st6", [P, NB, 6])
            dif = sb1("dif", [P, NB])
            xn = sb1("xn", [P, 2, D])
            xnT = sb1("xnT", [P, 2, D])
            hrow = sb1("hrow", [P, 4, ROW])
            bounds = sb1("bounds", [P, NB])
            dsts = G[:, 1, 0:EC].bitcast(I32)
            cmp = [G[:, 2 + i, 0:EC] for i in range(2)]
            cnt = sb1("cnt", [P, NB])
            rp = sb1("rp", [P, NB + 1])
            cf = sb1("cf", [P, NB])
            ci = sb1("ci", [P, NB], I32)
            nf = sb1("nf", [P, NB])
            csi = sb1("csi", [P, NB])
            fb = sb1("fb", [P, NB])
            df = sb1("df", [P, NB])
            sid = sb1("sid", [P, 4], I32)
            sidf = sb1("sidf", [P, 4])
            ge = sb1("ge", [P, 4, NB])
            gd = sb1("gd", [P, 4, NB])
            bs = sb1("bs", [P, 4])
            fs = sb1("fs", [P, 4])
            es = sb1("es", [P, 4])
            esi = sb1("esi", [P, 4], I32)
            bsi = sb1("bsi", [P, 4], I32)
            bsf = sb1("bsf", [P, 4])

            XCH = 4
            CT = -(-(NB - 1) // XCH)
            NLP = 28
            s_x = [sem1(f"s_x{i}") for i in range(XCH + 1)]
            s_w = sem1("s_w")
            s_dst = sem1("s_dst")
            s_tail0 = sem1("s_tail0")
            s_zero = sem1("s_zero")
            s_zst = sem1("s_zst")
            dA = sem1("dA")
            dB = sem1("dB")
            s_std = sem1("s_std")
            s_rstd = sem1("s_rstd")
            s_xn = sem1("s_xn")
            s_xt = sem1("s_xt")
            s_xtc = sem1("s_xtc")
            s_h = sem1("s_h")
            s_hr = sem1("s_hr")
            s_tab = [sem1(f"s_tab{i}") for i in range(4)]
            s_cnt = sem1("s_cnt")
            s_cps = sem1("s_cps")
            s_sch = sem1("s_sch")
            s_schd = sem1("s_schd")
            s_schl = sem1("s_schl")
            block = c1.enter_context(nc.Block())

            @block.sync
            def _(sp):
                for i in range(XCH):
                    t0, t1 = i * CT, min((i + 1) * CT, NB - 1)
                    sp.dma_start(x_sb[:, t0:t1, :], x[t0 * P:t1 * P, :].rearrange("(t p) d -> p t d", p=P)).then_inc(s_x[i], 16)
                sp.wait_ge(s_tail0, 1)
                sp.dma_start(x_sb[0:TAIL, NB - 1, :], x[(NB - 1) * P:N, :]).then_inc(s_x[XCH], 16)
                sp.wait_ge(s_zero, 1)
                for c in range(NX):
                    sp.dma_start(xbuf[c * SL:(c + 1) * SL, :].rearrange("(p s) d -> p (s d)", p=P),
                                 G[:, 0, 0:SL // P * XR]).then_inc(s_zst, 16)

                def put_rows(t, r, n):
                    sp.wait_ge(s_hr, t + 1)
                    sp.dma_start(table[bass.ds(t * P, P), :], hrow[:, r, :]).then_inc(s_tab[r], 16)

                slots(sp, NB, 4, [(0, put_rows)])
                sp.wait_ge(s_sch, 1)
                sp.dma_start(sched_e, esi[:, :]).then_inc(s_schd, 16)
                sp.dma_start(sched_b, bsi[:, :]).then_inc(s_schd, 16)
                sp.dma_start(sched_f, bsf[:, :]).then_inc(s_schd, 16)
                sp.wait_ge(s_schd, 48)
                sp.dma_start(etab[:, :], sched_e.rearrange("(a p) q -> a (p q)", a=1)).then_inc(s_schl, 16)
                sp.dma_start(btab[:, :], sched_b.rearrange("(a p) q -> a (p q)", a=1)).then_inc(s_schl, 16)
                sp.dma_start(bbase[:, :], sched_f.rearrange("(a p) q -> a (p q)", a=1).to_broadcast([P, TS])).then_inc(s_schl, 16)
                sp.wait_ge(s_schl, 48)
                for i in range(4):
                    sp.wait_ge(s_tab[i], 16 * len(range(i, NB, 4)))
                sp.wait_ge(s_zst, 16 * NX)

            @block.gpsimd
            def _(pool):
                pool.memset(G[:, 0, :], 0.0).then_inc(s_zero, 1)
                pool.iota(iota_n[:, :], [[1, P]], base=0, channel_multiplier=0,
                          allow_small_or_imprecise_dtypes=True).then_inc(s_const, 1)
                pool.iota(bounds[:, :], [[P, NB]], base=P, channel_multiplier=0,
                          allow_small_or_imprecise_dtypes=True).then_inc(s_const, 1)
                pool.iota(sid[:, :], [[1, 4]], base=0, channel_multiplier=4).then_inc(s_const, 1)
                pool.memset(ident[:, :], 0.0).then_inc(s_const, 1)
                pool.memset(is_last_p[:, :], 0.0).then_inc(s_const, 1)
                pool.wait_ge(s_const, 5)
                pool.affine_select(out=ident[:, :], in_=ident[:, :], compare_op=ALU.not_equal, fill=1.0, base=0,
                                   pattern=[[-1, P]], channel_multiplier=1).then_inc(s_const, 1)
                pool.affine_select(out=is_last_p[:, :], in_=is_last_p[:, :], compare_op=ALU.not_equal, fill=1.0,
                                   base=-(P - 1), pattern=[[0, 1]], channel_multiplier=1).then_inc(s_const, 1)
                pool.memset(acc[:, :], 0.0).then_inc(s_const, 1)

            @block.scalar
            def _(act):
                act.dma_start(dsts, dstp).then_inc(s_dst, 16)
                act.dma_start(Ws, W.rearrange("(k p) d -> p k d", p=P)).then_inc(s_w, 16)
                for i, a in enumerate((att_s, att_d)):
                    act.dma_start(att[:, i, :], a.rearrange("(o h) c -> o (h c)", o=1).to_broadcast([P, D])).then_inc(s_w, 16)
                act.wait_ge(dA, 4)
                act.activation(rstd[:, :], mv[:, :, 1], ACT.Sqrt, bias=epst[:, :]).then_inc(s_std, 1)

                def copy_xt(t, r, n):
                    act.wait_ge(s_xt, t + 1)
                    wait_for(act, s_h, t - 1)
                    act.copy(xnT[:, r % 2, :], bank[r % 2][:, 0:D]).then_inc(s_xtc, 1)

                def copy_h(t, r, n):
                    act.wait_ge(s_h, t + 1)
                    wait_for(act, s_tab[r], 16 * n)
                    act.copy(hrow[:, r, :], bank[2 + r % 2][:, 0:ROW])
                    act.copy(adst[:, bass.ds(t * HEADS, HEADS)], bank[2 + r % 2][:, ROW:ROW + HEADS]).then_inc(s_hr, 1)

                slots(act, NB, 4, [(0, copy_xt), (1, copy_h)])

            @block.tensor
            def _(pe):
                pe.wait_ge(s_const, 8)

                def turn(t, r, n):
                    pe.wait_ge(s_xn, t + 1)
                    wait_for(pe, s_xtc, t - 1)
                    for k in range(KD):
                        mm = pe.transpose(bank[r][:, k * P:(k + 1) * P], xn[:, r, k * P:(k + 1) * P], ident[:, :])
                    mm.then_inc(s_xt, 1)

                def project(t, r, n):
                    pe.wait_ge(s_xtc, t + 1)
                    wait_for(pe, s_hr, t - 1)
                    for k in range(KD):
                        mm = pe.matmul(bank[2 + r][:, 0:ROW + HEADS], xnT[:, r, k * P:(k + 1) * P], Wx[:, k, :],
                                       start=(k == 0), stop=(k == KD - 1))
                    mm.then_inc(s_h, 1)

                slots(pe, NB, 2, [(0, turn), (1, project)])
                pe.wait_ge(s_cnt, NB)
                pe.matmul(bank[4][:, 0:NB], ones[:, :], cnt[:, :], start=True, stop=True).then_inc(s_cps, 1)

            @block.vector
            def _(dve):
                dve.memset(x_sb[:, NB - 1, :], 0.0).then_inc(s_tail0, 1)
                dve.memset(epst[:, :], EPS).then_inc(dA, 1)
                dve.memset(ones[:, :], 1.0).then_inc(dA, 1)

                dve.wait_ge(s_dst, 16)
                dve.wait_ge(s_const, 8)

                def count(off):
                    def f(t, r, n):
                        b = t + off
                        wait_for(dve, s_cnt, b - 1)
                        dve.tensor_scalar(cmp[r % 2], dsts, bounds[:, bass.ds(b, 1)], 0.0, ALU.is_lt, ALU.add,
                                          accum_out=cnt[:, bass.ds(b, 1)]).then_inc(s_cnt, 1)
                    return f

                slots(dve, NB - NLP, 2, [(0, count(0))])

                def stats(t0):
                    def f(t, r, n):
                        dve.bn_stats(st6[:, bass.ds(t + t0, 1), :].rearrange("p a s -> p (a s)"),
                                     x_sb[:, bass.ds(t + t0, 1), :].rearrange("p a s -> p (a s)"))
                    return f

                for i in range(XCH):
                    dve.wait_ge(s_x[i], 16)
                    slots(dve, min(CT, NB - 1 - i * CT), 4, [(0, stats(i * CT))])
                dve.wait_ge(s_x[XCH], 16)
                dve.bn_stats(st6[:, NB - 1, :], x_sb[:, NB - 1, :]).then_inc(dA, 1)
                dve.wait_ge(dA, 3)

                dve.tensor_tensor(mv[:, :, 0], st6[:, :, 1], st6[:, :, 4], ALU.add).then_inc(dB, 1)
                dve.tensor_tensor(mv[:, :, 1], st6[:, :, 2], st6[:, :, 5], ALU.add).then_inc(dB, 1)
                dve.tensor_tensor(dif[:, :], st6[:, :, 1], st6[:, :, 4], ALU.subtract).then_inc(dB, 1)
                dve.wait_ge(dB, 3)
                dve.scalar_tensor_tensor(dif[:, :], dif[:, :], 0.25, dif[:, :], ALU.mult, ALU.mult).then_inc(dB, 1)
                dve.tensor_scalar(mv[:, :, 0], mv[:, :, 0], 0.5, None, ALU.mult).then_inc(dB, 1)
                dve.wait_ge(dB, 5)
                dve.scalar_tensor_tensor(mv[:, :, 1], mv[:, :, 1], 1.0 / D, dif[:, :], ALU.mult, ALU.add).then_inc(dA, 1)
                dve.wait_ge(s_w, 48)
                for k in range(KD):
                    last = dve.tensor_copy(Wx[:, k, 0:ROW].rearrange("p (h g) -> p h g", g=GC)[:, :, 0:HC],
                                           Ws[:, k, :].rearrange("p (h c) -> p h c", c=HC))
                for i in range(2):
                    for k in range(KD):
                        dve.tensor_tensor(Wt[:, k, :], Ws[:, k, :], att[:, i, :], ALU.mult).then_inc(dA, 1)
                    dve.wait_ge(dA, 4 + 4 * i + 2)
                    for k in range(KD):
                        dst = (Wx[:, k, 0:ROW].rearrange("p (h g) -> p h g", g=GC)[:, :, HC] if i == 0
                               else Wx[:, k, ROW:ROW + HEADS])
                        dve.tensor_reduce(dst, Wt[:, k, :].rearrange("p (h c) -> p h c", c=HC), AX_X, ALU.add).then_inc(dA, 1)
                    dve.wait_ge(dA, 4 + 4 * i + 4)
                dve.wait_ge(s_std, 1)
                dve.reciprocal(rstd[:, :], rstd[:, :]).then_inc(s_rstd, 1)
                dve.wait_ge(s_rstd, 1)

                def normalise(t0):
                    def f(t, r, n):
                        wait_for(dve, s_xt, t + t0 - 1)
                        dve.tensor_scalar(xn[:, r, :], x_sb[:, bass.ds(t + t0, 1), :].rearrange("p a s -> p (a s)"),
                                          mv[:, bass.ds(t + t0, 1), 0], rstd[:, bass.ds(t + t0, 1)],
                                          ALU.subtract, ALU.mult).then_inc(s_xn, 1)
                    return f

                assert NLP % 2 == 0
                slots(dve, NLP, 2, [(0, normalise(0)), (0, count(NB - NLP))])
                slots(dve, NB - NLP, 2, [(0, normalise(NLP))])
                dve.wait_ge(s_cps, 1)
                link = sem1("link")
                dve.memset(rp[:, 0:1], 0.0).then_inc(link, 1)
                dve.tensor_copy(rp[:, 1:NB + 1], bank[4][:, 0:NB]).then_inc(link, 1)
                dve.wait_ge(link, 2)
                dve.tensor_tensor(cf[:, :], rp[:, 1:NB + 1], rp[:, 0:NB], ALU.subtract).then_inc(link, 1)
                dve.wait_ge(link, 3)
                dve.tensor_scalar(ci[:, :], cf[:, :], float(STEP - 1), None, ALU.add).then_inc(link, 1)
                dve.wait_ge(link, 4)
                dve.tensor_scalar(ci[:, :], ci[:, :], STEP.bit_length() - 1, None, ALU.logical_shift_right).then_inc(link, 1)
                dve.wait_ge(link, 5)
                dve.tensor_copy(nf[:, :], ci[:, :]).then_inc(link, 1)
                dve.wait_ge(link, 6)
                dve.tensor_tensor_scan(csi[:, :], ones[:, 0:NB], nf[:, :], 0.0, ALU.mult, ALU.add).then_inc(link, 1)
                dve.wait_ge(link, 7)
                dve.tensor_tensor(fb[:, :], csi[:, :], nf[:, :], ALU.subtract).then_inc(link, 1)
                dve.wait_ge(link, 8)
                dve.scalar_tensor_tensor(fb[:, :], fb[:, :], -float(STEP), rp[:, 0:NB], ALU.mult, ALU.add).then_inc(link, 1)
                dve.memset(df[:, NB - 1:NB], 0.0).then_inc(link, 1)
                dve.tensor_copy(sidf[:, :], sid[:, :]).then_inc(link, 1)
                dve.wait_ge(link, 11)
                dve.tensor_tensor(df[:, 0:NB - 1], fb[:, 1:NB], fb[:, 0:NB - 1], ALU.subtract).then_inc(link, 1)
                for q in range(4):
                    dve.tensor_scalar(ge[:, q, :], csi[:, :], sidf[:, q:q + 1], None, ALU.is_le).then_inc(link, 1)
                dve.wait_ge(link, 16)
                dve.tensor_reduce(bs[:, :], ge[:, :, :], AX_X, ALU.add).then_inc(link, 1)
                dve.tensor_tensor(gd[:, :, :], ge[:, :, :], df[:, :].unsqueeze(1).to_broadcast([P, 4, NB]),
                                  ALU.mult).then_inc(link, 1)
                dve.wait_ge(link, 18)
                dve.tensor_reduce(fs[:, :], gd[:, :, :], AX_X, ALU.add).then_inc(link, 1)
                dve.tensor_scalar(bsf[:, :], bs[:, :], float(NB - 1), None, ALU.min).then_inc(link, 1)
                dve.wait_ge(link, 20)
                dve.scalar_tensor_tensor(es[:, :], sidf[:, :], float(STEP), fs[:, :], ALU.mult, ALU.add).then_inc(link, 1)
                dve.tensor_copy(bsi[:, :], bsf[:, :]).then_inc(link, 1)
                dve.wait_ge(link, 22)
                dve.tensor_scalar(esi[:, :], es[:, :], float(E), None, ALU.min).then_inc(link, 1)
                dve.tensor_scalar(bsf[:, :], bsf[:, :], float(P), None, ALU.mult).then_inc(link, 1)
                dve.wait_ge(link, 24)
                dve.engine_nop().then_inc(s_sch, 1)

        with ExitStack() as c2:
            def sb2(name, shape, dt=F32):
                return c2.enter_context(nc.sbuf_tensor(name, shape, dt))

            def sem2(name):
                return ctx.enter_context(nc.semaphore(name))

            ohTb, ohb = (ohT[:, i].rearrange("p j e -> p (j e)").bitcast(BF16).rearrange("p (r j e) -> p r j e", r=2, j=NJ)
                         for i in range(2))
            H1 = UN + 1
            ei = sb2("ei", [P, PH, NJ, 4], I32)
            nl = sb2("nl", [P, NJ, 2])
            drel = sb2("drel", [P, 2, NJ])
            dist = sb2("dist", [P, NA, P])
            mk = sb2("mk", [P, 2, NJ * HEADS])
            scm = sb2("scm", [P, PH, NJ * HEADS])
            mT = sb2("mT", [NJ * HEADS, P])
            fm = sb2("fm", [NJ * HEADS, P])
            lm = sb2("lm", [P, NJ, HEADS])
            lmr = sb2("lmr", [P, NJ, HEADS])
            lmb = sb2("lmb", [P, 3, NJ, HEADS + 1], BF16)
            identb = sb2("identb", [P, P], BF16)
            adr = sb2("adr", [P, NB * HEADS])
            adb = sb2("adb", [P, 3, NB * HEADS], BF16)
            t8 = sb2("t8", [P, NJ])
            cand = sb2("cand", [P, NJ, HEADS])
            cm = sb2("cm", [P, UN, HEADS])
            zb = sb2("zb", [P, UN, HEADS])
            zc = sb2("zc", [P, HEADS, H1])
            blk = sb2("blk", [P, TS])
            mk5 = sb2("mk5", [P, HEADS, H1])
            adu = sb2("adu", [P, 2, UN, HEADS])
            mx = sb2("mx", [P, 2, HEADS, H1])
            mxr = sb2("mxr", [P, UN, HEADS])
            dmb = sb2("dmb", [P, 2, 3, UN, 2 * HEADS], BF16)
            mold = sb2("mold", [P, HEADS, UN])
            dfm = sb2("dfm", [P, 2, HEADS, UN])
            so = sb2("so", [P, 2, HEADS, UN])
            a1 = sb2("a1", [P, NJ, HEADS])
            a2 = sb2("a2", [P, NJ, HEADS])
            a3 = sb2("a3", [P, NJ, HEADS])
            a4 = sb2("a4", [P, NJ, HEADS])
            cur = sb2("cur", [P, 2, ROW])
            scaled = sb2("scaled", [P, ROW])

            s_ei = [sem2(f"s_ei{r}") for r in range(PH)]
            s_g = [sem2(f"s_g{r}") for r in range(PH)]
            a_sc, a_mk, a_oh, a_so, a_ex, a_d, a_dist, a_one, a_f32, a_acc = (
                sem2("a_" + n) for n in "sc mk oh so ex d dist one f32 acc".split())
            p_tr, p_oh, p_fm, p_nm, p_de, p_agg = (sem2("p_" + n) for n in "tr oh fm nm de agg".split())
            d_tab, d_pre, d_drel, d_mk, d_oh, d_scan, d_lm, d_mk5, d_c, d_mp, d_al, d_msg, d_sc, d_acc = (
                sem2("d_" + n) for n in "tab pre drel mk oh scan lm mk5 c mp al msg sc acc".split())
            N_C, N_AL, N_LM, N_MP = 9, 4, 5, 4

            bTR, bOH, bNM, bDE, bAG = bank[0], bank[1:3], bank[3], bank[4], bank[5:7]

            bOHb = [bOH[i][:, 0:NJ // 2 * P // 2].bitcast(BF16) for i in range(2)]

            def G4(r):
                return G[:, r, :].rearrange("p (j h g) -> p j h g", j=NJ, g=GC)

            block = c2.enter_context(nc.Block())

            def schedule_regs(eng, tab, regs, t, top):
                eng.load(regs, tab[0:1, bass.ds(t * UN, UN)])
                return [eng.snap(q, min_val=0, max_val=top) for q in regs]

            @block.sync
            def _(sp):
                regs = [sp.alloc_register(f"sp_e{u}") for u in range(UN)]

                def load_edges(t, r, n):
                    e0 = schedule_regs(sp, etab, regs, t, E)
                    wait_for(sp, s_g[r], 16 * NJ * n)
                    own(sp, gate_sp)
                    wait_for(sp, d_drel, t - PH + 1)
                    own(sp, gate_sp)
                    for u in range(UN):
                        sp.dma_start(ei[:, r, u * SUB:(u + 1) * SUB, :].rearrange("p s c -> p (s c)"),
                                     ed[bass.ds(e0[u], STEP), :].rearrange("(p s) c -> p (s c)", s=SUB)).then_inc(s_ei[r], 16)

                slots(sp, NBATCH, PH, [(0, load_edges)])

            @block.gpsimd
            def _(pool):
                def gather(t, r, n):
                    pool.wait_ge(s_ei[r], 16 * UN * (n + 1))
                    own(pool, gate)
                    for j in range(NJ):
                        if j % PW == 0 and not (isinstance(t, int) and t < PH):
                            pool.wait_ge(p_agg, NQ * (t - PH) + j // PW + 1)
                            own(pool, gate)
                        pool.indirect_dma_start(G[:, r, j * ROW:(j + 1) * ROW], None, table,
                                                bass.IndirectOffsetOnAxis(ei[:, r, j, 0:1], 0)).then_inc(s_g[r], 16)

                slots(pool, NBATCH, PH, [(0, gather)])

            @block.scalar
            def _(act):
                regs_d = [act.alloc_register(f"act_d{u}") for u in range(UN)]
                regs_a = [act.alloc_register(f"act_a{u}") for u in range(UN)]

                def scale_old(t, r, n):
                    act.wait_ge(d_c, N_C * (t + 1))
                    wait_for(act, d_sc, UN * (t - 1))
                    act.activation(so[:, r % 2], dfm[:, r % 2], ACT.Exp).then_inc(a_so, 1)

                def take_asrc(t, r, n):
                    act.wait_ge(s_g[r], 16 * NJ * (n + 1))
                    wait_for(act, d_al, N_AL * (t - PH + 1))
                    act.copy(scm[:, r].rearrange("p (j h) -> p j h", h=HEADS), G4(r)[:, :, :, HC]).then_inc(a_sc, 1)

                def exps(t, r, n):
                    act.wait_ge(d_al, N_AL * (t + 1))
                    act.activation(G4(r)[:, :, :, HC], a4[:, :, :], ACT.Exp).then_inc(a_ex, 1)

                def copy_mask(t, r, n):
                    act.wait_ge(p_tr, t + 1)
                    wait_for(act, d_scan, t)
                    act.copy(mT[:, :], bTR[0:NJ * HEADS, P:2 * P]).then_inc(a_mk, 1)

                def copy_oht(half):
                    def f(t, r, n):
                        act.wait_ge(p_oh, 2 * t + half + 1)
                        if half == 0:
                            wait_for(act, p_de, t - 1)
                        act.copy(ohTb[:, r % 2, half * 4:half * 4 + 4, :].rearrange("p j e -> p (j e)"),
                                 bOHb[half]).then_inc(a_oh, 1)
                    return f

                def take_adst(t, r, n):
                    b = schedule_regs(act, btab, regs_d, t, NB - 1)
                    wait_for(act, p_de, t - 1)
                    for u in range(UN):
                        act.copy(adu[:, r % 2, u, :], adst[:, bass.ds(b[u] * HEADS, HEADS)])
                        o = act.copy(dmb[:, r % 2, :, u, 0:HEADS], adb[:, :, bass.ds(b[u] * HEADS, HEADS)])
                    o.then_inc(a_d, 1)

                def one_hots(t, r, n):
                    act.wait_ge(d_drel, t + 1)
                    wait_for(act, a_one, t)
                    for i in range(NA):
                        o = act.activation(dist[:, i, :], iota_n[:, :], ACT.Abs, scale=-1.0,
                                           bias=drel[:, r % 2, NJ - NA + i:NJ - NA + i + 1])
                    o.then_inc(a_dist, 1)

                def one_hots_out(t, r, n):
                    act.wait_ge(a_dist, t + 1)
                    wait_for(act, p_nm, t - 1)
                    wait_for(act, a_f32, t - 1)
                    act.activation(ohb[:, r % 2, NJ - NA:NJ, :], dist[:, :, :], ACT.Relu, scale=-1.0, bias=1.0).then_inc(a_one, 1)

                def one_hots_f32(t, r, n):
                    act.wait_ge(d_oh, t + 1)
                    act.wait_ge(a_one, t + 1)
                    wait_for(act, p_agg, NQ * (t - 1))
                    act.copy(oh[:, r % 2], ohb[:, r % 2]).then_inc(a_f32, 1)

                def keep(us):
                    def f(t, r, n):
                        b = schedule_regs(act, btab, regs_a, t, NB - 1)
                        for u in us:
                            act.wait_ge(d_acc, UN * t + u + 1)
                            wait_for(act, a_acc, UN * t + u)
                            own(act, gate_act)
                            act.copy(acc[:, bass.ds(b[u] * ROW, ROW)], cur[:, u % 2, :]).then_inc(a_acc, 1)
                    return f

                act.wait_ge(d_tab, 12)
                slots(act, NBATCH, PH, [
                    (2, scale_old), (0, take_asrc), (2, exps), (0, copy_mask), (0, one_hots), (0, one_hots_out),
                    (1, one_hots_f32), (3, keep([1])), (0, copy_oht(0)), (0, copy_oht(1)), (0, take_adst), (2, keep([0]))])

            @block.tensor
            def _(pe):
                pe.wait_ge(d_tab, 12)

                def spread(t, r, n):
                    pe.wait_ge(a_oh, 2 * t + 2)
                    pe.wait_ge(d_mp, N_MP * (t + 1))
                    pe.wait_ge(a_d, t + 1)
                    wait_for(pe, d_al, N_AL * t)
                    for j in range(NJ):
                        for i in range(3):
                            mm = pe.matmul(bDE[:, j * 16:j * 16 + 16], ohTb[:, r % 2, j, :], dmb[:, r % 2, i, j // SUB, :],
                                           start=(i == 0), stop=(i == 2))
                    mm.then_inc(p_de, 1)

                def turn(t, r, n):
                    wait_for(pe, d_lm, N_LM * (t - 1) + 1)
                    pe.wait_ge(a_sc, t + 1)
                    pe.wait_ge(d_mk, t + 1)
                    own(pe, gate_pe)
                    pe.transpose(bTR[0:NJ * HEADS, 0:P], scm[:, r], ident[:, :])
                    pe.transpose(bTR[0:NJ * HEADS, P:2 * P], mk[:, r % 2], ident[:, :]).then_inc(p_tr, 1)

                def turn_oh(half):
                    def f(t, r, n):
                        if half == 0:
                            pe.wait_ge(d_oh, t + 1)
                        if half == 1 or NA > 4:
                            pe.wait_ge(a_one, t + 1)
                        wait_for(pe, a_oh, 2 * (t - 1) + half + 1)
                        for j in range(4):
                            mm = pe.transpose(bOHb[half][:, j * P:(j + 1) * P], ohb[:, r % 2, half * 4 + j, :], identb[:, :])
                        mm.then_inc(p_oh, 1)
                    return f

                def turn_max(t, r, n):
                    pe.wait_ge(d_scan, t + 1)
                    own(pe, gate_pe)
                    pe.transpose(bTR[:, 2 * P:2 * P + NJ * HEADS], fm[:, :], ident[0:NJ * HEADS, 0:NJ * HEADS]).then_inc(p_fm, 1)

                def node_max(t, r, n):
                    pe.wait_ge(d_lm, N_LM * (t + 1))
                    pe.wait_ge(d_oh, t + 1)
                    pe.wait_ge(a_one, t + 1)
                    wait_for(pe, d_c, N_C * t)
                    for j in range(NJ):
                        for i in range(3):
                            mm = pe.matmul(bNM[:, j * 9:j * 9 + 9], ohb[:, r % 2, j, :], lmb[:, i, j, :], start=(i == 0), stop=(i == 2))
                    mm.then_inc(p_nm, 1)

                def total(q):
                    u, s0 = q * PW // SUB, q * PW % SUB

                    def f(t, r, n):
                        if q == 0:
                            pe.wait_ge(a_f32, t + 1)
                        pe.wait_ge(d_msg, NQ * t + q + 1)
                        if s0 == 0:
                            wait_for(pe, d_acc, UN * t + u - 1)
                        for s in range(s0, s0 + PW):
                            j = u * SUB + s
                            mm = pe.matmul(bAG[u % 2][:, 0:ROW], oh[:, r % 2, j, :], G[:, r, j * ROW:(j + 1) * ROW],
                                           start=(s == 0), stop=(s == SUB - 1))
                        mm.then_inc(p_agg, 1)
                    return f

                slots(pe, NBATCH, PH, [
                    (0, turn), (1, node_max), (2, total(0)), (0, turn_max), (2, total(1)), (0, turn_oh(0)), (0, turn_oh(1)), (1, spread),
                    (2, total(2)), (2, total(3))])

            @block.vector
            def _(dve):
                dve.memset(cur[:, :, :], 0.0).then_inc(d_tab, 1)
                dve.memset(mx[:, 1, :, :], -BIG).then_inc(d_tab, 1)
                dve.memset(mk5[:, :, 0], -BIG).then_inc(d_tab, 1)
                dve.memset(blk[:, 0:1], 1.0).then_inc(d_tab, 1)
                dve.memset(lmb[:, :, :, :], 0.0).then_inc(d_tab, 1)
                dve.tensor_copy(identb[:, :], ident[:, :]).then_inc(d_tab, 1)
                dve.tensor_copy(adb[:, 0, :], adst[:, :]).then_inc(d_tab, 1)
                dve.tensor_tensor(blk[:, 1:TS], bbase[:, 1:TS], bbase[:, 0:TS - 1], ALU.not_equal).then_inc(d_tab, 1)
                dve.wait_ge(d_tab, 8)
                dve.tensor_scalar(blk[:, :], blk[:, :], -BIG, None, ALU.mult).then_inc(d_tab, 1)
                dve.tensor_tensor(adr[:, :], adst[:, :], adb[:, 0, :], ALU.subtract).then_inc(d_tab, 1)
                dve.wait_ge(d_tab, 10)
                dve.tensor_copy(adb[:, 1, :], adr[:, :]).then_inc(d_tab, 1)
                dve.wait_ge(d_tab, 11)
                dve.tensor_tensor(adb[:, 2, :], adr[:, :], adb[:, 1, :], ALU.subtract).then_inc(d_tab, 1)
                dve.wait_ge(d_tab, 12)

                def edge_marks(t, r, n):
                    e = ei[:, r]
                    dve.wait_ge(s_ei[r], 16 * UN * (n + 1))
                    dve.tensor_tensor(nl[:, :, :], e[:, :, 2].unsqueeze(2).to_broadcast([P, NJ, 2]), e[:, :, 1:4:2],
                                      ALU.not_equal).then_inc(d_pre, 1)
                    wait_for(dve, a_dist, t - 1)
                    dve.tensor_tensor(drel[:, r % 2, :].rearrange("p (u s) -> p u s", s=SUB),
                                      e[:, :, 2].rearrange("p (u s) -> p u s", s=SUB),
                                      bbase[:, bass.ds(t * UN, UN)].unsqueeze(2).to_broadcast([P, UN, SUB]),
                                      ALU.subtract).then_inc(d_drel, 1)

                def scan_marks(t, r, n):
                    wait_for(dve, p_tr, t - 1)
                    dve.wait_ge(d_pre, 2 * t + 1)
                    dve.tensor_scalar(mk[:, r % 2].rearrange("p (j h) -> p j h", h=HEADS),
                                      nl[:, :, 0].unsqueeze(2).to_broadcast([P, NJ, HEADS]), -BIG, None, ALU.mult).then_inc(d_mk, 1)

                def last_marks(t, r, n):
                    wait_for(dve, p_nm, t)
                    dve.tensor_scalar(lmb[:, 0, :, HEADS], nl[:, :, 1], is_last_p[:, 0:1], None, ALU.max).then_inc(d_pre, 1)

                def one_hot(j):
                    def f(t, r, n):
                        if j == 0:
                            dve.wait_ge(d_drel, t + 1)
                            wait_for(dve, p_nm, t - 1)
                            wait_for(dve, a_f32, t - 1)
                        o = dve.tensor_scalar(ohb[:, r % 2, j, :], iota_n[:, :], drel[:, r % 2, j:j + 1], None, ALU.is_equal)
                        if j == NJ - NA - 1:
                            o.then_inc(d_oh, 1)
                    return f

                de = bDE[:, 0:NJ * 16].rearrange("p (j c) -> p j c", c=16)

                def with_dst(t, r, n):
                    dve.wait_ge(p_de, t + 1)
                    dve.tensor_tensor(a1[:, :, :], scm[:, r].rearrange("p (j h) -> p j h", h=HEADS),
                                      de[:, :, 0:HEADS], ALU.add).then_inc(d_al, 1)

                def alpha(t, r, n):
                    dve.wait_ge(d_al, N_AL * t + 1)
                    dve.scalar_tensor_tensor(a2[:, :, :], a1[:, :, :], SLOPE, a1[:, :, :], ALU.mult, ALU.max).then_inc(d_al, 1)

                def less_max(t, r, n):
                    dve.wait_ge(d_al, N_AL * t + 2)
                    dve.tensor_tensor(a3[:, :, :], a2[:, :, :], de[:, :, HEADS:16], ALU.subtract).then_inc(d_al, 1)

                def bounded(t, r, n):
                    dve.wait_ge(d_al, N_AL * t + 3)
                    wait_for(dve, a_ex, t)
                    dve.tensor_scalar(a4[:, :, :], a3[:, :, :], 0.0, None, ALU.min).then_inc(d_al, 1)

                def scan(t, r, n):
                    dve.wait_ge(a_mk, t + 1)
                    wait_for(dve, p_fm, t)
                    dve.tensor_tensor_scan(fm[:, :], mT[:, :], bTR[0:NJ * HEADS, 0:P], -BIG, ALU.add, ALU.max).then_inc(d_scan, 1)

                def last_max(t, r, n):
                    dve.wait_ge(p_fm, t + 1)
                    dve.wait_ge(d_pre, 2 * (t + 1))
                    dve.tensor_tensor(lm[:, :, :],
                                      bTR[:, 2 * P:2 * P + NJ * HEADS].rearrange("p (j h) -> p j h", h=HEADS),
                                      lmb[:, 0, :, HEADS].unsqueeze(2).to_broadcast([P, NJ, HEADS]), ALU.mult).then_inc(d_lm, 1)

                def last_max_part(i):
                    def f(t, r, n):
                        dve.wait_ge(d_lm, N_LM * t + 1 + i)
                        if i == 0:
                            o = dve.tensor_copy(lmb[:, 0, :, 0:HEADS], lm[:, :, :])
                        elif i == 1:
                            o = dve.tensor_tensor(lmr[:, :, :], lm[:, :, :], lmb[:, 0, :, 0:HEADS], ALU.subtract)
                        elif i == 2:
                            o = dve.tensor_copy(lmb[:, 1, :, 0:HEADS], lmr[:, :, :])
                        else:
                            o = dve.tensor_tensor(lmb[:, 2, :, 0:HEADS], lmr[:, :, :], lmb[:, 1, :, 0:HEADS], ALU.subtract)
                        o.then_inc(d_lm, 1)
                    return f

                def node_max_part(i):
                    def f(t, r, n):
                        m = mx[:, r % 2, :, 1:H1].rearrange("p h u -> p u h")
                        hi, mid, lo = (dmb[:, r % 2, k, :, HEADS:2 * HEADS] for k in range(3))
                        if i == 0:
                            dve.wait_ge(d_c, N_C * t + 7)
                            wait_for(dve, p_de, t - 1)
                            o = dve.tensor_copy(hi, m)
                        else:
                            dve.wait_ge(d_mp, N_MP * t + i)
                        if i == 1:
                            o = dve.tensor_tensor(mxr[:, :, :], m, hi, ALU.subtract)
                        elif i == 2:
                            o = dve.tensor_copy(mid, mxr[:, :, :])
                        elif i == 3:
                            o = dve.tensor_tensor(lo, mxr[:, :, :], mid, ALU.subtract)
                        o.then_inc(d_mp, 1)
                    return f

                nm = bNM[:, 0:NJ * 9].rearrange("p (j c) -> p j c", c=9)

                def presence(t, r, n):
                    dve.wait_ge(p_nm, t + 1)
                    dve.tensor_scalar(t8[:, :], nm[:, :, HEADS], BIG, -BIG, ALU.mult, ALU.add).then_inc(d_c, 1)
                    wait_for(dve, d_c, N_C * t)
                    dve.tensor_copy(zc[:, :, 0], mx[:, (r + 1) % 2, :, UN]).then_inc(d_c, 1)
                    wait_for(dve, d_c, N_C * t)
                    dve.tensor_copy(mk5[:, :, 1:H1], blk[:, bass.ds(t * UN, UN)].unsqueeze(1).to_broadcast([P, HEADS, UN])).then_inc(d_mk5, 1)

                def candidates(t, r, n):
                    dve.wait_ge(d_c, N_C * t + 2)
                    dve.tensor_tensor(cand[:, :, :], nm[:, :, 0:HEADS], t8[:, :].unsqueeze(2).to_broadcast([P, NJ, HEADS]),
                                      ALU.add).then_inc(d_c, 1)

                def of_superstep(t, r, n):
                    dve.wait_ge(d_c, N_C * t + 3)
                    dve.tensor_reduce(cm[:, :, :], cand[:, :, :].rearrange("p (u s) h -> p u h s", s=SUB), AX_X, ALU.max).then_inc(d_c, 1)

                def with_adst(t, r, n):
                    dve.wait_ge(d_c, N_C * t + 4)
                    dve.wait_ge(a_d, t + 1)
                    dve.tensor_tensor(zb[:, :, :], cm[:, :, :], adu[:, r % 2],
                                      ALU.add).then_inc(d_c, 1)

                def leaky(t, r, n):
                    dve.wait_ge(d_c, N_C * t + 5)
                    dve.scalar_tensor_tensor(zc[:, :, 1:H1].rearrange("p h u -> p u h"), zb[:, :, :], SLOPE, zb[:, :, :],
                                             ALU.mult, ALU.max).then_inc(d_c, 1)

                def running(t, r, n):
                    dve.wait_ge(d_c, N_C * t + 6)
                    dve.wait_ge(d_mk5, t + 1)
                    dve.tensor_tensor_scan(mx[:, r % 2, :, :].rearrange("p h u -> p (h u)"),
                                           mk5[:, :, :].rearrange("p h u -> p (h u)"),
                                           zc[:, :, :].rearrange("p h u -> p (h u)"), -BIG, ALU.add, ALU.max).then_inc(d_c, 1)

                def before(t, r, n):
                    dve.wait_ge(d_c, N_C * t + 7)
                    dve.tensor_tensor(mold[:, :, :], mx[:, r % 2, :, 0:UN], mk5[:, :, 1:H1], ALU.add).then_inc(d_c, 1)

                def change(t, r, n):
                    dve.wait_ge(d_c, N_C * t + 8)
                    wait_for(dve, a_so, t - 1)
                    dve.tensor_tensor(dfm[:, r % 2], mold[:, :, :], mx[:, r % 2, :, 1:H1], ALU.subtract).then_inc(d_c, 1)

                def weigh(q):
                    def f(t, r, n):
                        if q == 0:
                            dve.wait_ge(a_ex, t + 1)
                        g = G4(r)[:, q * PW:(q + 1) * PW].rearrange("p s h g -> p (s h) g")
                        dve.tensor_tensor(g[:, :, 0:HC], g[:, :, 0:HC], g[:, :, HC:GC].to_broadcast([P, PW * HEADS, HC]),
                                          ALU.mult).then_inc(d_msg, 1)
                    return f

                def rescale(u):
                    def f(t, r, n):
                        if u == 0:
                            dve.wait_ge(a_so, t + 1)
                        wait_for(dve, d_acc, UN * t + u)
                        dve.tensor_tensor(scaled[:, :].rearrange("p (h g) -> p h g", g=GC),
                                          cur[:, (u + 1) % 2, :].rearrange("p (h g) -> p h g", g=GC),
                                          so[:, r % 2, :, u:u + 1].to_broadcast([P, HEADS, GC]), ALU.mult).then_inc(d_sc, 1)
                    return f

                def add_new(u):
                    def f(t, r, n):
                        dve.wait_ge(d_sc, UN * t + u + 1)
                        dve.wait_ge(p_agg, NQ * t + (u + 1) * NQ // UN)
                        wait_for(dve, a_acc, UN * t + u - 1)
                        dve.tensor_tensor(cur[:, u % 2, :], scaled[:, :], bAG[u % 2][:, 0:ROW], ALU.add).then_inc(d_acc, 1)
                    return f

                slots(dve, NBATCH, PH, [
                    (0, edge_marks), (3, rescale(1)), (0, scan_marks), (2, with_dst), (0, one_hot(0)), (2, alpha), (0, one_hot(1)),
                    (2, less_max), (2, bounded), (3, add_new(1)), 
                    (2, weigh(0)), (1, presence), (0, scan), (1, candidates), (2, weigh(1)), (1, of_superstep), (0, last_marks),
                    (1, with_adst), (0, last_max), (1, leaky), (0, last_max_part(0)),
                    (1, running), (2, weigh(2)), (1, before), (1, node_max_part(0)), (0, last_max_part(1)),
                    (1, change), (1, node_max_part(1)), (0, last_max_part(2)),
                    (1, node_max_part(2)), (2, rescale(0)), (0, last_max_part(3)), (1, node_max_part(3)),
                    (2, weigh(3)), (2, add_new(0))])

        w1f = sb("w1f", [P, KD, F])
        w2f = sb("w2f", [P, FC, D])
        s_wt = [sem("s_wt0"), sem("s_wt1")]

        with ExitStack() as c3:
            def sb3(name, shape, dt=F32):
                return c3.enter_context(nc.sbuf_tensor(name, shape, dt))

            def sem3(name):
                return ctx.enter_context(nc.semaphore(name))

            biasT = sb3("biasT", [P, 3, D])
            gw = sb3("gw", [P, KD, NX])
            gb = sb3("gb", [P, NX])
            nmr = sb3("nmr", [P, NB])
            rden = sb3("rden", [P, NB, HEADS])
            st = sb3("st", [P, NB, 6])
            mean = sb3("mean", [P, NB])
            var = sb3("var", [P, NB])
            dif = sb3("dif3", [P, NB])
            rs = sb3("rs", [P, NB])
            xr, xb, o1, o2 = (G[:, i, 0:4 * D].rearrange("p (r d) -> p r d", r=4) for i in range(4))
            exb, gn, m1, xt2 = (G[:, i, 4 * D:8 * D].rearrange("p (r d) -> p r d", r=4) for i in range(4))
            xs = sb3("xs", [P, 4, D])
            ohf = oh[:, :, :, :].rearrange("p a b c -> p (a b c)")
            ohTf = ohT[:, :, :, :].rearrange("p a b c -> p (a b c)")
            NE = NB * NX

            def small(i):
                base = (ohf, ohTf)[i // 4]
                return base[:, (i % 4) * 512:(i % 4) * 512 + NE].rearrange("p (t e) -> p t e", e=NX)

            L, dl, pe_, eq, used, first, tot, inc = (small(i) for i in range(8))
            pos = G[:, 0, 1024:1024 + NE].rearrange("p (t e) -> p t e", e=NX)
            fp = G[:, 1, 1024:1024 + NE].rearrange("p (t e) -> p t e", e=NX)
            fe = G[:, 2, 1024:1024 + NE].rearrange("p (t e) -> p t e", e=NX)
            mx, ssum, prb, posf, ef, fsum, kept, slot, sfar = (sb3(f"tk{i}", [P, NB]) for i in range(9))
            tokf = sb3("tokf", [P, NB])
            acc_t = acc[:, :].rearrange("p (t g) -> p t g", g=ROW)
            GT = 7
            sidx = sb3("sidx", [P, NB], I32)
            tri = sb3("tri", [P, P])
            e8 = sb3("e8", [P, NX])
            vcol = sb3("vcol", [P, 1])

            s_par = sem3("s_par")
            c_const = sem3("c_const")
            v_ = sem3("v_")
            v_var, a_std, a_p = (sem3(n) for n in ("v_var", "a_std", "a_p"))
            r_xr, r_xb, r_o1, r_o2, r_ex, r_e1, r_v, r_st = (sem3("r_" + n) for n in "xr xb o1 o2 ex e1 v st".split())
            q_g, q_xb, q_m, q_x1, q_st = (sem3("q_" + n) for n in "g xb m x1 st".split())
            w_n, w_k, w_t, w_tc, w_l, w_L = (sem3("w_" + n) for n in "n k t tc l L".split())
            v_first, p_cum, v_idx, s_sc, s_xst = (sem3(n) for n in ("v_first", "p_cum", "v_idx", "s_sc", "s_xst"))
            v_nmr, v_dl = sem3("v_nmr"), sem3("v_dl")

            def tile(a, t):
                return a[:, bass.ds(t, 1), :].rearrange("p a s -> p (a s)")

            def acc_row(t):
                return acc[:, bass.ds(t * ROW, D)]

            block = c3.enter_context(nc.Block())

            @block.sync
            def _(sp):
                for i, a in enumerate((bias, ln_s, ln_b)):
                    sp.dma_start(biasT[:, i, :], a.rearrange("(o d) -> o d", o=1).to_broadcast([P, D])).then_inc(s_par, 16)
                sp.dma_start(gw[:, :, :], gate_w.rearrange("(k p) e -> p k e", p=P)).then_inc(s_par, 16)
                sp.dma_start(gb[:, :], gate_b.rearrange("(o d) -> o d", o=1).to_broadcast([P, NX])).then_inc(s_par, 16)
                sp.dma_start(w1f[:, :, :], w1[0].rearrange("(k p) f -> p k f", p=P)).then_inc(s_wt[0], 16)
                sp.dma_start(w2f[:, :, :], w2[0].rearrange("(c p) d -> p c d", p=P)).then_inc(s_wt[0], 16)
                stores = 0
                for t0 in range(0, NB, GT):
                    t1 = min(NB, t0 + GT)
                    sp.wait_ge(q_x1, t1)
                    sp.dma_start(xres[t0 * P:t1 * P, :].rearrange("(t p) d -> p t d", p=P), x_sb[:, t0:t1, :]).then_inc(s_xst, 16)
                    full = min(t1, NB - 1)
                    sp.dma_start(out[t0 * P:full * P, :].rearrange("(t p) d -> p t d", p=P), x_sb[:, t0:full, :]).then_inc(s_xst, 16)
                    stores += 2
                sp.dma_start(out[(NB - 1) * P:N, :], x_sb[0:TAIL, NB - 1, :]).then_inc(s_xst, 16)
                sp.wait_ge(s_xst, 16 * (stores + 1))

            @block.gpsimd
            def _(pool):
                pool.memset(tri[:, :], 1.0).then_inc(c_const, 1)
                pool.memset(vcol[:, :], 1.0).then_inc(c_const, 1)
                pool.iota(e8[:, :], [[1, NX]], base=0, channel_multiplier=0,
                          allow_small_or_imprecise_dtypes=True).then_inc(c_const, 1)
                pool.iota(tokf[:, :], [[P, NB]], base=-FAR, channel_multiplier=1,
                          allow_small_or_imprecise_dtypes=True).then_inc(c_const, 1)
                pool.wait_ge(c_const, 4)
                pool.affine_select(out=tri[:, :], in_=tri[:, :], compare_op=ALU.is_ge, fill=0.0, base=0,
                                   pattern=[[1, P]], channel_multiplier=-1).then_inc(c_const, 1)
                pool.affine_select(out=vcol[:, :], in_=vcol[:, :], compare_op=ALU.is_ge, fill=0.0, base=TAIL - 1,
                                   pattern=[[0, 1]], channel_multiplier=-1).then_inc(c_const, 1)
                pool.wait_ge(s_par, 80)

                def add_bias(t, r, n):
                    pool.wait_ge(r_xr, t + 1)
                    pool.tensor_tensor(xb[:, r, :], xr[:, r, :], biasT[:, 0, :], ALU.add).then_inc(r_xb, 1)

                def add_agg(t, r, n):
                    pool.wait_ge(r_o1, t + 1)
                    pool.wait_ge(r_xb, t + 1)
                    wait_for(pool, r_v, t - 3)
                    pool.tensor_tensor(o2[:, r, :], o1[:, r, :], xb[:, r, :], ALU.add).then_inc(r_o2, 1)

                slots(pool, NB, 4, [(0, add_bias), (1, add_agg)])

                def add_lnb(t, r, n):
                    pool.tensor_tensor(tile(x_sb, t), tile(x_sb, t), biasT[:, 2, :], ALU.add).then_inc(q_xb, 1)

                slots(pool, NB, 2, [(0, add_lnb)])
                pool.wait_ge(v_idx, 1)
                pool.wait_ge(w_k, NB)
                for t in range(NB):
                    pool.indirect_dma_start(xbuf, bass.IndirectOffsetOnAxis(sidx[:, t:t + 1], 0),
                                            acc[:, t * ROW:t * ROW + XR], None,
                                            bounds_check=NX * SL - 1, oob_is_err=False).then_inc(s_sc, 16)
                pool.wait_ge(s_sc, 16 * NB)

            @block.scalar
            def _(act):
                act.wait_ge(v_nmr, 1)

                def norm_x(t, r, n):
                    wait_for(act, r_xb, t - 3)
                    own(act, gate_act)
                    act.activation(xr[:, r, :], tile(x_sb, t), ACT.Identity, scale=rstd[:, bass.ds(t, 1)],
                                   bias=nmr[:, bass.ds(t, 1)]).then_inc(r_xr, 1)

                def exp_o(t, r, n):
                    act.wait_ge(r_o2, t + 1)
                    act.activation(exb[:, r, :], o2[:, r, :], ACT.Exp).then_inc(r_ex, 1)

                slots(act, NB, 4, [(0, norm_x), (2, exp_o)])
                act.wait_ge(v_var, 1)
                act.activation(rs[:, :], var[:, :], ACT.Sqrt, bias=epst[:, :]).then_inc(a_std, 1)
                act.wait_ge(v_nmr, 2)

                def norm_v(t, r, n):
                    wait_for(act, q_m, t - 3)
                    own(act, gate_act)
                    act.activation(gn[:, r, :], acc_row(t), ACT.Identity, scale=rs[:, bass.ds(t, 1)],
                                   bias=nmr[:, bass.ds(t, 1)]).then_inc(q_g, 1)

                slots(act, NB, 4, [(0, norm_v)])
                act.wait_ge(v_var, 2)
                act.activation(rs[:, :], var[:, :], ACT.Sqrt, bias=epst[:, :]).then_inc(a_std, 1)
                act.wait_ge(v_nmr, 3)

                def norm_x1(t, r, n):
                    wait_for(act, w_t, t - 3)
                    wait_for(act, w_k, t - 3)
                    own(act, gate_act)
                    act.activation(xs[:, r, :], tile(x_sb, t), ACT.Identity, scale=rs[:, bass.ds(t, 1)],
                                   bias=nmr[:, bass.ds(t, 1)]).then_inc(w_n, 1)

                slots(act, NB, 4, [(0, norm_x1)])
                act.wait_ge(v_dl, 1)
                act.activation(pe_, dl, ACT.Exp).then_inc(a_p, 1)

            @block.tensor
            def _(pe):
                pe.wait_ge(s_par, 80)
                pe.wait_ge(c_const, 6)

                def turn(t, r, n):
                    pe.wait_ge(w_n, t + 1)
                    wait_for(pe, w_tc, t - 1)
                    for k in range(KD):
                        mm = pe.transpose(bank[r % 2][:, k * P:(k + 1) * P],
                                          xs[:, r, k * P:(k + 1) * P], ident[:, :])
                    mm.then_inc(w_t, 1)

                def logits(t, r, n):
                    pe.wait_ge(w_tc, t + 1)
                    wait_for(pe, w_L, t - 1)
                    for k in range(KD):
                        mm = pe.matmul(bank[2 + r % 2][:, 0:NX], xt2[:, r, k * P:(k + 1) * P], gw[:, k, :],
                                       start=(k == 0), stop=(k == KD - 1))
                    mm.then_inc(w_l, 1)

                slots(pe, NB, 4, [(0, turn), (1, logits)])
                pe.wait_ge(v_first, 1)
                pe.matmul(bank[4][:, 0:NE], tri[:, :], first.rearrange("p t e -> p (t e)"), start=True, stop=True)
                pe.matmul(bank[5][:, 0:NE], ones[:, :], first.rearrange("p t e -> p (t e)"), start=True,
                          stop=True).then_inc(p_cum, 1)

            @block.vector
            def _(dve):
                link = [0]

                def chained(ins, wait=True):
                    link[0] += 1
                    ins.then_inc(v_, 1)
                    if wait:
                        dve.wait_ge(v_, link[0])

                def join_stats(n):
                    chained(dve.tensor_tensor(mean[:, :], st[:, :, 1], st[:, :, 4], ALU.add), False)
                    chained(dve.tensor_tensor(var[:, :], st[:, :, 2], st[:, :, 5], ALU.add), False)
                    chained(dve.tensor_tensor(dif[:, :], st[:, :, 1], st[:, :, 4], ALU.subtract))
                    chained(dve.scalar_tensor_tensor(dif[:, :], dif[:, :], 0.25, dif[:, :], ALU.mult, ALU.mult))
                    dve.scalar_tensor_tensor(var[:, :], var[:, :], 1.0 / D, dif[:, :], ALU.mult, ALU.add).then_inc(v_var, 1)
                    dve.wait_ge(a_std, n)
                    chained(dve.reciprocal(rs[:, :], rs[:, :]))
                    dve.scalar_tensor_tensor(nmr[:, :], mean[:, :], -0.5, rs[:, :], ALU.mult, ALU.mult).then_inc(v_nmr, 1)

                dve.scalar_tensor_tensor(nmr[:, :], mv[:, :, 0], -1.0, rstd[:, :], ALU.mult, ALU.mult).then_inc(v_nmr, 1)
                dens = acc[:, :].rearrange("p (t h g) -> p (t h) g", h=HEADS, g=GC)[:, :, HC]
                rflat = rden[:, :, :].rearrange("p t h -> p (t h)")
                chained(dve.tensor_scalar(rflat, dens, 1e-16, None, ALU.add))
                chained(dve.reciprocal(rflat, rflat))

                def average(t, r, n):
                    wait_for(dve, r_o2, t - 3)
                    dve.tensor_tensor(o1[:, r, :].rearrange("p (h c) -> p h c", c=HC),
                                      acc[:, bass.ds(t * ROW, ROW)].rearrange("p (h g) -> p h g", g=GC)[:, :, 0:HC],
                                      rden[:, bass.ds(t, 1), :].rearrange("p a h -> p (a h)").unsqueeze(2).to_broadcast([P, HEADS, HC]),
                                      ALU.mult).then_inc(r_o1, 1)

                def elu_below(t, r, n):
                    dve.wait_ge(r_ex, t + 1)
                    dve.tensor_scalar(exb[:, r, :], exb[:, r, :], 1.0, -1.0, ALU.min, ALU.add).then_inc(r_e1, 1)

                def elu(t, r, n):
                    dve.wait_ge(r_e1, t + 1)
                    dve.wait_ge(r_o1, t + 1)
                    dve.scalar_tensor_tensor(acc_row(t), o2[:, r, :], 0.0, exb[:, r, :], ALU.max, ALU.add).then_inc(r_v, 1)

                def stats(t, r, n):
                    dve.wait_ge(r_v, t + 1)
                    dve.bn_stats(tile(st, t), acc_row(t)).then_inc(r_st, 1)

                slots(dve, NB, 4, [(0, average), (3, elu_below), (4, stats), (3, elu)])
                dve.wait_ge(r_st, NB)
                join_stats(1)

                def second(t, r, n):
                    dve.wait_ge(q_g, t + 1)
                    wait_for(dve, q_x1, t - 3)
                    dve.tensor_tensor(m1[:, r, :], gn[:, r, :], biasT[:, 1, :], ALU.mult).then_inc(q_m, 1)

                def second_add(t, r, n):
                    dve.wait_ge(q_m, t + 1)
                    dve.wait_ge(q_xb, t + 1)
                    dve.tensor_tensor(tile(x_sb, t), m1[:, r, :], tile(x_sb, t), ALU.add).then_inc(q_x1, 1)

                def second_stats(t, r, n):
                    dve.wait_ge(q_x1, t + 1)
                    dve.bn_stats(tile(st, t), tile(x_sb, t)).then_inc(q_st, 1)

                slots(dve, NB, 4, [(0, second), (2, second_stats), (1, second_add)])
                dve.wait_ge(q_st, NB)
                join_stats(2)

                def keep_xn(t, r, n):
                    dve.wait_ge(w_n, t + 1)
                    dve.tensor_copy(acc_row(t), xs[:, r, :]).then_inc(w_k, 1)

                def copy_xt(t, r, n):
                    dve.wait_ge(w_t, t + 1)
                    wait_for(dve, w_l, t - 3)
                    dve.tensor_copy(xt2[:, r, :], bank[r % 2][:, 0:D]).then_inc(w_tc, 1)

                def take_logits(t, r, n):
                    dve.wait_ge(w_l, t + 1)
                    dve.tensor_tensor(L[:, bass.ds(t, 1), :].rearrange("p a e -> p (a e)"), bank[2 + r % 2][:, 0:NX], gb[:, :],
                                      ALU.add).then_inc(w_L, 1)

                slots(dve, NB, 4, [(0, keep_xn), (1, copy_xt), (2, take_logits)])
                dve.wait_ge(w_L, NB)

                def over_e(a):
                    return a[:, :].unsqueeze(2).to_broadcast([P, NB, NX])

                chained(dve.tensor_reduce(mx[:, :], L, AX_X, ALU.max))
                dve.tensor_tensor(dl, L, over_e(mx), ALU.subtract).then_inc(v_dl, 1)
                dve.wait_ge(a_p, 1)
                chained(dve.tensor_reduce(ssum[:, :], pe_, AX_X, ALU.add), False)
                chained(dve.tensor_scalar(eq, pe_, 1.0, None, ALU.is_ge), False)
                chained(dve.memset(used, 0.0))
                chained(dve.reciprocal(prb[:, :], ssum[:, :]), False)
                for e in range(1, NX):
                    chained(dve.tensor_tensor(used[:, :, e], used[:, :, e - 1], eq[:, :, e - 1], ALU.max))
                chained(dve.tensor_tensor(first, eq, used, ALU.is_gt))
                dve.wait_ge(c_const, 6)
                dve.tensor_scalar(first[:, NB - 1, :], first[:, NB - 1, :], vcol[:, 0:1], None, ALU.mult).then_inc(v_first, 1)
                dve.wait_ge(p_cum, 1)
                chained(dve.tensor_copy(tot.rearrange("p t e -> p (t e)"), bank[5][:, 0:NE]))
                for e in range(NX):
                    chained(dve.tensor_tensor_scan(inc[:, :, e], ones[:, 0:NB], tot[:, :, e], 0.0, ALU.mult, ALU.add), e == NX - 1)
                chained(dve.tensor_tensor(inc, inc, tot, ALU.subtract))
                chained(dve.scalar_tensor_tensor(pos.rearrange("p t e -> p (t e)"), bank[4][:, 0:NE], -1.0,
                                                 inc.rearrange("p t e -> p (t e)"), ALU.add, ALU.add))
                chained(dve.tensor_tensor(fp, pos, first, ALU.mult), False)
                chained(dve.tensor_tensor(fe, first, e8[:, :].unsqueeze(1).to_broadcast([P, NB, NX]), ALU.mult))
                chained(dve.tensor_reduce(posf[:, :], fp, AX_X, ALU.add), False)
                chained(dve.tensor_reduce(ef[:, :], fe, AX_X, ALU.add), False)
                chained(dve.tensor_reduce(fsum[:, :], first, AX_X, ALU.add))
                chained(dve.scalar_tensor_tensor(kept[:, :], posf[:, :], float(CAP), fsum[:, :], ALU.is_lt, ALU.mult), False)
                chained(dve.scalar_tensor_tensor(slot[:, :], ef[:, :], float(SL), posf[:, :], ALU.mult, ALU.add))
                chained(dve.tensor_tensor(acc_t[:, :, D], prb[:, :], kept[:, :], ALU.mult), False)
                chained(dve.tensor_copy(acc_t[:, :, D + 1], tokf[:, :]), False)
                chained(dve.scalar_tensor_tensor(sfar[:, :], slot[:, :], -float(FAR), kept[:, :], ALU.add, ALU.mult))
                dve.tensor_scalar(sidx[:, :], sfar[:, :], float(FAR), None, ALU.add).then_inc(v_idx, 1)

        with ExitStack() as c4:
            def sem4(name):
                return ctx.enter_context(nc.semaphore(name))

            CH = SL // 2
            MT = CH // P
            NI = 2 * NX
            w1s = [w1f[:, :, :], acc[:, 0:KD * F].rearrange("p (k f) -> p k f", k=KD)]
            o = KD * F
            w2s = [w2f[:, :, :], acc[:, o:o + FC * D].rearrange("p (c d) -> p c d", c=FC)]
            o += FC * D
            xe = [acc[:, o + i * MT * XR:o + (i + 1) * MT * XR].rearrange("p (m d) -> p m d", m=MT) for i in range(4)]
            assert o + 4 * MT * XR <= NB * ROW and 4 * P * MT == 4 * CH
            h1 = [G[:, 2 * i:2 * i + 2, :].rearrange("p a b -> p (a b)")[:, 0:FC * CH].rearrange("p (c n) -> p c n", c=FC)
                  for i in range(2)]
            xT = [oh[:, i].rearrange("p a b -> p (a b)")[:, 0:KD * CH].rearrange("p (k n) -> p k n", k=KD) for i in range(2)]
            yo = [ohT[:, i].rearrange("p a b -> p (a b)")[:, 0:MT * D].rearrange("p (m d) -> p m d", m=MT) for i in range(2)]
            b1s = c4.enter_context(nc.sbuf_tensor("b1s", [P, NX * FC], F32))
            b2s = c4.enter_context(nc.sbuf_tensor("b2s", [P, NX * D], F32))

            xf = x_sb[:, :, :].rearrange("p t d -> p (t d)")
            xg = [xf[:, i * MT * D:(i + 1) * MT * D].rearrange("p (m d) -> p m d", m=MT) for i in range(2)]
            yc, bad, nan, zero = (xf[:, (i + 2) * MT * D:(i + 3) * MT * D].rearrange("p (m d) -> p m d", m=MT) for i in range(4))
            bad, nan = bad.bitcast(I32), nan.bitcast(I32)
            wm = c4.enter_context(nc.sbuf_tensor("wm", [P, 4, MT], F32))
            ti = c4.enter_context(nc.sbuf_tensor("ti", [P, 4, MT], I32))

            s_b = sem4("s_b")
            s_xe = [sem4(f"s_xe{i}") for i in range(4)]
            s_out = [sem4(f"s_out{i}") for i in range(4)]
            s_xg = [sem4(f"s_xg{i}") for i in range(2)]
            m_t, m_th, m_xt, m_h, m_relu, m_y, m_yo, m_z, m_id = (sem4("m_" + n) for n in "t th xt h relu y yo z id".split())
            k_w, k_b, k_n, k_c, k_p, k_q, k_o = (sem4("k_" + n) for n in "w b n c p q o".split())
            block = c4.enter_context(nc.Block())

            @block.sync
            def _(sp):
                sp.dma_start(b1s[:, :], b1).then_inc(s_b, 16)
                sp.dma_start(b2s[:, :], b2.rearrange("(o e) d -> o (e d)", o=1).to_broadcast([P, NX * D])).then_inc(s_b, 16)

                def load(t, r, n):
                    wait_for(sp, m_t, t - 3)
                    wait_for(sp, m_id, t - 3)
                    sp.dma_start(xe[r],
                                 xbuf[bass.ds(t * CH, CH), :].rearrange("(m p) d -> p m d", p=P)).then_inc(s_xe[r], 16)
                    if r % 2 == 0 and not (isinstance(t, int) and t == 0):
                        e = 2 * n + r // 2
                        wait_for(sp, m_y, MT * (t - 2))
                        sp.dma_start(w1s[r // 2], w1[bass.ds(e, 1)].rearrange("o (k p) f -> p (o k) f", p=P)).then_inc(s_wt[r // 2], 16)
                        sp.dma_start(w2s[r // 2], w2[bass.ds(e, 1)].rearrange("o (c p) d -> p (o c) d", p=P)).then_inc(s_wt[r // 2], 16)

                slots(sp, NI, 4, [(0, load)])

            @block.gpsimd
            def _(pool):
                pool.wait_ge(m_z, 3)

                def residuals(t, r, n):
                    pool.wait_ge(m_id, t + 1)
                    own(pool, gate)
                    if not (isinstance(t, int) and t < 2):
                        pool.wait_ge(k_o, t - 1)
                        own(pool, gate)
                    for m in range(MT):
                        pool.indirect_dma_start(xg[r % 2][:, m, :], None, xres, bass.IndirectOffsetOnAxis(ti[:, r, m:m + 1], 0),
                                                bounds_check=NB * P - 1, oob_is_err=False).then_inc(s_xg[r % 2], 16)

                def scatter(t, r, n):
                    pool.wait_ge(k_o, t + 1)
                    own(pool, gate)
                    for m in range(MT):
                        pool.indirect_dma_start(out, bass.IndirectOffsetOnAxis(ti[:, r, m:m + 1], 0), yo[r % 2][:, m, :], None,
                                                bounds_check=N - 1, oob_is_err=False).then_inc(s_out[r], 16)

                slots(pool, NI, 4, [(0, residuals), (1, scatter)])
                for i in range(4):
                    pool.wait_ge(s_out[i], 16 * MT * (NI // 4))

            @block.tensor
            def _(pe):
                def turn(t, r, n):
                    pe.wait_ge(s_xe[r], 16 * (n + 1))
                    for half in range(2):
                        wait_for(pe, m_xt, 2 * t + half - 1)
                        for m in range(MT // 2):
                            for k in range(KD):
                                c = half * (MT // 2) + m
                                mm = pe.transpose(bank[half][:, k * 256 + m * P:k * 256 + (m + 1) * P],
                                                  xe[r][:, c, k * P:(k + 1) * P], ident[:, :])
                        mm.then_inc(m_t if half == 1 else m_th, 1)

                def up(t, r, n):
                    pe.wait_ge(m_xt, 2 * t + 2)
                    pe.wait_ge(s_wt[r // 2], 32 * (n + 1))
                    for c in range(FC):
                        wait_for(pe, m_relu, FC * t + c - 3)
                        for k in range(KD):
                            mm = pe.matmul(bank[2 + c % 4][:, 0:CH], w1s[r // 2][:, k, c * P:(c + 1) * P], xT[r % 2][:, k, :],
                                           start=(k == 0), stop=(k == KD - 1))
                        mm.then_inc(m_h, 1)

                def down(t, r, n):
                    pe.wait_ge(m_relu, FC * (t + 1))
                    for m in range(MT):
                        wait_for(pe, m_yo, MT * t + m - 1)
                        for c in range(FC):
                            mm = pe.matmul(bank[6 + m % 2][:, 0:D], h1[r % 2][:, c, m * P:(m + 1) * P], w2s[r // 2][:, c, :],
                                           start=(c == 0), stop=(c == FC - 1))
                        mm.then_inc(m_y, 1)

                slots(pe, NI, 4, [(1, up), (0, turn), (1, down)])

            @block.scalar
            def _(act):
                act.wait_ge(s_b, 32)

                def relu(t, r, n):
                    wait_for(act, m_y, MT * (t - 1))
                    for c in range(FC):
                        act.wait_ge(m_h, FC * t + c + 1)
                        e = 2 * n + r // 2
                        own(act, gate_act)
                        act.activation(h1[r % 2][:, c, :], bank[2 + c % 4][:, 0:CH], ACT.Relu,
                                       bias=b1s[:, bass.ds(e * FC + c, 1)]).then_inc(m_relu, 1)

                slots(act, NI, 4, [(0, relu)])

            @block.vector
            def _(dve):
                dve.memset(zero, 0.0).then_inc(m_z, 1)
                dve.memset(xg[0], 0.0).then_inc(m_z, 1)
                dve.memset(xg[1], 0.0).then_inc(m_z, 1)
                dve.wait_ge(m_z, 3)
                dve.wait_ge(s_b, 32)

                def copy_xt(t, r, n):
                    wait_for(dve, m_h, FC * (t - 1))
                    for half in range(2):
                        if half == 0:
                            dve.wait_ge(m_th, t + 1)
                        else:
                            dve.wait_ge(m_t, t + 1)
                        dve.tensor_copy(xT[r % 2][:, :, half * 256:(half + 1) * 256],
                                        bank[half][:, :].rearrange("p (k n) -> p k n", k=KD)).then_inc(m_xt, 1)

                def take_ids(t, r, n):
                    dve.wait_ge(s_xe[r], 16 * (n + 1))
                    wait_for(dve, s_out[r], 16 * MT * n)
                    wait_for(dve, k_w, t - 3)
                    dve.tensor_copy(wm[:, r, :], xe[r][:, :, D])
                    dve.tensor_scalar(ti[:, r, :], xe[r][:, :, D + 1], float(FAR), None, ALU.add).then_inc(m_id, 1)

                def add_b2(t, r, n):
                    e = 2 * n + r // 2
                    wait_for(dve, s_out[(r - 2) % 4], 16 * MT * (n + (r - 2) // 4 + 1))
                    for m in range(MT):
                        dve.wait_ge(m_y, MT * t + m + 1)
                        dve.tensor_tensor(yo[r % 2][:, m, :], bank[6 + m % 2][:, 0:D], b2s[:, bass.ds(e * D, D)],
                                          ALU.add).then_inc(m_yo, 1)

                def weigh_y(t, r, n):
                    y = yo[r % 2]
                    dve.wait_ge(m_yo, MT * (t + 1))
                    dve.wait_ge(m_id, t + 1)
                    dve.tensor_tensor(y, y, wm[:, r, :].unsqueeze(2).to_broadcast([P, MT, D]), ALU.mult).then_inc(k_w, 1)
                    dve.wait_ge(k_w, t + 1)
                    wait_for(dve, k_q, t)
                    dve.tensor_scalar(bad, y, 0.0, 0.0, ALU.mult, ALU.not_equal).then_inc(k_b, 1)
                    dve.tensor_tensor(nan, y, y, ALU.not_equal).then_inc(k_n, 1)
                    dve.tensor_scalar(yc, y, 10000.0, -10000.0, ALU.min, ALU.max).then_inc(k_c, 1)
                    dve.wait_ge(k_c, t + 1)
                    dve.wait_ge(k_n, t + 1)
                    dve.wait_ge(k_b, t + 1)
                    own(dve, gate_dve)
                    dve.copy_predicated(y, bad, yc).then_inc(k_p, 1)
                    dve.wait_ge(k_p, t + 1)
                    own(dve, gate_dve)
                    dve.copy_predicated(y, nan, zero).then_inc(k_q, 1)
                    dve.wait_ge(k_q, t + 1)
                    dve.wait_ge(s_xg[r % 2], 16 * MT * (2 * n + r // 2 + 1))
                    dve.tensor_tensor(y, y, xg[r % 2], ALU.add).then_inc(k_o, 1)

                slots(dve, NI, 4, [(0, copy_xt), (0, take_ids), (1, add_b2), (1, weigh_y)])


def kernel(**inputs):
    import numpy as np
    import concourse.bacc as bacc
    from concourse.bass_utils import run_bass_kernel_spmd as run

    nc = bacc.Bacc("TRN2", target_bir_lowering=False, num_devices=1)
    src, dst = np.asarray(inputs["src"]), np.asarray(inputs["dst"])
    e = src.shape[0]
    pad = np.full(2 * STEP, PAD_NODE, np.int32)
    d = np.concatenate([np.full(SUB, -1, np.int32), dst, pad, np.full(SUB, PAD_NODE, np.int32)])
    m = e + 2 * STEP
    ed = np.stack([np.concatenate([src, np.zeros(2 * STEP, np.int32)]), d[0:m], d[SUB:SUB + m], d[2 * SUB:2 * SUB + m]], axis=1)
    cols = -(-e // P)
    dstp = np.concatenate([dst, np.full(P * cols - e, PAD_NODE, np.int32)]).reshape(P, cols)
    arrays = {"ed": np.ascontiguousarray(ed), "dstp": np.ascontiguousarray(dstp)}
    for name in ("x", "L0_gnn_W", "L0_gnn_att_src", "L0_gnn_att_dst", "L0_gnn_bias", "L0_gnn_ln_scale", "L0_gnn_ln_bias",
                 "L0_ffn_gate_w", "L0_ffn_gate_b", "L0_ffn_w1", "L0_ffn_b1", "L0_ffn_w2", "L0_ffn_b2"):
        arrays[name] = np.ascontiguousarray(inputs[name])
    b1 = arrays["L0_ffn_b1"]
    arrays["L0_ffn_b1"] = np.ascontiguousarray(b1.reshape(b1.shape[0], -1, P).transpose(2, 0, 1).reshape(P, -1))
    aps = {k: nc.dram_tensor("in_" + k, a.shape, mybir.dt.from_np(a.dtype), kind="ExternalInput").ap() for k, a in arrays.items()}
    o = nc.dram_tensor("out", [arrays["x"].shape[0], arrays["x"].shape[1]], F32, kind="ExternalOutput").ap()
    build(nc, aps["x"], aps["ed"], aps["dstp"], *[aps[k] for k in list(arrays)[3:]], o)
    r = run(nc, [{"in_" + k: a for k, a in arrays.items()}], core_ids=[0])
    return r.results[0]["out"]
```

```python
from contextlib import ExitStack

import concourse.bass as bass
from concourse import mybir

P = 128
F32 = mybir.dt.float32
I32 = mybir.dt.int32
BF16 = mybir.dt.bfloat16
ACT = mybir.ActivationFunctionType
ALU = mybir.AluOpType
AX_X = mybir.AxisListType.X

HEADS, HC = 8, 32
GC = HC + 1
SUB = 2
STEP = SUB * P
UN = 6
NJ = SUB * UN
NA = 10
NQ = 6
PW = NJ // NQ
PH = 4
PAD_NODE = 9999
BIG = 1.0e30
SLOPE = 0.2
EPS = 1e-5
FAR = 1 << 20


def wait_for(eng, sem, count):
    if isinstance(count, int) and count <= 0:
        return
    eng.wait_ge(sem, count)


def own(eng, carrier):
    eng.sem_inc(carrier, 1)


def slots(eng, total, period, stages, first=0):
    lag_max = max(lag for lag, _ in stages)
    loops = (total - period) // period
    assert lag_max <= period and loops >= 1 and first % period == 0

    def straight(s):
        for lag, f in stages:
            t = s - lag
            if 0 <= t < total:
                f(first + t, t % period, (first + t) // period)

    for s in range(period):
        straight(s)
    with eng.Fori(1, 1 + loops) as k:
        for r in range(period):
            for lag, f in stages:
                d = r - lag
                f(k * period + (first + d), d % period, k + (first + d) // period)
    for s in range(period * (1 + loops), total + lag_max):
        straight(s)


def build(nc, x, ed, dstp, W, att_s, att_d, bias, ln_s, ln_b, gate_w, gate_b, w1, b1, w2, b2, out):
    N, D = x.shape
    E = ed.shape[0] - 2 * STEP
    NB = -(-N // P)
    TAIL = N - (NB - 1) * P
    ROW = HEADS * GC
    NX = gate_w.shape[1]
    F = w1.shape[2]
    CAP = -(-5 * N // (4 * NX))
    SL = -(-CAP // P) * P
    NSTEP = (E + NB * (STEP - 1)) // STEP
    NBATCH = -(-NSTEP // UN)
    TS = 4 * P
    assert NBATCH * UN <= TS and D == HEADS * HC
    DIV = 1 << 12
    PART = -(-DIV // SUB)
    assert (E // P + SUB) * SUB < DIV and (E // P + SUB) * PART < 1 << 24
    NH = NJ // 2
    EC = dstp.shape[1]
    KD = D // P
    FC = F // P

    table = nc.dram_tensor("table", [NB * P, ROW], F32).ap()
    sched_e = nc.dram_tensor("sched_e", [P, TS // P], I32).ap()
    sched_b = nc.dram_tensor("sched_b", [P, TS // P], I32).ap()
    sched_f = nc.dram_tensor("sched_f", [P, TS // P], F32).ap()
    XR = D + 2
    xbuf = nc.dram_tensor("xbuf", [NX * SL, XR], F32).ap()
    xres = nc.dram_tensor("xres", [NB * P, D], F32).ap()

    with ExitStack() as ctx:
        def sb(name, shape, dt=F32):
            return ctx.enter_context(nc.sbuf_tensor(name, shape, dt))

        def sem(name):
            return ctx.enter_context(nc.semaphore(name))

        bank = [ctx.enter_context(nc.psum_tensor(f"bank{i}", [P, 512], F32)) for i in range(8)]

        x_sb = sb("x_sb", [P, NB, D])
        acc = sb("acc", [P, NB * ROW])
        G = sb("G", [P, PH, NJ * ROW])
        oh = sb("oh", [P, 2, NJ, P])
        ohT = sb("ohT", [P, 2, NJ, P])
        adst = sb("adst", [P, NB * HEADS])
        mv = sb("mv", [P, NB, 2])
        rstd = sb("rstd", [P, NB])
        ident = sb("ident", [P, P])
        iota_n = sb("iota_n", [P, P])
        ones = sb("ones", [P, P])
        is_last_p = sb("is_last_p", [P, 1])
        epst = sb("epst", [P, 1])
        etab = sb("etab", [1, TS], I32)
        btab = sb("btab", [1, TS], I32)
        bbase = sb("bbase", [P, TS])
        s_const = sem("s_const")
        gate, gate_sp, gate_pe, gate_act, gate_dve = (sem(n) for n in ("gate", "gate_sp", "gate_pe", "gate_act", "gate_dve"))

        with ExitStack() as c1:
            def sb1(name, shape, dt=F32):
                return c1.enter_context(nc.sbuf_tensor(name, shape, dt))

            def sem1(name):
                return ctx.enter_context(nc.semaphore(name))

            Ws = oh[:, :, :, :].rearrange("p a b c -> p (a b c)")[:, 0:KD * D].rearrange("p (k d) -> p k d", k=KD)
            Wt = ohT[:, :, :, :].rearrange("p a b c -> p (a b c)")[:, 0:KD * D].rearrange("p (k d) -> p k d", k=KD)
            Wx = sb1("Wx", [P, KD, ROW + HEADS])
            att = sb1("att", [P, 2, D])
            st6 = sb1("st6", [P, NB, 6])
            dif = sb1("dif", [P, NB])
            xn = sb1("xn", [P, 4, D])
            xnT = sb1("xnT", [P, 2, D])
            hrow = sb1("hrow", [P, 4, ROW])
            bounds = sb1("bounds", [P, NB])
            dsts = G[:, 1, 0:EC].bitcast(I32)
            dstq = G[:, 1, EC:2 * EC].bitcast(I32)
            dstb = G[:, 1, 2 * EC:2 * EC + EC // 2 + 1].bitcast(BF16)[:, 0:EC]
            cmp = [G[:, 2 + i, 0:EC // 2 + 1].bitcast(BF16)[:, 0:EC] for i in range(2)]
            assert 2 * EC + EC // 2 + 1 <= NJ * ROW and NB < 256
            cnt = sb1("cnt", [P, NB])
            rp = sb1("rp", [P, NB + 1])
            cf = sb1("cf", [P, NB])
            ci = sb1("ci", [P, NB], I32)
            nf = sb1("nf", [P, NB])
            csi = sb1("csi", [P, NB])
            fb = sb1("fb", [P, NB])
            df = sb1("df", [P, NB])
            sid = sb1("sid", [P, 4], I32)
            sidf = sb1("sidf", [P, 4])
            ge = sb1("ge", [P, 4, NB])
            gd = sb1("gd", [P, 4, NB])
            bs = sb1("bs", [P, 4])
            fs = sb1("fs", [P, 4])
            es = sb1("es", [P, 4])
            esi = sb1("esi", [P, 4], I32)
            bsi = sb1("bsi", [P, 4], I32)
            bsf = sb1("bsf", [P, 4])

            XCH = 4
            CT = -(-(NB - 1) // XCH)
            ZR = 2 * P
            ZT = NX * SL // ZR
            assert ZT % 4 == 0 and ZT + 8 <= NB
            SUMT = 4 * ((NB - 9) // 4)
            starts = [i * CT for i in range(XCH)] + [NB]
            chunks = list(zip(starts[:-1], starts[1:]))
            NC0, NCF = 4, 2
            s_x = [sem1(f"s_x{i}") for i in range(XCH + 1)]
            s_w = sem1("s_w")
            s_dst = sem1("s_dst")
            s_tail0 = sem1("s_tail0")
            s_zero = sem1("s_zero")
            s_zst = sem1("s_zst")
            dA = sem1("dA")
            dB = sem1("dB")
            s_std = sem1("s_std")
            s_rstd = sem1("s_rstd")
            s_st = sem1("s_st")
            s_q = sem1("s_q")
            s_var = sem1("s_var")
            s_xn = sem1("s_xn")
            s_xt = sem1("s_xt")
            s_xtc = sem1("s_xtc")
            s_h = sem1("s_h")
            s_hr = sem1("s_hr")
            s_tab = [sem1(f"s_tab{i}") for i in range(4)]
            s_cnt = sem1("s_cnt")
            s_cps = sem1("s_cps")
            s_sch = sem1("s_sch")
            s_schd = sem1("s_schd")
            s_schl = sem1("s_schl")
            block = c1.enter_context(nc.Block())

            @block.sync
            def _(sp):
                for i in range(XCH):
                    t0, t1 = i * CT, min((i + 1) * CT, NB - 1)
                    sp.dma_start(x_sb[:, t0:t1, :], x[t0 * P:t1 * P, :].rearrange("(t p) d -> p t d", p=P)).then_inc(s_x[i], 16)
                    if i == 0:
                        for k, a in enumerate((att_s, att_d)):
                            sp.dma_start(att[:, k, :], a.rearrange("(o h) c -> o (h c)", o=1).to_broadcast([P, D])).then_inc(s_w, 16)
                sp.wait_ge(s_tail0, 1)
                sp.dma_start(x_sb[0:TAIL, NB - 1, :], x[(NB - 1) * P:N, :]).then_inc(s_x[XCH], 16)
                sp.wait_ge(s_zero, 1)

                def put_rows(t, r, n):
                    sp.wait_ge(s_hr, t + 1)
                    sp.dma_start(table[bass.ds(t * P, P), :], hrow[:, r, :]).then_inc(s_tab[r], 16)

                def put_zeros(t, r, n):
                    sp.dma_start(xbuf[bass.ds(t * ZR, ZR), :].rearrange("(p s) d -> p (s d)", p=P),
                                 G[:, 0, 0:ZR // P * XR]).then_inc(s_zst, 16)

                slots(sp, ZT, 4, [(0, put_rows), (0, put_zeros)])
                slots(sp, NB - ZT, 4, [(0, put_rows)], first=ZT)
                for i in range(4):
                    sp.wait_ge(s_tab[i], 16 * len(range(i, NB, 4)))
                sp.wait_ge(s_zst, 16 * ZT)

            @block.gpsimd
            def _(pool):
                pool.iota(iota_n[:, :], [[1, P]], base=0, channel_multiplier=0,
                          allow_small_or_imprecise_dtypes=True).then_inc(s_const, 1)
                pool.iota(bounds[:, :], [[1, NB]], base=1, channel_multiplier=0,
                          allow_small_or_imprecise_dtypes=True).then_inc(s_const, 1)
                pool.iota(sid[:, :], [[1, 4]], base=0, channel_multiplier=4).then_inc(s_const, 1)
                pool.memset(ident[:, :], 0.0).then_inc(s_const, 1)
                pool.memset(is_last_p[:, :], 0.0).then_inc(s_const, 1)
                pool.wait_ge(s_const, 5)
                pool.affine_select(out=ident[:, :], in_=ident[:, :], compare_op=ALU.not_equal, fill=1.0, base=0,
                                   pattern=[[-1, P]], channel_multiplier=1).then_inc(s_const, 1)
                pool.affine_select(out=is_last_p[:, :], in_=is_last_p[:, :], compare_op=ALU.not_equal, fill=1.0,
                                   base=-(P - 1), pattern=[[0, 1]], channel_multiplier=1).then_inc(s_const, 1)
                pool.memset(G[:, 0, :], 0.0).then_inc(s_zero, 1)
                pool.memset(acc[:, :], 0.0)
                pool.wait_ge(s_sch, 1)
                pool.dma_start(sched_e, esi[:, :]).then_inc(s_schd, 16)
                pool.dma_start(sched_b, bsi[:, :]).then_inc(s_schd, 16)
                pool.dma_start(sched_f, bsf[:, :]).then_inc(s_schd, 16)
                pool.wait_ge(s_schd, 48)
                pool.dma_start(etab[:, :], sched_e.rearrange("(a p) q -> a (p q)", a=1)).then_inc(s_schl, 16)
                pool.dma_start(btab[:, :], sched_b.rearrange("(a p) q -> a (p q)", a=1)).then_inc(s_schl, 16)
                pool.dma_start(bbase[:, :], sched_f.rearrange("(a p) q -> a (p q)", a=1).to_broadcast([P, TS])).then_inc(s_schl, 16)
                pool.wait_ge(s_schl, 48)

            @block.scalar
            def _(act):
                act.dma_start(dsts, dstp).then_inc(s_dst, 16)
                act.dma_start(Ws, W.rearrange("(k p) d -> p k d", p=P)).then_inc(s_w, 16)

                def deviation(i):
                    a, b = chunks[i]
                    act.wait_ge(s_var, i + 1)
                    act.activation(rstd[:, a:b], mv[:, a:b, 1], ACT.Sqrt, bias=epst[:, :]).then_inc(s_std, 1)

                def deviation_next(t, r, n):
                    for i in range(1, XCH):
                        if isinstance(t, int) and t == chunks[i][0] - 1:
                            deviation(i)

                def copy_xt(t, r, n):
                    act.wait_ge(s_xt, t + 1)
                    wait_for(act, s_h, t - 1)
                    act.copy(xnT[:, r % 2, :], bank[r % 2][:, 0:D]).then_inc(s_xtc, 1)

                def copy_h(t, r, n):
                    act.wait_ge(s_h, t + 1)
                    wait_for(act, s_tab[r], 16 * n)
                    act.copy(hrow[:, r, :], bank[2 + r % 2][:, 0:ROW])
                    act.copy(adst[:, bass.ds(t * HEADS, HEADS)], bank[2 + r % 2][:, ROW:ROW + HEADS]).then_inc(s_hr, 1)

                deviation(0)
                for a, b in chunks:
                    slots(act, b - a, 4, [(0, copy_xt), (1, deviation_next), (1, copy_h)], first=a)

            @block.tensor
            def _(pe):
                pe.wait_ge(s_const, 7)

                def turn(t, r, n):
                    pe.wait_ge(s_xn, t + 1)
                    wait_for(pe, s_xtc, t - 1)
                    for k in range(KD):
                        mm = pe.transpose(bank[r % 2][:, k * P:(k + 1) * P], xn[:, r, k * P:(k + 1) * P], ident[:, :])
                    mm.then_inc(s_xt, 1)

                def project(t, r, n):
                    pe.wait_ge(s_xtc, t + 1)
                    wait_for(pe, s_hr, t - 1)
                    for k in range(KD):
                        mm = pe.matmul(bank[2 + r % 2][:, 0:ROW + HEADS], xnT[:, r % 2, k * P:(k + 1) * P], Wx[:, k, :],
                                       start=(k == 0), stop=(k == KD - 1))
                    mm.then_inc(s_h, 1)

                slots(pe, SUMT, 4, [(0, turn), (1, project)])
                pe.wait_ge(s_cnt, NB)
                pe.matmul(bank[4][:, 0:NB], ones[:, :], cnt[:, :], start=True, stop=True).then_inc(s_cps, 1)
                slots(pe, NB - SUMT, 4, [(0, turn), (1, project)], first=SUMT)

            @block.vector
            def _(dve):
                dve.memset(x_sb[:, NB - 1, :], 0.0).then_inc(s_tail0, 1)
                dve.memset(epst[:, :], EPS).then_inc(dA, 1)
                dve.memset(ones[:, :], 1.0).then_inc(dA, 1)

                counted = [0]

                def count(off):
                    def f(t, r, n):
                        b = t + off
                        wait_for(dve, s_cnt, b - 1)
                        dve.tensor_scalar(cmp[r % 2], dstb, bounds[:, bass.ds(b, 1)], 0.0, ALU.is_lt, ALU.add,
                                          accum_out=cnt[:, bass.ds(b, 1)]).then_inc(s_cnt, 1)
                    return f

                def count_some(number):
                    for b in range(counted[0], counted[0] + number):
                        count(0)(b, b % 2, b // 2)
                    counted[0] += number

                def stats(t, r, n):
                    dve.bn_stats(st6[:, bass.ds(t, 1), :].rearrange("p a s -> p (a s)"),
                                 x_sb[:, bass.ds(t, 1), :].rearrange("p a s -> p (a s)"))

                def normalise(t, r, n):
                    wait_for(dve, s_xt, t - 3)
                    dve.tensor_scalar(xn[:, r, :], x_sb[:, bass.ds(t, 1), :].rearrange("p a s -> p (a s)"),
                                      mv[:, bass.ds(t, 1), 0], rstd[:, bass.ds(t, 1)],
                                      ALU.subtract, ALU.mult).then_inc(s_xn, 1)

                dve.wait_ge(s_w, 48)
                for k in range(KD):
                    dve.tensor_copy(Wx[:, k, 0:ROW].rearrange("p (h g) -> p h g", g=GC)[:, :, 0:HC],
                                    Ws[:, k, :].rearrange("p (h c) -> p h c", c=HC))
                for i in range(2):
                    for k in range(KD):
                        dve.tensor_tensor(Wt[:, k, :], Ws[:, k, :], att[:, i, :], ALU.mult).then_inc(dA, 1)
                    dve.wait_ge(dA, 2 + 4 * i + 2)
                    for k in range(KD):
                        dst = (Wx[:, k, 0:ROW].rearrange("p (h g) -> p h g", g=GC)[:, :, HC] if i == 0
                               else Wx[:, k, ROW:ROW + HEADS])
                        dve.tensor_reduce(dst, Wt[:, k, :].rearrange("p (h c) -> p h c", c=HC), AX_X, ALU.add).then_inc(dA, 1)
                    dve.wait_ge(dA, 2 + 4 * i + 4)
                dve.wait_ge(s_dst, 16)
                dve.wait_ge(s_const, 7)
                dve.tensor_scalar(dstq, dsts, P.bit_length() - 1, None, ALU.logical_shift_right).then_inc(s_q, 1)
                dve.wait_ge(s_q, 1)
                dve.tensor_copy(dstb, dstq).then_inc(s_q, 1)
                dve.wait_ge(s_q, 2)
                count_some(NC0)

                def stats_ahead(t, r, n):
                    stats(t + CT, r, n)

                for i, (a, b) in enumerate(chunks):
                    if i == 0:
                        dve.wait_ge(s_x[0], 16)
                        slots(dve, b - a - 1, 4, [(0, stats)], first=a)
                    if i == XCH - 1:
                        dve.wait_ge(s_x[XCH], 16)
                        stats(NB - 2, 0, 0)
                    dve.bn_stats(st6[:, b - 1, :], x_sb[:, b - 1, :]).then_inc(s_st, 1)
                    dve.wait_ge(s_st, i + 1)
                    st, mvc, dc = st6[:, a:b], mv[:, a:b], dif[:, a:b]
                    dve.tensor_tensor(mvc[:, :, 0], st[:, :, 1], st[:, :, 4], ALU.add).then_inc(dB, 1)
                    dve.tensor_tensor(mvc[:, :, 1], st[:, :, 2], st[:, :, 5], ALU.add).then_inc(dB, 1)
                    dve.tensor_tensor(dc, st[:, :, 1], st[:, :, 4], ALU.subtract).then_inc(dB, 1)
                    dve.wait_ge(dB, 5 * i + 3)
                    dve.scalar_tensor_tensor(dc, dc, 0.25, dc, ALU.mult, ALU.mult).then_inc(dB, 1)
                    dve.tensor_scalar(mvc[:, :, 0], mvc[:, :, 0], 0.5, None, ALU.mult).then_inc(dB, 1)
                    dve.wait_ge(dB, 5 * i + 5)
                    dve.scalar_tensor_tensor(mvc[:, :, 1], mvc[:, :, 1], 1.0 / D, dc, ALU.mult, ALU.add).then_inc(s_var, 1)
                    if i < XCH - 1:
                        count_some(NCF)
                    dve.wait_ge(s_std, i + 1)
                    dve.reciprocal(rstd[:, a:b], rstd[:, a:b]).then_inc(s_rstd, 1)
                    dve.wait_ge(s_rstd, i + 1)
                    if i == XCH - 1:
                        slots(dve, SUMT + 4 - a, 4, [(0, normalise), (0, count(counted[0] - a))], first=a)
                        counted[0] += SUMT + 4 - a
                        count_some(NB - counted[0])
                        break
                    dve.wait_ge(s_x[i + 1], 16)
                    ahead = CT - 1
                    assert counted[0] % 2 == 0 and a % 2 == 0
                    slots(dve, ahead - 1, 4, [(0, normalise), (0, stats_ahead), (0, count(counted[0] - a))], first=a)
                    counted[0] += ahead - 1
                    for t in (b - 2, b - 1):
                        normalise(t, t % 4, t // 4)
                        if t == b - 2:
                            stats_ahead(t, 0, 0)
                dve.wait_ge(s_cps, 1)
                link = sem1("link")
                dve.memset(rp[:, 0:1], 0.0).then_inc(link, 1)
                dve.tensor_copy(rp[:, 1:NB + 1], bank[4][:, 0:NB]).then_inc(link, 1)
                dve.wait_ge(link, 2)
                dve.tensor_tensor(cf[:, :], rp[:, 1:NB + 1], rp[:, 0:NB], ALU.subtract).then_inc(link, 1)
                dve.wait_ge(link, 3)
                dve.tensor_scalar(ci[:, :], cf[:, :], float(STEP - 1), None, ALU.add).then_inc(link, 1)
                dve.wait_ge(link, 4)
                dve.tensor_scalar(ci[:, :], ci[:, :], P.bit_length() - 1, None, ALU.logical_shift_right).then_inc(link, 1)
                dve.wait_ge(link, 5)
                dve.tensor_scalar(ci[:, :], ci[:, :], float(PART), None, ALU.mult).then_inc(link, 1)
                dve.wait_ge(link, 6)
                dve.tensor_scalar(ci[:, :], ci[:, :], DIV.bit_length() - 1, None, ALU.logical_shift_right).then_inc(link, 1)
                dve.wait_ge(link, 7)
                dve.tensor_copy(nf[:, :], ci[:, :]).then_inc(link, 1)
                dve.wait_ge(link, 8)
                dve.tensor_tensor_scan(csi[:, :], ones[:, 0:NB], nf[:, :], 0.0, ALU.mult, ALU.add).then_inc(link, 1)
                dve.wait_ge(link, 9)
                dve.tensor_tensor(fb[:, :], csi[:, :], nf[:, :], ALU.subtract).then_inc(link, 1)
                dve.wait_ge(link, 10)
                dve.scalar_tensor_tensor(fb[:, :], fb[:, :], -float(STEP), rp[:, 0:NB], ALU.mult, ALU.add).then_inc(link, 1)
                dve.memset(df[:, NB - 1:NB], 0.0).then_inc(link, 1)
                dve.tensor_copy(sidf[:, :], sid[:, :]).then_inc(link, 1)
                dve.wait_ge(link, 13)
                dve.tensor_tensor(df[:, 0:NB - 1], fb[:, 1:NB], fb[:, 0:NB - 1], ALU.subtract).then_inc(link, 1)
                for q in range(4):
                    dve.tensor_scalar(ge[:, q, :], csi[:, :], sidf[:, q:q + 1], None, ALU.is_le).then_inc(link, 1)
                dve.wait_ge(link, 18)
                dve.tensor_reduce(bs[:, :], ge[:, :, :], AX_X, ALU.add).then_inc(link, 1)
                dve.tensor_tensor(gd[:, :, :], ge[:, :, :], df[:, :].unsqueeze(1).to_broadcast([P, 4, NB]),
                                  ALU.mult).then_inc(link, 1)
                dve.wait_ge(link, 20)
                dve.tensor_reduce(fs[:, :], gd[:, :, :], AX_X, ALU.add).then_inc(link, 1)
                dve.tensor_scalar(bsf[:, :], bs[:, :], float(NB - 1), None, ALU.min).then_inc(link, 1)
                dve.wait_ge(link, 22)
                dve.scalar_tensor_tensor(es[:, :], sidf[:, :], float(STEP), fs[:, :], ALU.mult, ALU.add).then_inc(link, 1)
                dve.tensor_copy(bsi[:, :], bsf[:, :]).then_inc(link, 1)
                dve.wait_ge(link, 24)
                dve.tensor_scalar(esi[:, :], es[:, :], float(E), None, ALU.min).then_inc(link, 1)
                dve.tensor_scalar(bsf[:, :], bsf[:, :], float(P), None, ALU.mult).then_inc(link, 1)
                dve.wait_ge(link, 26)
                dve.engine_nop().then_inc(s_sch, 1)
                for t in range(SUMT + 4, NB):
                    normalise(t, t % 4, t // 4)

        with ExitStack() as c2:
            def sb2(name, shape, dt=F32):
                return c2.enter_context(nc.sbuf_tensor(name, shape, dt))

            def sem2(name):
                return ctx.enter_context(nc.semaphore(name))

            ohTb, ohb = (ohT[:, i].rearrange("p j e -> p (j e)").bitcast(BF16).rearrange("p (r j e) -> p r j e", r=2, j=NJ)
                         for i in range(2))
            H1 = UN + 1
            ei = sb2("ei", [P, PH, NJ, 4], I32)
            nl = sb2("nl", [P, NJ, 2])
            drel = sb2("drel", [P, 2, NJ])
            dist = sb2("dist", [P, NA, P], BF16)
            mk = sb2("mk", [P, 2, NJ * HEADS])
            scm = sb2("scm", [P, PH, NJ * HEADS])
            mT = sb2("mT", [NJ * HEADS, P])
            fm = sb2("fm", [NJ * HEADS, P])
            lm = sb2("lm", [P, NJ, HEADS])
            lmr = sb2("lmr", [P, NJ, HEADS])
            lmb = sb2("lmb", [P, 3, NJ, HEADS + 1], BF16)
            identb = sb2("identb", [P, P], BF16)
            adr = sb2("adr", [P, NB * HEADS])
            adb = sb2("adb", [P, 3, NB * HEADS], BF16)
            t8 = sb2("t8", [P, NJ])
            cand = sb2("cand", [P, NJ, HEADS])
            cm = sb2("cm", [P, UN, HEADS])
            zb = sb2("zb", [P, UN, HEADS])
            zc = sb2("zc", [P, HEADS, H1])
            blk = sb2("blk", [P, TS])
            mk5 = sb2("mk5", [P, HEADS, H1])
            adu = sb2("adu", [P, 2, UN, HEADS])
            mx = sb2("mx", [P, 2, HEADS, H1])
            mxr = sb2("mxr", [P, UN, HEADS])
            dmb = sb2("dmb", [P, 2, 3, UN, 2 * HEADS], BF16)
            mold = sb2("mold", [P, HEADS, UN])
            dfm = sb2("dfm", [P, 2, HEADS, UN])
            so = sb2("so", [P, 2, HEADS, UN])
            a1 = sb2("a1", [P, NJ, HEADS])
            a2 = sb2("a2", [P, NJ, HEADS])
            a3 = sb2("a3", [P, NJ, HEADS])
            a4 = sb2("a4", [P, NJ, HEADS])
            cur = sb2("cur", [P, 2, ROW])
            scaled = sb2("scaled", [P, ROW])

            s_ei = [sem2(f"s_ei{r}") for r in range(PH)]
            s_g = [sem2(f"s_g{r}") for r in range(PH)]
            a_sc, a_mk, a_oh, a_so, a_ex, a_d, a_dist, a_one, a_f32, a_acc = (
                sem2("a_" + n) for n in "sc mk oh so ex d dist one f32 acc".split())
            p_tr, p_oh, p_fm, p_nm, p_de, p_agg = (sem2("p_" + n) for n in "tr oh fm nm de agg".split())
            d_tab, d_pre, d_drel, d_mk, d_oh, d_scan, d_lm, d_mk5, d_c, d_mp, d_al, d_msg, d_sc, d_acc = (
                sem2("d_" + n) for n in "tab pre drel mk oh scan lm mk5 c mp al msg sc acc".split())
            N_C, N_AL, N_LM, N_MP = 9, 4, 5, 4

            bTR, bOH, bNM, bDE, bAG = bank[0], bank[1:3], bank[3], bank[4], bank[5:7]

            bOHb = [bOH[i][:, 0:NJ // 2 * P // 2].bitcast(BF16) for i in range(2)]

            def G4(r):
                return G[:, r, :].rearrange("p (j h g) -> p j h g", j=NJ, g=GC)

            block = c2.enter_context(nc.Block())

            def schedule_regs(eng, tab, regs, t, top):
                eng.load(regs, tab[0:1, bass.ds(t * UN, UN)])
                return [eng.snap(q, min_val=0, max_val=top) for q in regs]

            @block.sync
            def _(sp):
                regs = [sp.alloc_register(f"sp_e{u}") for u in range(UN)]

                def load_edges(t, r, n):
                    e0 = schedule_regs(sp, etab, regs, t, E)
                    wait_for(sp, s_g[r], 16 * NJ * n)
                    own(sp, gate_sp)
                    wait_for(sp, d_drel, t - PH + 1)
                    own(sp, gate_sp)
                    for u in range(UN):
                        sp.dma_start(ei[:, r, u * SUB:(u + 1) * SUB, :].rearrange("p s c -> p (s c)"),
                                     ed[bass.ds(e0[u], STEP), :].rearrange("(p s) c -> p (s c)", s=SUB)).then_inc(s_ei[r], 16)

                slots(sp, NBATCH, PH, [(0, load_edges)])

            @block.gpsimd
            def _(pool):
                def gather(t, r, n):
                    pool.wait_ge(s_ei[r], 16 * UN * (n + 1))
                    own(pool, gate)
                    for j in range(NJ):
                        if j % PW == 0 and not (isinstance(t, int) and t < PH):
                            pool.wait_ge(p_agg, NQ * (t - PH) + j // PW + 1)
                            own(pool, gate)
                        pool.indirect_dma_start(G[:, r, j * ROW:(j + 1) * ROW], None, table,
                                                bass.IndirectOffsetOnAxis(ei[:, r, j, 0:1], 0)).then_inc(s_g[r], 16)

                slots(pool, NBATCH, PH, [(0, gather)])

            @block.scalar
            def _(act):
                regs_d = [act.alloc_register(f"act_d{u}") for u in range(UN)]
                regs_a = [act.alloc_register(f"act_a{u}") for u in range(UN)]

                def scale_old(t, r, n):
                    act.wait_ge(d_c, N_C * (t + 1))
                    wait_for(act, d_sc, UN * (t - 1))
                    act.activation(so[:, r % 2], dfm[:, r % 2], ACT.Exp).then_inc(a_so, 1)

                def take_asrc(t, r, n):
                    act.wait_ge(s_g[r], 16 * NJ * (n + 1))
                    wait_for(act, d_al, N_AL * (t - PH + 1))
                    act.copy(scm[:, r].rearrange("p (j h) -> p j h", h=HEADS), G4(r)[:, :, :, HC]).then_inc(a_sc, 1)

                def exps(t, r, n):
                    act.wait_ge(d_al, N_AL * (t + 1))
                    act.activation(G4(r)[:, :, :, HC], a4[:, :, :], ACT.Exp).then_inc(a_ex, 1)

                def copy_mask(t, r, n):
                    act.wait_ge(p_tr, t + 1)
                    wait_for(act, d_scan, t)
                    act.copy(mT[:, :], bTR[0:NJ * HEADS, P:2 * P]).then_inc(a_mk, 1)

                def copy_oht(half):
                    def f(t, r, n):
                        act.wait_ge(p_oh, 2 * t + half + 1)
                        if half == 0:
                            wait_for(act, p_de, t - 1)
                        act.copy(ohTb[:, r % 2, half * NH:(half + 1) * NH, :].rearrange("p j e -> p (j e)"),
                                 bOHb[half]).then_inc(a_oh, 1)
                    return f

                def take_adst(t, r, n):
                    b = schedule_regs(act, btab, regs_d, t, NB - 1)
                    wait_for(act, p_de, t - 1)
                    for u in range(UN):
                        act.copy(adu[:, r % 2, u, :], adst[:, bass.ds(b[u] * HEADS, HEADS)])
                        o = act.copy(dmb[:, r % 2, :, u, 0:HEADS], adb[:, :, bass.ds(b[u] * HEADS, HEADS)])
                    o.then_inc(a_d, 1)

                def one_hots(t, r, n):
                    act.wait_ge(d_drel, t + 1)
                    wait_for(act, a_one, t)
                    for i in range(NA):
                        o = act.activation(dist[:, i, :], iota_n[:, :], ACT.Abs, scale=-1.0,
                                           bias=drel[:, r % 2, NJ - NA + i:NJ - NA + i + 1])
                    o.then_inc(a_dist, 1)

                def one_hots_out(t, r, n):
                    act.wait_ge(a_dist, t + 1)
                    wait_for(act, p_nm, t - 1)
                    wait_for(act, a_f32, t - 1)
                    act.activation(ohb[:, r % 2, NJ - NA:NJ, :], dist[:, :, :], ACT.Relu, scale=-1.0, bias=1.0).then_inc(a_one, 1)

                def one_hots_f32(t, r, n):
                    act.wait_ge(d_oh, t + 1)
                    act.wait_ge(a_one, t + 1)
                    wait_for(act, p_agg, NQ * (t - 1))
                    act.copy(oh[:, r % 2], ohb[:, r % 2]).then_inc(a_f32, 1)

                def keep(us):
                    def f(t, r, n):
                        b = schedule_regs(act, btab, regs_a, t, NB - 1)
                        for u in us:
                            act.wait_ge(d_acc, UN * t + u + 1)
                            wait_for(act, a_acc, UN * t + u)
                            own(act, gate_act)
                            act.copy(acc[:, bass.ds(b[u] * ROW, ROW)], cur[:, u % 2, :]).then_inc(a_acc, 1)
                    return f

                act.wait_ge(d_tab, 12)
                slots(act, NBATCH, PH, [
                    (2, scale_old), (0, take_asrc), (2, exps), (3, keep([4])), (0, copy_mask), (0, one_hots), (3, keep([5])), (0, one_hots_out),
                    (1, one_hots_f32), (2, keep([0])), (0, take_adst), (0, copy_oht(0)), (2, keep([1])), (0, copy_oht(1)),
                    (2, keep([2])), (2, keep([3]))])

            @block.tensor
            def _(pe):
                pe.wait_ge(d_tab, 12)

                def spread(t, r, n):
                    pe.wait_ge(a_oh, 2 * t + 2)
                    pe.wait_ge(d_mp, N_MP * (t + 1))
                    pe.wait_ge(a_d, t + 1)
                    wait_for(pe, d_al, N_AL * t)
                    for j in range(NJ):
                        for i in range(3):
                            mm = pe.matmul(bDE[:, j * 16:j * 16 + 16], ohTb[:, r % 2, j, :], dmb[:, r % 2, i, j // SUB, :],
                                           start=(i == 0), stop=(i == 2))
                    mm.then_inc(p_de, 1)

                def turn(t, r, n):
                    wait_for(pe, d_lm, N_LM * (t - 1) + 1)
                    pe.wait_ge(a_sc, t + 1)
                    pe.wait_ge(d_mk, t + 1)
                    own(pe, gate_pe)
                    pe.transpose(bTR[0:NJ * HEADS, 0:P], scm[:, r], ident[:, :])
                    pe.transpose(bTR[0:NJ * HEADS, P:2 * P], mk[:, r % 2], ident[:, :]).then_inc(p_tr, 1)

                def turn_oh(half):
                    def f(t, r, n):
                        if half == 0:
                            pe.wait_ge(d_oh, t + 1)
                        if half == 1 or NA > NH:
                            pe.wait_ge(a_one, t + 1)
                        wait_for(pe, a_oh, 2 * (t - 1) + half + 1)
                        for j in range(NH):
                            mm = pe.transpose(bOHb[half][:, j * P:(j + 1) * P], ohb[:, r % 2, half * NH + j, :], identb[:, :])
                        mm.then_inc(p_oh, 1)
                    return f

                def turn_max(t, r, n):
                    pe.wait_ge(d_scan, t + 1)
                    own(pe, gate_pe)
                    pe.transpose(bTR[:, 2 * P:2 * P + NJ * HEADS], fm[:, :], ident[0:NJ * HEADS, 0:NJ * HEADS]).then_inc(p_fm, 1)

                def node_max(t, r, n):
                    pe.wait_ge(d_lm, N_LM * (t + 1))
                    pe.wait_ge(d_oh, t + 1)
                    pe.wait_ge(a_one, t + 1)
                    wait_for(pe, d_c, N_C * t)
                    for j in range(NJ):
                        for i in range(3):
                            mm = pe.matmul(bNM[:, j * 9:j * 9 + 9], ohb[:, r % 2, j, :], lmb[:, i, j, :], start=(i == 0), stop=(i == 2))
                    mm.then_inc(p_nm, 1)

                def total(q):
                    u, s0 = q * PW // SUB, q * PW % SUB

                    def f(t, r, n):
                        if q == 0:
                            pe.wait_ge(a_f32, t + 1)
                        pe.wait_ge(d_msg, NQ * t + q + 1)
                        if s0 == 0:
                            wait_for(pe, d_acc, UN * t + u - 1)
                        for s in range(s0, s0 + PW):
                            j = u * SUB + s
                            mm = pe.matmul(bAG[u % 2][:, 0:ROW], oh[:, r % 2, j, :], G[:, r, j * ROW:(j + 1) * ROW],
                                           start=(s == 0), stop=(s == SUB - 1))
                        mm.then_inc(p_agg, 1)
                    return f

                slots(pe, NBATCH, PH, [
                    (0, turn), (1, node_max), (2, total(0)), (0, turn_max), (2, total(1)), (2, total(2)), (0, turn_oh(0)), (0, turn_oh(1)),
                    (2, total(3)), (1, spread), (2, total(4)), (2, total(5))])

            @block.vector
            def _(dve):
                dve.memset(cur[:, :, :], 0.0).then_inc(d_tab, 1)
                dve.memset(mx[:, 1, :, :], -BIG).then_inc(d_tab, 1)
                dve.memset(mk5[:, :, 0], -BIG).then_inc(d_tab, 1)
                dve.memset(blk[:, 0:1], 1.0).then_inc(d_tab, 1)
                dve.memset(lmb[:, :, :, :], 0.0).then_inc(d_tab, 1)
                dve.tensor_copy(identb[:, :], ident[:, :]).then_inc(d_tab, 1)
                dve.tensor_copy(adb[:, 0, :], adst[:, :]).then_inc(d_tab, 1)
                dve.tensor_tensor(blk[:, 1:TS], bbase[:, 1:TS], bbase[:, 0:TS - 1], ALU.not_equal).then_inc(d_tab, 1)
                dve.wait_ge(d_tab, 8)
                dve.tensor_scalar(blk[:, :], blk[:, :], -BIG, None, ALU.mult).then_inc(d_tab, 1)
                dve.tensor_tensor(adr[:, :], adst[:, :], adb[:, 0, :], ALU.subtract).then_inc(d_tab, 1)
                dve.wait_ge(d_tab, 10)
                dve.tensor_copy(adb[:, 1, :], adr[:, :]).then_inc(d_tab, 1)
                dve.wait_ge(d_tab, 11)
                dve.tensor_tensor(adb[:, 2, :], adr[:, :], adb[:, 1, :], ALU.subtract).then_inc(d_tab, 1)
                dve.wait_ge(d_tab, 12)

                def edge_marks(t, r, n):
                    e = ei[:, r]
                    dve.wait_ge(s_ei[r], 16 * UN * (n + 1))
                    dve.tensor_tensor(nl[:, :, :], e[:, :, 2].unsqueeze(2).to_broadcast([P, NJ, 2]), e[:, :, 1:4:2],
                                      ALU.not_equal).then_inc(d_pre, 1)
                    wait_for(dve, a_dist, t - 1)
                    dve.tensor_tensor(drel[:, r % 2, :].rearrange("p (u s) -> p u s", s=SUB),
                                      e[:, :, 2].rearrange("p (u s) -> p u s", s=SUB),
                                      bbase[:, bass.ds(t * UN, UN)].unsqueeze(2).to_broadcast([P, UN, SUB]),
                                      ALU.subtract).then_inc(d_drel, 1)

                def scan_marks(t, r, n):
                    wait_for(dve, p_tr, t - 1)
                    dve.wait_ge(d_pre, 2 * t + 1)
                    dve.tensor_scalar(mk[:, r % 2].rearrange("p (j h) -> p j h", h=HEADS),
                                      nl[:, :, 0].unsqueeze(2).to_broadcast([P, NJ, HEADS]), -BIG, None, ALU.mult).then_inc(d_mk, 1)

                def last_marks(t, r, n):
                    wait_for(dve, p_nm, t)
                    dve.tensor_scalar(lmb[:, 0, :, HEADS], nl[:, :, 1], is_last_p[:, 0:1], None, ALU.max).then_inc(d_pre, 1)

                def one_hot(j):
                    def f(t, r, n):
                        if j == 0:
                            dve.wait_ge(d_drel, t + 1)
                            wait_for(dve, p_nm, t - 1)
                            wait_for(dve, a_f32, t - 1)
                        o = dve.tensor_scalar(ohb[:, r % 2, j, :], iota_n[:, :], drel[:, r % 2, j:j + 1], None, ALU.is_equal)
                        if j == NJ - NA - 1:
                            o.then_inc(d_oh, 1)
                    return f

                de = bDE[:, 0:NJ * 16].rearrange("p (j c) -> p j c", c=16)

                def with_dst(t, r, n):
                    dve.wait_ge(p_de, t + 1)
                    dve.tensor_tensor(a1[:, :, :], scm[:, r].rearrange("p (j h) -> p j h", h=HEADS),
                                      de[:, :, 0:HEADS], ALU.add).then_inc(d_al, 1)

                def alpha(t, r, n):
                    dve.wait_ge(d_al, N_AL * t + 1)
                    dve.scalar_tensor_tensor(a2[:, :, :], a1[:, :, :], SLOPE, a1[:, :, :], ALU.mult, ALU.max).then_inc(d_al, 1)

                def less_max(t, r, n):
                    dve.wait_ge(d_al, N_AL * t + 2)
                    dve.tensor_tensor(a3[:, :, :], a2[:, :, :], de[:, :, HEADS:16], ALU.subtract).then_inc(d_al, 1)

                def bounded(t, r, n):
                    dve.wait_ge(d_al, N_AL * t + 3)
                    wait_for(dve, a_ex, t)
                    dve.tensor_scalar(a4[:, :, :], a3[:, :, :], 0.0, None, ALU.min).then_inc(d_al, 1)

                def scan(t, r, n):
                    dve.wait_ge(a_mk, t + 1)
                    wait_for(dve, p_fm, t)
                    dve.tensor_tensor_scan(fm[:, :], mT[:, :], bTR[0:NJ * HEADS, 0:P], -BIG, ALU.add, ALU.max).then_inc(d_scan, 1)

                def last_max(t, r, n):
                    dve.wait_ge(p_fm, t + 1)
                    dve.wait_ge(d_pre, 2 * (t + 1))
                    dve.tensor_tensor(lm[:, :, :],
                                      bTR[:, 2 * P:2 * P + NJ * HEADS].rearrange("p (j h) -> p j h", h=HEADS),
                                      lmb[:, 0, :, HEADS].unsqueeze(2).to_broadcast([P, NJ, HEADS]), ALU.mult).then_inc(d_lm, 1)

                def last_max_part(i):
                    def f(t, r, n):
                        dve.wait_ge(d_lm, N_LM * t + 1 + i)
                        if i == 0:
                            o = dve.tensor_copy(lmb[:, 0, :, 0:HEADS], lm[:, :, :])
                        elif i == 1:
                            o = dve.tensor_tensor(lmr[:, :, :], lm[:, :, :], lmb[:, 0, :, 0:HEADS], ALU.subtract)
                        elif i == 2:
                            o = dve.tensor_copy(lmb[:, 1, :, 0:HEADS], lmr[:, :, :])
                        else:
                            o = dve.tensor_tensor(lmb[:, 2, :, 0:HEADS], lmr[:, :, :], lmb[:, 1, :, 0:HEADS], ALU.subtract)
                        o.then_inc(d_lm, 1)
                    return f

                def node_max_part(i):
                    def f(t, r, n):
                        m = mx[:, r % 2, :, 1:H1].rearrange("p h u -> p u h")
                        hi, mid, lo = (dmb[:, r % 2, k, :, HEADS:2 * HEADS] for k in range(3))
                        if i == 0:
                            dve.wait_ge(d_c, N_C * t + 7)
                            wait_for(dve, p_de, t - 1)
                            o = dve.tensor_copy(hi, m)
                        else:
                            dve.wait_ge(d_mp, N_MP * t + i)
                        if i == 1:
                            o = dve.tensor_tensor(mxr[:, :, :], m, hi, ALU.subtract)
                        elif i == 2:
                            o = dve.tensor_copy(mid, mxr[:, :, :])
                        elif i == 3:
                            o = dve.tensor_tensor(lo, mxr[:, :, :], mid, ALU.subtract)
                        o.then_inc(d_mp, 1)
                    return f

                nm = bNM[:, 0:NJ * 9].rearrange("p (j c) -> p j c", c=9)

                def presence(t, r, n):
                    dve.wait_ge(p_nm, t + 1)
                    dve.tensor_scalar(t8[:, :], nm[:, :, HEADS], BIG, -BIG, ALU.mult, ALU.add).then_inc(d_c, 1)
                    wait_for(dve, d_c, N_C * t)
                    dve.tensor_copy(zc[:, :, 0], mx[:, (r + 1) % 2, :, UN]).then_inc(d_c, 1)
                    wait_for(dve, d_c, N_C * t)
                    dve.tensor_copy(mk5[:, :, 1:H1], blk[:, bass.ds(t * UN, UN)].unsqueeze(1).to_broadcast([P, HEADS, UN])).then_inc(d_mk5, 1)

                def candidates(t, r, n):
                    dve.wait_ge(d_c, N_C * t + 2)
                    dve.tensor_tensor(cand[:, :, :], nm[:, :, 0:HEADS], t8[:, :].unsqueeze(2).to_broadcast([P, NJ, HEADS]),
                                      ALU.add).then_inc(d_c, 1)

                def of_superstep(t, r, n):
                    dve.wait_ge(d_c, N_C * t + 3)
                    dve.tensor_reduce(cm[:, :, :], cand[:, :, :].rearrange("p (u s) h -> p u h s", s=SUB), AX_X, ALU.max).then_inc(d_c, 1)

                def with_adst(t, r, n):
                    dve.wait_ge(d_c, N_C * t + 4)
                    dve.wait_ge(a_d, t + 1)
                    dve.tensor_tensor(zb[:, :, :], cm[:, :, :], adu[:, r % 2],
                                      ALU.add).then_inc(d_c, 1)

                def leaky(t, r, n):
                    dve.wait_ge(d_c, N_C * t + 5)
                    dve.scalar_tensor_tensor(zc[:, :, 1:H1].rearrange("p h u -> p u h"), zb[:, :, :], SLOPE, zb[:, :, :],
                                             ALU.mult, ALU.max).then_inc(d_c, 1)

                def running(t, r, n):
                    dve.wait_ge(d_c, N_C * t + 6)
                    dve.wait_ge(d_mk5, t + 1)
                    dve.tensor_tensor_scan(mx[:, r % 2, :, :].rearrange("p h u -> p (h u)"),
                                           mk5[:, :, :].rearrange("p h u -> p (h u)"),
                                           zc[:, :, :].rearrange("p h u -> p (h u)"), -BIG, ALU.add, ALU.max).then_inc(d_c, 1)

                def before(t, r, n):
                    dve.wait_ge(d_c, N_C * t + 7)
                    dve.tensor_tensor(mold[:, :, :], mx[:, r % 2, :, 0:UN], mk5[:, :, 1:H1], ALU.add).then_inc(d_c, 1)

                def change(t, r, n):
                    dve.wait_ge(d_c, N_C * t + 8)
                    wait_for(dve, a_so, t - 1)
                    dve.tensor_tensor(dfm[:, r % 2], mold[:, :, :], mx[:, r % 2, :, 1:H1], ALU.subtract).then_inc(d_c, 1)

                def weigh(q):
                    def f(t, r, n):
                        if q == 0:
                            dve.wait_ge(a_ex, t + 1)
                        g = G4(r)[:, q * PW:(q + 1) * PW].rearrange("p s h g -> p (s h) g")
                        dve.tensor_tensor(g[:, :, 0:HC], g[:, :, 0:HC], g[:, :, HC:GC].to_broadcast([P, PW * HEADS, HC]),
                                          ALU.mult).then_inc(d_msg, 1)
                    return f

                def rescale(u):
                    def f(t, r, n):
                        if u == 0:
                            dve.wait_ge(a_so, t + 1)
                        wait_for(dve, d_acc, UN * t + u)
                        dve.tensor_tensor(scaled[:, :].rearrange("p (h g) -> p h g", g=GC),
                                          cur[:, (u + 1) % 2, :].rearrange("p (h g) -> p h g", g=GC),
                                          so[:, r % 2, :, u:u + 1].to_broadcast([P, HEADS, GC]), ALU.mult).then_inc(d_sc, 1)
                    return f

                def add_new(u):
                    def f(t, r, n):
                        dve.wait_ge(d_sc, UN * t + u + 1)
                        dve.wait_ge(p_agg, NQ * t + (u + 1) * NQ // UN)
                        wait_for(dve, a_acc, UN * t + u - 1)
                        dve.tensor_tensor(cur[:, u % 2, :], scaled[:, :], bAG[u % 2][:, 0:ROW], ALU.add).then_inc(d_acc, 1)
                    return f

                slots(dve, NBATCH, PH, [
                    (0, edge_marks), (3, rescale(4)), (0, scan_marks), (2, with_dst), (3, add_new(4)), (2, alpha), (0, one_hot(0)),
                    (2, less_max), (3, rescale(5)), (2, bounded), (0, one_hot(1)), (3, add_new(5)),
                    (2, weigh(0)), (1, presence), (0, scan), (1, candidates), (2, weigh(1)), (1, of_superstep), (2, rescale(0)),
                    (1, with_adst), (0, last_marks), (2, weigh(2)), (1, leaky), (2, add_new(0)), (1, running), (0, last_max), (2, rescale(1)),
                    (0, last_max_part(0)), (1, before), (1, node_max_part(0)), (2, weigh(3)), (0, last_max_part(1)), (1, change),
                    (1, node_max_part(1)), (2, add_new(1)), (0, last_max_part(2)), (1, node_max_part(2)), (2, rescale(2)),
                    (0, last_max_part(3)), (1, node_max_part(3)), (2, weigh(4)), (2, add_new(2)), (2, rescale(3)),
                    (2, weigh(5)), (2, add_new(3))])

        w1f = sb("w1f", [P, KD, F])
        w2f = sb("w2f", [P, FC, D])
        s_wt = [sem("s_wt0"), sem("s_wt1")]

        with ExitStack() as c3:
            def sb3(name, shape, dt=F32):
                return c3.enter_context(nc.sbuf_tensor(name, shape, dt))

            def sem3(name):
                return ctx.enter_context(nc.semaphore(name))

            biasT = G[:, 3, 8 * D:11 * D].rearrange("p (i d) -> p i d", i=3)
            gw = sb3("gw", [P, KD, NX])
            gb = sb3("gb", [P, NX])
            nmr = sb3("nmr", [P, NB])
            rden = sb3("rden", [P, NB, HEADS])
            st = sb3("st", [P, NB, 6])
            mean = sb3("mean", [P, NB])
            var = sb3("var", [P, NB])
            dif = sb3("dif3", [P, NB])
            rs = sb3("rs", [P, NB])
            xr, xb, o1, o2 = (G[:, i, 0:4 * D].rearrange("p (r d) -> p r d", r=4) for i in range(4))
            exb, gn, m1, xt2 = (G[:, i, 4 * D:8 * D].rearrange("p (r d) -> p r d", r=4) for i in range(4))
            ohf = oh[:, :, :, :].rearrange("p a b c -> p (a b c)")
            xs = ohf[:, 2048:2048 + 4 * D].rearrange("p (r d) -> p r d", r=4)
            ohTf = ohT[:, :, :, :].rearrange("p a b c -> p (a b c)")
            NE = NB * NX

            def small(i):
                base = (ohf, ohTf)[i // 4]
                return base[:, (i % 4) * 512:(i % 4) * 512 + NE].rearrange("p (t e) -> p t e", e=NX)

            L, dl, pe_, eq, used, first, tot, inc = (small(i) for i in range(8))
            pos = G[:, 0, 1024:1024 + NE].rearrange("p (t e) -> p t e", e=NX)
            fp = G[:, 1, 1024:1024 + NE].rearrange("p (t e) -> p t e", e=NX)
            fe = G[:, 2, 1024:1024 + NE].rearrange("p (t e) -> p t e", e=NX)
            mx, ssum, prb, posf, ef, fsum, kept, slot, sfar = (sb3(f"tk{i}", [P, NB]) for i in range(9))
            tokf = sb3("tokf", [P, NB])
            acc_t = acc[:, :].rearrange("p (t g) -> p t g", g=ROW)
            NORM_FIRST = 8
            GT = 7
            sidx = sb3("sidx", [P, NB], I32)
            tri = sb3("tri", [P, P])
            e8 = sb3("e8", [P, NX])
            cs = sb3("cs", [P, NX])
            vcol = sb3("vcol", [P, 1])

            s_par = sem3("s_par")
            c_const = sem3("c_const")
            v_ = sem3("v_")
            v_var, a_std, a_p = (sem3(n) for n in ("v_var", "a_std", "a_p"))
            r_xr, r_xb, r_o1, r_o2, r_ex, r_e1, r_v, r_st = (sem3("r_" + n) for n in "xr xb o1 o2 ex e1 v st".split())
            q_g, q_xb, q_m, q_x1, q_k, q_st = (sem3("q_" + n) for n in "g xb m x1 k st".split())
            w_n, w_t, w_tc, w_l, w_L, p_cs = (sem3(n) for n in "w_n w_t w_tc w_l w_L p_cs".split())
            v_first, p_cum, v_idx, s_sc, s_xst = (sem3(n) for n in ("v_first", "p_cum", "v_idx", "s_sc", "s_xst"))
            v_nmr, v_dl = sem3("v_nmr"), sem3("v_dl")

            def tile(a, t):
                return a[:, bass.ds(t, 1), :].rearrange("p a s -> p (a s)")

            def acc_row(t):
                return acc[:, bass.ds(t * ROW, D)]

            block = c3.enter_context(nc.Block())

            @block.sync
            def _(sp):
                for i, a in enumerate((bias, ln_s, ln_b)):
                    sp.dma_start(biasT[:, i, :], a.rearrange("(o d) -> o d", o=1).to_broadcast([P, D])).then_inc(s_par, 16)
                sp.dma_start(gw[:, :, :], gate_w.rearrange("(k p) e -> p k e", p=P)).then_inc(s_par, 16)
                sp.dma_start(gb[:, :], gate_b.rearrange("(o d) -> o d", o=1).to_broadcast([P, NX])).then_inc(s_par, 16)
                sp.dma_start(w1f[:, :, :], w1[0].rearrange("(k p) f -> p k f", p=P)).then_inc(s_wt[0], 16)
                sp.dma_start(w2f[:, :, :], w2[0].rearrange("(c p) d -> p c d", p=P)).then_inc(s_wt[0], 16)
                stores = 0
                for t0 in range(0, NB, GT):
                    t1 = min(NB, t0 + GT)
                    sp.wait_ge(q_k, t1)
                    sp.dma_start(xres[t0 * P:t1 * P, :].rearrange("(t p) d -> p t d", p=P), x_sb[:, t0:t1, :]).then_inc(s_xst, 16)
                    full = min(t1, NB - 1)
                    sp.dma_start(out[t0 * P:full * P, :].rearrange("(t p) d -> p t d", p=P), x_sb[:, t0:full, :]).then_inc(s_xst, 16)
                    stores += 2
                sp.dma_start(out[(NB - 1) * P:N, :], x_sb[0:TAIL, NB - 1, :]).then_inc(s_xst, 16)
                sp.wait_ge(s_xst, 16 * (stores + 1))

            @block.gpsimd
            def _(pool):
                pool.memset(tri[:, :], 1.0).then_inc(c_const, 1)
                pool.memset(vcol[:, :], 1.0).then_inc(c_const, 1)
                pool.iota(e8[:, :], [[1, NX]], base=0, channel_multiplier=0,
                          allow_small_or_imprecise_dtypes=True).then_inc(c_const, 1)
                pool.iota(tokf[:, :], [[P, NB]], base=-FAR, channel_multiplier=1,
                          allow_small_or_imprecise_dtypes=True).then_inc(c_const, 1)
                pool.wait_ge(c_const, 4)
                pool.affine_select(out=tri[:, :], in_=tri[:, :], compare_op=ALU.is_ge, fill=0.0, base=0,
                                   pattern=[[1, P]], channel_multiplier=-1).then_inc(c_const, 1)
                pool.affine_select(out=vcol[:, :], in_=vcol[:, :], compare_op=ALU.is_ge, fill=0.0, base=TAIL - 1,
                                   pattern=[[0, 1]], channel_multiplier=-1).then_inc(c_const, 1)
                pool.wait_ge(s_par, 80)

                def add_bias(t, r, n):
                    pool.wait_ge(r_xr, t + 1)
                    pool.tensor_tensor(xb[:, r, :], xr[:, r, :], biasT[:, 0, :], ALU.add).then_inc(r_xb, 1)

                def add_agg(t, r, n):
                    pool.wait_ge(r_o1, t + 1)
                    pool.wait_ge(r_xb, t + 1)
                    wait_for(pool, r_v, t - 3)
                    pool.tensor_tensor(o2[:, r, :], o1[:, r, :], xb[:, r, :], ALU.add).then_inc(r_o2, 1)

                slots(pool, NB, 4, [(0, add_bias), (1, add_agg)])

                def add_lnb(t, r, n):
                    pool.tensor_tensor(tile(x_sb, t), tile(x_sb, t), biasT[:, 2, :], ALU.add).then_inc(q_xb, 1)

                slots(pool, NB, 2, [(0, add_lnb)])
                pool.wait_ge(v_idx, 1)
                for t in range(NB):
                    pool.wait_ge(w_n, t + 1)
                    pool.indirect_dma_start(xbuf, bass.IndirectOffsetOnAxis(sidx[:, t:t + 1], 0),
                                            acc[:, t * ROW:t * ROW + XR], None,
                                            bounds_check=NX * SL - 1, oob_is_err=False).then_inc(s_sc, 16)
                pool.wait_ge(s_sc, 16 * NB)

            @block.scalar
            def _(act):
                act.wait_ge(v_nmr, 1)

                def norm_x(t, r, n):
                    wait_for(act, r_xb, t - 3)
                    own(act, gate_act)
                    act.activation(xr[:, r, :], tile(x_sb, t), ACT.Identity, scale=rstd[:, bass.ds(t, 1)],
                                   bias=nmr[:, bass.ds(t, 1)]).then_inc(r_xr, 1)

                def exp_o(t, r, n):
                    act.wait_ge(r_o2, t + 1)
                    act.activation(exb[:, r, :], o2[:, r, :], ACT.Exp).then_inc(r_ex, 1)

                slots(act, NB, 4, [(0, norm_x), (2, exp_o)])
                act.wait_ge(v_var, 1)
                act.activation(rs[:, :], var[:, :], ACT.Sqrt, bias=epst[:, :]).then_inc(a_std, 1)
                act.wait_ge(v_nmr, 2)

                def norm_v(t, r, n):
                    wait_for(act, q_m, t - 3)
                    own(act, gate_act)
                    act.activation(gn[:, r, :], acc_row(t), ACT.Identity, scale=rs[:, bass.ds(t, 1)],
                                   bias=nmr[:, bass.ds(t, 1)]).then_inc(q_g, 1)

                def keep_x1(t, r, n):
                    act.wait_ge(q_x1, t + 1)
                    act.copy(tile(x_sb, t), xs[:, r, :]).then_inc(q_k, 1)

                def copy_xt(t, r, n):
                    act.wait_ge(w_t, t + 1)
                    act.copy(xt2[:, r, :], bank[r % 2][:, 0:D]).then_inc(w_tc, 1)

                slots(act, NB, 4, [(0, norm_v), (3, copy_xt), (2, keep_x1)])
                act.wait_ge(v_var, 2)
                act.activation(rs[:, :], var[:, :], ACT.Sqrt, bias=epst[:, :]).then_inc(a_std, 1)
                act.wait_ge(v_nmr, 3)

                def norm_x1(t, r, n):
                    own(act, gate_act)
                    act.activation(acc_row(t), tile(x_sb, t), ACT.Identity, scale=rs[:, bass.ds(t, 1)],
                                   bias=nmr[:, bass.ds(t, 1)]).then_inc(w_n, 1)

                slots(act, NORM_FIRST, 4, [(0, norm_x1)])
                act.wait_ge(v_dl, 1)
                act.activation(pe_, dl, ACT.Exp).then_inc(a_p, 1)
                slots(act, NB - NORM_FIRST, 4, [(0, norm_x1)], first=NORM_FIRST)

            @block.tensor
            def _(pe):
                pe.wait_ge(s_par, 80)
                pe.wait_ge(c_const, 6)

                for k in range(KD):
                    mm = pe.matmul(bank[4][:, 0:NX], ones[:, :], gw[:, k, :], start=(k == 0), stop=(k == KD - 1))
                mm.then_inc(p_cs, 1)

                def turn(t, r, n):
                    pe.wait_ge(q_x1, t + 1)
                    wait_for(pe, w_tc, t - 1)
                    for k in range(KD):
                        mm = pe.transpose(bank[r % 2][:, k * P:(k + 1) * P],
                                          xs[:, r, k * P:(k + 1) * P], ident[:, :])
                    mm.then_inc(w_t, 1)

                def logits(t, r, n):
                    pe.wait_ge(w_tc, t + 1)
                    wait_for(pe, w_L, t - 1)
                    for k in range(KD):
                        mm = pe.matmul(bank[2 + r % 2][:, 0:NX], xt2[:, r, k * P:(k + 1) * P], gw[:, k, :],
                                       start=(k == 0), stop=(k == KD - 1))
                    mm.then_inc(w_l, 1)

                slots(pe, NB, 4, [(0, turn), (1, logits)])
                pe.wait_ge(v_first, 1)
                pe.matmul(bank[4][:, 0:NE], tri[:, :], first.rearrange("p t e -> p (t e)"), start=True, stop=True)
                pe.matmul(bank[5][:, 0:NE], ones[:, :], first.rearrange("p t e -> p (t e)"), start=True,
                          stop=True).then_inc(p_cum, 1)

            @block.vector
            def _(dve):
                link = [0]

                def chained(ins, wait=True):
                    link[0] += 1
                    ins.then_inc(v_, 1)
                    if wait:
                        dve.wait_ge(v_, link[0])

                def join_stats(n):
                    chained(dve.tensor_tensor(mean[:, :], st[:, :, 1], st[:, :, 4], ALU.add), False)
                    chained(dve.tensor_tensor(var[:, :], st[:, :, 2], st[:, :, 5], ALU.add), False)
                    chained(dve.tensor_tensor(dif[:, :], st[:, :, 1], st[:, :, 4], ALU.subtract))
                    chained(dve.scalar_tensor_tensor(dif[:, :], dif[:, :], 0.25, dif[:, :], ALU.mult, ALU.mult))
                    dve.scalar_tensor_tensor(var[:, :], var[:, :], 1.0 / D, dif[:, :], ALU.mult, ALU.add).then_inc(v_var, 1)
                    dve.wait_ge(a_std, n)
                    chained(dve.reciprocal(rs[:, :], rs[:, :]))
                    dve.scalar_tensor_tensor(nmr[:, :], mean[:, :], -0.5, rs[:, :], ALU.mult, ALU.mult).then_inc(v_nmr, 1)

                dve.scalar_tensor_tensor(nmr[:, :], mv[:, :, 0], -1.0, rstd[:, :], ALU.mult, ALU.mult).then_inc(v_nmr, 1)
                dens = acc[:, :].rearrange("p (t h g) -> p (t h) g", h=HEADS, g=GC)[:, :, HC]
                rflat = rden[:, :, :].rearrange("p t h -> p (t h)")
                chained(dve.tensor_scalar(rflat, dens, 1e-16, None, ALU.add))
                chained(dve.reciprocal(rflat, rflat))

                def average(t, r, n):
                    wait_for(dve, r_o2, t - 3)
                    dve.tensor_tensor(o1[:, r, :].rearrange("p (h c) -> p h c", c=HC),
                                      acc[:, bass.ds(t * ROW, ROW)].rearrange("p (h g) -> p h g", g=GC)[:, :, 0:HC],
                                      rden[:, bass.ds(t, 1), :].rearrange("p a h -> p (a h)").unsqueeze(2).to_broadcast([P, HEADS, HC]),
                                      ALU.mult).then_inc(r_o1, 1)

                def elu_below(t, r, n):
                    dve.wait_ge(r_ex, t + 1)
                    dve.tensor_scalar(exb[:, r, :], exb[:, r, :], 1.0, -1.0, ALU.min, ALU.add).then_inc(r_e1, 1)

                def elu(t, r, n):
                    dve.wait_ge(r_e1, t + 1)
                    dve.wait_ge(r_o1, t + 1)
                    dve.scalar_tensor_tensor(acc_row(t), o2[:, r, :], 0.0, exb[:, r, :], ALU.max, ALU.add).then_inc(r_v, 1)

                def stats(t, r, n):
                    dve.wait_ge(r_v, t + 1)
                    dve.bn_stats(tile(st, t), acc_row(t)).then_inc(r_st, 1)

                slots(dve, NB, 4, [(0, average), (3, elu_below), (4, stats), (3, elu)])
                dve.wait_ge(r_st, NB)
                join_stats(1)

                def second(t, r, n):
                    dve.wait_ge(q_g, t + 1)
                    wait_for(dve, q_x1, t - 3)
                    dve.tensor_tensor(m1[:, r, :], gn[:, r, :], biasT[:, 1, :], ALU.mult).then_inc(q_m, 1)

                def second_add(t, r, n):
                    dve.wait_ge(q_m, t + 1)
                    dve.wait_ge(q_xb, t + 1)
                    wait_for(dve, w_t, t - 3)
                    wait_for(dve, q_k, t - 3)
                    wait_for(dve, q_st, t - 3)
                    dve.tensor_tensor(xs[:, r, :], m1[:, r, :], tile(x_sb, t), ALU.add).then_inc(q_x1, 1)

                def second_stats(t, r, n):
                    dve.wait_ge(q_x1, t + 1)
                    dve.bn_stats(tile(st, t), xs[:, r, :]).then_inc(q_st, 1)

                def take_logits(t, r, n):
                    dve.wait_ge(w_l, t + 1)
                    dve.tensor_copy(L[:, bass.ds(t, 1), :].rearrange("p a e -> p (a e)"), bank[2 + r % 2][:, 0:NX]).then_inc(w_L, 1)

                dve.wait_ge(p_cs, 1)
                chained(dve.tensor_copy(cs[:, :], bank[4][:, 0:NX]))
                slots(dve, NB, 4, [(0, second), (2, second_stats), (1, second_add), (4, take_logits)])
                dve.wait_ge(q_st, NB)
                dve.wait_ge(w_L, NB)
                join_stats(2)
                dve.wait_ge(v_nmr, 3)

                def over_t(a):
                    return a[:, :].unsqueeze(1).to_broadcast([P, NB, NX])

                def over_e(a):
                    return a[:, :].unsqueeze(2).to_broadcast([P, NB, NX])

                chained(dve.tensor_tensor(L, L, over_e(rs), ALU.mult), False)
                chained(dve.tensor_tensor(tot, over_e(nmr), over_t(cs), ALU.mult))
                chained(dve.tensor_tensor(L, L, tot, ALU.add))
                chained(dve.tensor_tensor(L, L, over_t(gb), ALU.add))
                chained(dve.tensor_reduce(mx[:, :], L, AX_X, ALU.max))
                dve.tensor_tensor(dl, L, over_e(mx), ALU.subtract).then_inc(v_dl, 1)
                dve.wait_ge(a_p, 1)
                chained(dve.tensor_reduce(ssum[:, :], pe_, AX_X, ALU.add), False)
                chained(dve.tensor_scalar(eq, pe_, 1.0, None, ALU.is_ge), False)
                chained(dve.memset(used, 0.0))
                chained(dve.reciprocal(prb[:, :], ssum[:, :]), False)
                for e in range(1, NX):
                    chained(dve.tensor_tensor(used[:, :, e], used[:, :, e - 1], eq[:, :, e - 1], ALU.max))
                chained(dve.tensor_tensor(first, eq, used, ALU.is_gt))
                dve.wait_ge(c_const, 6)
                dve.tensor_scalar(first[:, NB - 1, :], first[:, NB - 1, :], vcol[:, 0:1], None, ALU.mult).then_inc(v_first, 1)
                dve.wait_ge(p_cum, 1)
                chained(dve.tensor_copy(tot.rearrange("p t e -> p (t e)"), bank[5][:, 0:NE]))
                for e in range(NX):
                    chained(dve.tensor_tensor_scan(inc[:, :, e], ones[:, 0:NB], tot[:, :, e], 0.0, ALU.mult, ALU.add), e == NX - 1)
                chained(dve.tensor_tensor(inc, inc, tot, ALU.subtract))
                chained(dve.scalar_tensor_tensor(pos.rearrange("p t e -> p (t e)"), bank[4][:, 0:NE], -1.0,
                                                 inc.rearrange("p t e -> p (t e)"), ALU.add, ALU.add))
                chained(dve.tensor_tensor(fp, pos, first, ALU.mult), False)
                chained(dve.tensor_tensor(fe, first, e8[:, :].unsqueeze(1).to_broadcast([P, NB, NX]), ALU.mult))
                chained(dve.tensor_reduce(posf[:, :], fp, AX_X, ALU.add), False)
                chained(dve.tensor_reduce(ef[:, :], fe, AX_X, ALU.add), False)
                chained(dve.tensor_reduce(fsum[:, :], first, AX_X, ALU.add))
                chained(dve.scalar_tensor_tensor(kept[:, :], posf[:, :], float(CAP), fsum[:, :], ALU.is_lt, ALU.mult), False)
                chained(dve.scalar_tensor_tensor(slot[:, :], ef[:, :], float(SL), posf[:, :], ALU.mult, ALU.add))
                chained(dve.tensor_tensor(acc_t[:, :, D], prb[:, :], kept[:, :], ALU.mult), False)
                chained(dve.tensor_copy(acc_t[:, :, D + 1], tokf[:, :]), False)
                chained(dve.scalar_tensor_tensor(sfar[:, :], slot[:, :], -float(FAR), kept[:, :], ALU.add, ALU.mult))
                dve.tensor_scalar(sidx[:, :], sfar[:, :], float(FAR), None, ALU.add).then_inc(v_idx, 1)

        with ExitStack() as c4:
            def sem4(name):
                return ctx.enter_context(nc.semaphore(name))

            CH = SL // 2
            MT = CH // P
            NI = 2 * NX
            used = [CH, CAP - CH]
            last_m = used[1] - (MT - 1) * P
            assert 0 < last_m <= P

            def rows(r, m):
                return last_m if r % 2 == 1 and m == MT - 1 else P

            w1s = [w1f[:, :, :], acc[:, 0:KD * F].rearrange("p (k f) -> p k f", k=KD)]
            o = KD * F
            w2s = [w2f[:, :, :], acc[:, o:o + FC * D].rearrange("p (c d) -> p c d", c=FC)]
            o += FC * D
            xe = [acc[:, o + i * MT * XR:o + (i + 1) * MT * XR].rearrange("p (m d) -> p m d", m=MT) for i in range(4)]
            assert o + 4 * MT * XR <= NB * ROW and 4 * P * MT == 4 * CH
            h1 = [G[:, 2 * i:2 * i + 2, :].rearrange("p a b -> p (a b)")[:, 0:FC * CH].rearrange("p (c n) -> p c n", c=FC)
                  for i in range(2)]
            xT = [oh[:, i].rearrange("p a b -> p (a b)")[:, 0:KD * CH].rearrange("p (k n) -> p k n", k=KD) for i in range(2)]
            yo = [ohT[:, i].rearrange("p a b -> p (a b)")[:, 0:MT * D].rearrange("p (m d) -> p m d", m=MT) for i in range(2)]
            b1s = c4.enter_context(nc.sbuf_tensor("b1s", [P, NX * FC], F32))
            b2s = c4.enter_context(nc.sbuf_tensor("b2s", [P, NX * D], F32))

            xf = x_sb[:, :, :].rearrange("p t d -> p (t d)")
            xg = [xf[:, i * MT * D:(i + 1) * MT * D].rearrange("p (m d) -> p m d", m=MT) for i in range(2)]
            yc, bad, nan, zero = (xf[:, (i + 2) * MT * D:(i + 3) * MT * D].rearrange("p (m d) -> p m d", m=MT) for i in range(4))
            bad, nan = bad.bitcast(I32), nan.bitcast(I32)
            wm = c4.enter_context(nc.sbuf_tensor("wm", [P, 4, MT], F32))
            ti = c4.enter_context(nc.sbuf_tensor("ti", [P, 4, MT], I32))

            s_b = sem4("s_b")
            s_xe = [sem4(f"s_xe{i}") for i in range(4)]
            s_out = [sem4(f"s_out{i}") for i in range(4)]
            s_xg = [sem4(f"s_xg{i}") for i in range(2)]
            m_t, m_th, m_xt, m_h, m_relu, m_y, m_yo, m_z, m_id = (sem4("m_" + n) for n in "t th xt h relu y yo z id".split())
            k_w, k_b, k_n, k_c, k_p, k_q, k_o = (sem4("k_" + n) for n in "w b n c p q o".split())
            block = c4.enter_context(nc.Block())

            @block.sync
            def _(sp):
                sp.dma_start(b1s[:, :], b1).then_inc(s_b, 16)
                sp.dma_start(b2s[:, :], b2.rearrange("(o e) d -> o (e d)", o=1).to_broadcast([P, NX * D])).then_inc(s_b, 16)

                def load(t, r, n):
                    wait_for(sp, m_t, t - 3)
                    wait_for(sp, m_id, t - 3)
                    sp.dma_start(xe[r],
                                 xbuf[bass.ds(t * CH, CH), :].rearrange("(m p) d -> p m d", p=P)).then_inc(s_xe[r], 16)
                    if r % 2 == 0 and not (isinstance(t, int) and t == 0):
                        e = 2 * n + r // 2
                        wait_for(sp, m_y, MT * (t - 2))
                        sp.dma_start(w1s[r // 2], w1[bass.ds(e, 1)].rearrange("o (k p) f -> p (o k) f", p=P)).then_inc(s_wt[r // 2], 16)
                        sp.dma_start(w2s[r // 2], w2[bass.ds(e, 1)].rearrange("o (c p) d -> p (o c) d", p=P)).then_inc(s_wt[r // 2], 16)

                slots(sp, NI, 4, [(0, load)])

            @block.gpsimd
            def _(pool):
                pool.wait_ge(m_z, 3)

                def residuals(t, r, n):
                    pool.wait_ge(m_id, t + 1)
                    own(pool, gate)
                    if not (isinstance(t, int) and t < 2):
                        pool.wait_ge(k_o, MT * (t - 1))
                        own(pool, gate)
                    for m in range(MT):
                        pool.indirect_dma_start(xg[r % 2][:, m, :], None, xres, bass.IndirectOffsetOnAxis(ti[:, r, m:m + 1], 0),
                                                bounds_check=NB * P - 1, oob_is_err=False).then_inc(s_xg[r % 2], 16)

                def scatter(t, r, n):
                    for m in range(MT):
                        pool.wait_ge(k_o, MT * t + m + 1)
                        own(pool, gate)
                        pm = rows(r, m)
                        pool.indirect_dma_start(out, bass.IndirectOffsetOnAxis(ti[0:pm, r, m:m + 1], 0), yo[r % 2][0:pm, m, :], None,
                                                bounds_check=N - 1, oob_is_err=False).then_inc(s_out[r], 16)

                slots(pool, NI, 4, [(0, residuals), (1, scatter)])
                for i in range(4):
                    pool.wait_ge(s_out[i], 16 * MT * (NI // 4))

            @block.tensor
            def _(pe):
                def turn(t, r, n):
                    pe.wait_ge(s_xe[r], 16 * (n + 1))
                    for half in range(2):
                        wait_for(pe, m_xt, 2 * t + half - 1)
                        for m in range(MT // 2):
                            for k in range(KD):
                                c = half * (MT // 2) + m
                                mm = pe.transpose(bank[half][:, k * 256 + m * P:k * 256 + (m + 1) * P],
                                                  xe[r][:, c, k * P:(k + 1) * P], ident[:, :])
                        mm.then_inc(m_t if half == 1 else m_th, 1)

                def up(t, r, n):
                    pe.wait_ge(m_xt, 2 * t + 2)
                    pe.wait_ge(s_wt[r // 2], 32 * (n + 1))
                    for c in range(FC):
                        wait_for(pe, m_relu, FC * t + c - 3)
                        for k in range(KD):
                            mm = pe.matmul(bank[2 + c % 4][:, 0:used[r % 2]], w1s[r // 2][:, k, c * P:(c + 1) * P],
                                           xT[r % 2][:, k, 0:used[r % 2]],
                                           start=(k == 0), stop=(k == KD - 1))
                        mm.then_inc(m_h, 1)

                def down(t, r, n):
                    pe.wait_ge(m_relu, FC * (t + 1))
                    for m in range(MT):
                        wait_for(pe, m_yo, MT * t + m - 1)
                        pm = rows(r, m)
                        for c in range(FC):
                            mm = pe.matmul(bank[6 + m % 2][0:pm, 0:D], h1[r % 2][:, c, m * P:m * P + pm], w2s[r // 2][:, c, :],
                                           start=(c == 0), stop=(c == FC - 1))
                        mm.then_inc(m_y, 1)

                slots(pe, NI, 4, [(1, up), (0, turn), (1, down)])

            @block.scalar
            def _(act):
                act.wait_ge(s_b, 32)

                def relu(t, r, n):
                    wait_for(act, m_y, MT * (t - 1))
                    for c in range(FC):
                        act.wait_ge(m_h, FC * t + c + 1)
                        e = 2 * n + r // 2
                        own(act, gate_act)
                        act.activation(h1[r % 2][:, c, 0:used[r % 2]], bank[2 + c % 4][:, 0:used[r % 2]], ACT.Relu,
                                       bias=b1s[:, bass.ds(e * FC + c, 1)]).then_inc(m_relu, 1)

                slots(act, NI, 4, [(0, relu)])

            @block.vector
            def _(dve):
                dve.memset(zero, 0.0).then_inc(m_z, 1)
                dve.memset(xg[0], 0.0).then_inc(m_z, 1)
                dve.memset(xg[1], 0.0).then_inc(m_z, 1)
                dve.wait_ge(m_z, 3)
                dve.wait_ge(s_b, 32)

                def copy_xt(t, r, n):
                    wait_for(dve, m_h, FC * (t - 1))
                    for half in range(2):
                        if half == 0:
                            dve.wait_ge(m_th, t + 1)
                        else:
                            dve.wait_ge(m_t, t + 1)
                        dve.tensor_copy(xT[r % 2][:, :, half * 256:(half + 1) * 256],
                                        bank[half][:, :].rearrange("p (k n) -> p k n", k=KD)).then_inc(m_xt, 1)

                def take_ids(t, r, n):
                    dve.wait_ge(s_xe[r], 16 * (n + 1))
                    wait_for(dve, s_out[r], 16 * MT * n)
                    wait_for(dve, k_w, MT * (t - 3))
                    dve.tensor_copy(wm[:, r, :], xe[r][:, :, D])
                    dve.tensor_scalar(ti[:, r, :], xe[r][:, :, D + 1], float(FAR), None, ALU.add).then_inc(m_id, 1)

                def finish(t, r, n):
                    e = 2 * n + r // 2
                    wait_for(dve, s_out[(r - 2) % 4], 16 * MT * (n + (r - 2) // 4 + 1))
                    dve.wait_ge(m_id, t + 1)
                    for m in range(MT):
                        dve.wait_ge(m_y, MT * t + m + 1)
                        pm = rows(r, m)
                        dve.tensor_tensor(yo[r % 2][0:pm, m, :], bank[6 + m % 2][0:pm, 0:D], b2s[0:pm, bass.ds(e * D, D)],
                                          ALU.add).then_inc(m_yo, 1)
                        weigh_y(t, r, n, m)

                def weigh_y(t, r, n, m):
                    pm = rows(r, m)
                    y, i = yo[r % 2][0:pm, m, :], m % 2
                    done = MT * t + m
                    dve.wait_ge(m_yo, done + 1)
                    dve.tensor_tensor(y, y, wm[0:pm, r, m:m + 1].to_broadcast([pm, D]), ALU.mult).then_inc(k_w, 1)
                    dve.wait_ge(k_w, done + 1)
                    wait_for(dve, k_q, done - 1)
                    dve.tensor_scalar(bad[0:pm, i], y, 0.0, 0.0, ALU.mult, ALU.not_equal).then_inc(k_b, 1)
                    dve.tensor_tensor(nan[0:pm, i], y, y, ALU.not_equal).then_inc(k_n, 1)
                    dve.tensor_scalar(yc[0:pm, i], y, 10000.0, -10000.0, ALU.min, ALU.max).then_inc(k_c, 1)
                    dve.wait_ge(k_c, done + 1)
                    dve.wait_ge(k_n, done + 1)
                    dve.wait_ge(k_b, done + 1)
                    own(dve, gate_dve)
                    dve.copy_predicated(y, bad[0:pm, i], yc[0:pm, i]).then_inc(k_p, 1)
                    dve.wait_ge(k_p, done + 1)
                    own(dve, gate_dve)
                    dve.copy_predicated(y, nan[0:pm, i], zero[0:pm, 0]).then_inc(k_q, 1)
                    dve.wait_ge(k_q, done + 1)
                    dve.wait_ge(s_xg[r % 2], 16 * MT * (2 * n + r // 2 + 1))
                    dve.tensor_tensor(y, y, xg[r % 2][0:pm, m, :], ALU.add).then_inc(k_o, 1)

                slots(dve, NI, 4, [(0, copy_xt), (0, take_ids), (1, finish)])


def kernel(**inputs):
    import numpy as np
    import concourse.bacc as bacc
    from concourse.bass_utils import run_bass_kernel_spmd as run

    nc = bacc.Bacc("TRN2", target_bir_lowering=False, num_devices=1)
    src, dst = np.asarray(inputs["src"]), np.asarray(inputs["dst"])
    e = src.shape[0]
    pad = np.full(2 * STEP, PAD_NODE, np.int32)
    d = np.concatenate([np.full(SUB, -1, np.int32), dst, pad, np.full(SUB, PAD_NODE, np.int32)])
    m = e + 2 * STEP
    ed = np.stack([np.concatenate([src, np.zeros(2 * STEP, np.int32)]), d[0:m], d[SUB:SUB + m], d[2 * SUB:2 * SUB + m]], axis=1)
    cols = -(-e // P)
    dstp = np.concatenate([dst, np.full(P * cols - e, PAD_NODE, np.int32)]).reshape(P, cols)
    arrays = {"ed": np.ascontiguousarray(ed), "dstp": np.ascontiguousarray(dstp)}
    for name in ("x", "L0_gnn_W", "L0_gnn_att_src", "L0_gnn_att_dst", "L0_gnn_bias", "L0_gnn_ln_scale", "L0_gnn_ln_bias",
                 "L0_ffn_gate_w", "L0_ffn_gate_b", "L0_ffn_w1", "L0_ffn_b1", "L0_ffn_w2", "L0_ffn_b2"):
        arrays[name] = np.ascontiguousarray(inputs[name])
    b1 = arrays["L0_ffn_b1"]
    arrays["L0_ffn_b1"] = np.ascontiguousarray(b1.reshape(b1.shape[0], -1, P).transpose(2, 0, 1).reshape(P, -1))
    aps = {k: nc.dram_tensor("in_" + k, a.shape, mybir.dt.from_np(a.dtype), kind="ExternalInput").ap() for k, a in arrays.items()}
    o = nc.dram_tensor("out", [arrays["x"].shape[0], arrays["x"].shape[1]], F32, kind="ExternalOutput").ap()
    build(nc, aps["x"], aps["ed"], aps["dstp"], *[aps[k] for k in list(arrays)[3:]], o)
    r = run(nc, [{"in_" + k: a for k, a in arrays.items()}], core_ids=[0])
    return r.results[0]["out"]
```
